# Optimizing a Trainium2 kernel written in Bass

```python
import numpy as np
import jax
import jax.numpy as jnp

def _softmax(x, axis=-1):
    return jax.nn.softmax(x, axis=axis)

def _gelu(x):
    return jax.nn.gelu(x, approximate=True)

def _silu(x):
    return jax.nn.silu(x)

def _sigmoid(x):
    return jax.nn.sigmoid(x)

def _layernorm(x, axis=-1, eps=1e-05):
    m = jnp.mean(x, axis=axis, keepdims=True)
    v = jnp.var(x, axis=axis, keepdims=True)
    return (x - m) / jnp.sqrt(v + eps)

def _scatter_add(tgt, idx, src, axis=0):
    return tgt.at[idx].add(src)

def _segment_sum(src, seg, n):
    return jax.ops.segment_sum(src, seg, n)
kernel_name = 'mk_xattn_ffn_d4_seqx_r4_6ef529'

def setup_inputs(seed: int=0):
    np.random.seed(seed)
    _w = jnp.asarray

    def _rec_inputs():
        import jax
        import jax.numpy as jnp
        _rk = jax.random.key(seed)
        x = -0.0005207 + 1.001 * jax.random.normal(jax.random.fold_in(_rk, 1), (8, 256, 256), jnp.float32)
        _lenS = 256 - jax.random.randint(jax.random.fold_in(_rk, 7), (8,), 0, max(1, 256 // 4) + 1, jnp.int32)
        _lenS2 = 256 - jax.random.randint(jax.random.fold_in(_rk, 8), (8,), 0, max(1, 256 // 4) + 1, jnp.int32)
        _ctx_1024P = jax.random.normal(jax.random.fold_in(_rk, 11), (8, 16, 256), jnp.float32)
        _ctx_1024c = jax.random.dirichlet(jax.random.fold_in(_rk, 511), 0.3 * jnp.ones((16,), jnp.float32), (8, 256))
        _ctx_1024t = jnp.einsum('bsk,bkd->bsd', _ctx_1024c, _ctx_1024P)
        _ctx_1024t = _ctx_1024t * jax.lax.rsqrt(jnp.mean(jnp.square(_ctx_1024t)) + 1e-12) * 0.953939
        ctx_1024 = -0.000514642 + 1.00011 * (_ctx_1024t + 0.3 * jax.random.normal(jax.random.fold_in(_rk, 611), (8, 256, 256), jnp.float32))
        _validS = jnp.arange(256)[None, :] < _lenS[:, None]
        _validS2 = jnp.arange(256)[None, :] < _lenS2[:, None]
        _causal = jnp.tril(jnp.ones((256, 256), dtype=bool))
        mask_BxS2_bk1 = jnp.broadcast_to(_validS2[:, :], (8, 256))
        mask_BxS2_if1 = jnp.where(jnp.ones((8, 256), dtype=bool), 1, 0).astype(jnp.int32)
        mask_BxS2_bk0 = jnp.logical_not(jnp.broadcast_to(_validS2[:, :], (8, 256)))
        return (x, ctx_1024, mask_BxS2_bk1, mask_BxS2_if1, mask_BxS2_bk0)
    x, ctx_1024, mask_BxS2_bk1, mask_BxS2_if1, mask_BxS2_bk0 = _rec_inputs()

    def _L0_xattn_setup():
        import jax, jax.numpy as jnp
        import numpy as np
        import math
        B, S, E, H = (1, 512, 256, 16)
        HD = E // H
        CAUSAL_HEADS = 4
        WINDOW = 63

        def _rope_tables(seq_len, head_dim):
            inv_freq = 1.0 / 10000.0 ** (jnp.arange(0, head_dim, 2, dtype=jnp.float32) / head_dim)
            t = jnp.arange(seq_len, dtype=jnp.float32)
            freqs = t[:, None] * inv_freq[None, :]
            return (jnp.cos(freqs)[None, None], jnp.sin(freqs)[None, None])

        def _apply_rope(x, cos, sin):
            x_even = x[..., ::2]
            x_odd = x[..., 1::2]
            r_even = x_even * cos - x_odd * sin
            r_odd = x_even * sin + x_odd * cos
            return jnp.stack((r_even, r_odd), axis=-1).reshape(x.shape)
        key = jax.random.key(seed)
        ks = jax.random.split(key, 11)
        sc = 0.02
        return {'query': jax.random.normal(ks[0], (B, S, E), jnp.float32), 'key': jax.random.normal(ks[1], (B, S, E), jnp.float32), 'value': jax.random.normal(ks[2], (B, S, E), jnp.float32), 'Wq': jax.random.normal(ks[3], (E, E), jnp.float32) * sc, 'bq': jax.random.normal(ks[4], (E,), jnp.float32) * sc, 'Wk': jax.random.normal(ks[5], (E, E), jnp.float32) * sc, 'bk': jax.random.normal(ks[6], (E,), jnp.float32) * sc, 'Wv': jax.random.normal(ks[7], (E, E), jnp.float32) * sc, 'bv': jax.random.normal(ks[8], (E,), jnp.float32) * sc, 'Wo': jax.random.normal(ks[9], (E, E), jnp.float32) * sc, 'bo': jax.random.normal(ks[10], (E,), jnp.float32) * sc}
    _L0_xattn_all = _L0_xattn_setup()
    _L0_xattn_in = {k: v for k, v in _L0_xattn_all.items() if k in ('Wq', 'bq', 'Wk', 'bk', 'Wv', 'bv', 'Wo', 'bo')}
    del _L0_xattn_all

    def _L0_ffn_setup():
        import jax, jax.numpy as jnp
        import numpy as np
        B, T, D, H, E = (4, 512, 256, 512, 8)
        TOP_K = int(E * 0.25)
        key = jax.random.key(seed)
        ks = jax.random.split(key, 6)
        x = jax.random.normal(ks[0], (B, T, D), dtype=jnp.float32)
        gate = jax.random.normal(ks[1], (D, E), dtype=jnp.float32)
        W1 = jax.random.normal(ks[2], (E, D, H), dtype=jnp.float32) * D ** (-0.5)
        b1 = jnp.zeros((E, H), dtype=jnp.float32)
        W2 = jax.random.normal(ks[3], (E, H, D), dtype=jnp.float32) * H ** (-0.5)
        b2 = jnp.zeros((E, D), dtype=jnp.float32)
        return {'x': x, 'gate': gate, 'W1': W1, 'b1': b1, 'W2': W2, 'b2': b2}
    _L0_ffn_all = _L0_ffn_setup()
    _L0_ffn_in = {k: v for k, v in _L0_ffn_all.items() if k in ('gate', 'W1', 'b1', 'W2', 'b2')}
    del _L0_ffn_all

    def _L1_xattn_setup():
        import jax, jax.numpy as jnp
        import numpy as np
        EPS = 1e-12

        def _l2_normalize(x, axis):
            n = jnp.sqrt(jnp.sum(x * x, axis=axis, keepdims=True))
            return x / jnp.maximum(n, EPS)
        key = jax.random.key(seed)
        ks = jax.random.split(key, 13)
        b, n, d, h = (8, 1024, 256, 16)
        scale = 0.02
        inp = {'query': jax.random.normal(ks[0], (b, n, d), jnp.float32), 'key': jax.random.normal(ks[1], (b, n, d), jnp.float32), 'value': jax.random.normal(ks[2], (b, n, d), jnp.float32), 'key_padding_mask': jax.random.randint(ks[3], (b, n), 0, 2).astype(bool), 'Wq': jax.random.normal(ks[4], (d, d), jnp.float32) * scale, 'bq': jax.random.normal(ks[5], (d,), jnp.float32) * scale, 'Wk': jax.random.normal(ks[6], (d, d), jnp.float32) * scale, 'bk': jax.random.normal(ks[7], (d,), jnp.float32) * scale, 'Wv': jax.random.normal(ks[8], (d, d), jnp.float32) * scale, 'bv': jax.random.normal(ks[9], (d,), jnp.float32) * scale, 'Wo': jax.random.normal(ks[10], (d, d), jnp.float32) * scale, 'bo': jax.random.normal(ks[11], (d,), jnp.float32) * scale}
        return inp
    _L1_xattn_all = _L1_xattn_setup()
    _L1_xattn_in = {k: v for k, v in _L1_xattn_all.items() if k in ('Wq', 'bq', 'Wk', 'bk', 'Wv', 'bv', 'Wo', 'bo')}
    del _L1_xattn_all

    def _L1_ffn_setup():
        import jax, jax.numpy as jnp
        import numpy as np
        HIDDEN = 256
        INNER = 1024

        def _weight_quant(w):
            scale = 1.0 / jnp.clip(jnp.mean(jnp.abs(w)), 1e-05)
            wq = jnp.clip(jnp.round(w * scale), -1.0, 1.0) / scale
            return w + jax.lax.stop_gradient(wq - w)

        def _act_quant(x):
            scale = 127.0 / jnp.clip(jnp.max(jnp.abs(x), axis=-1, keepdims=True), 1e-05)
            xq = jnp.clip(jnp.round(x * scale), -128.0, 127.0) / scale
            return x + jax.lax.stop_gradient(xq - x)

        def _bitlinear(x, w):
            return jnp.einsum('bsi,oi->bso', _act_quant(x), _weight_quant(w))
        key = jax.random.key(seed)
        k0, k1, k2, k3 = jax.random.split(key, 4)
        x = jax.random.normal(k0, (4, 512, HIDDEN), dtype=jnp.float32)
        w_gate = jax.random.normal(k1, (INNER, HIDDEN), dtype=jnp.float32) / np.sqrt(HIDDEN)
        w_up = jax.random.normal(k2, (INNER, HIDDEN), dtype=jnp.float32) / np.sqrt(HIDDEN)
        w_down = jax.random.normal(k3, (HIDDEN, INNER), dtype=jnp.float32) / np.sqrt(INNER)
        return {'x': x, 'w_gate': w_gate, 'w_up': w_up, 'w_down': w_down}
    _L1_ffn_all = _L1_ffn_setup()
    _L1_ffn_in = {k: v for k, v in _L1_ffn_all.items() if k in ('w_gate', 'w_up', 'w_down')}
    del _L1_ffn_all

    def _L2_xattn_setup():
        import jax, jax.numpy as jnp
        import numpy as np
        D_MODEL = 256
        N_HEADS = 16
        D_K = D_MODEL // N_HEADS
        B, L = (2, 512)

        def _dense_bf16(x, W, b):
            return jnp.matmul(x.astype(jnp.bfloat16), W.astype(jnp.bfloat16)) + b.astype(jnp.bfloat16)

        def _attention(q, k, v, mask):
            Lq, Ls, dk = (q.shape[2], k.shape[2], q.shape[3])
            scale = 1.0 / np.sqrt(dk)
            scores = jnp.einsum('bhqd,bhkd->bhqk', q, k) * scale
            causal = jnp.tril(jnp.ones((Lq, Ls), bool))
            full_mask = causal[None, None] & (mask[:, None, None, :] > 0)
            scores = jnp.where(full_mask, scores, -jnp.inf)
            p = jax.nn.softmax(scores, axis=-1)
            return jnp.einsum('bhqk,bhkd->bhqd', p, v)
        key = jax.random.key(seed)
        ks = jax.random.split(key, 8)
        inp = {'q': jax.random.normal(ks[0], (B, L, D_MODEL), jnp.float32), 'k': jax.random.normal(ks[1], (B, L, D_MODEL), jnp.float32), 'v': jax.random.normal(ks[2], (B, L, D_MODEL), jnp.float32), 'mask': jnp.ones((B, L), jnp.int32), 'Wq': jax.random.normal(ks[3], (D_MODEL, D_MODEL), jnp.float32) * 0.02, 'bq': jnp.zeros((D_MODEL,), jnp.float32), 'Wk': jax.random.normal(ks[4], (D_MODEL, D_MODEL), jnp.float32) * 0.02, 'bk': jnp.zeros((D_MODEL,), jnp.float32), 'Wv': jax.random.normal(ks[5], (D_MODEL, D_MODEL), jnp.float32) * 0.02, 'bv': jnp.zeros((D_MODEL,), jnp.float32), 'Wo': jax.random.normal(ks[6], (D_MODEL, D_MODEL), jnp.float32) * 0.02, 'bo': jnp.zeros((D_MODEL,), jnp.float32)}
        return inp
    _L2_xattn_all = _L2_xattn_setup()
    _L2_xattn_in = {k: v for k, v in _L2_xattn_all.items() if k in ('Wq', 'bq', 'Wk', 'bk', 'Wv', 'bv', 'Wo', 'bo')}
    del _L2_xattn_all

    def _L2_ffn_setup():
        import jax, jax.numpy as jnp
        import numpy as np
        DIM = 256
        DEPTH = 2
        HEADS = 8
        DIM_HEAD = 64
        WINDOW = 128
        INNER = HEADS * DIM_HEAD
        HID = int(DIM * 4 * 2 / 3)
        B, N = (2, 2048)
        QK_SCALE = 8.0

        def shift_token(t):
            t1, t2 = jnp.split(t, 2, axis=-1)
            t2 = jnp.pad(t2, ((0, 0), (1, 0), (0, 0)))[:, :-1]
            return jnp.concatenate([t1, t2], axis=-1)

        def l2norm(t):
            return t / jnp.clip(jnp.linalg.norm(t, axis=-1, keepdims=True), 1e-12)

        def rotate_half(x):
            x1, x2 = jnp.split(x, 2, axis=-1)
            return jnp.concatenate([-x2, x1], axis=-1)

        def rotary_xpos(q, k):
            n = q.shape[-2]
            half_idx = jnp.arange(0, DIM_HEAD, 2, dtype=jnp.float32)
            inv_freq = 1.0 / 10000.0 ** (half_idx / DIM_HEAD)
            t = jnp.arange(n, dtype=jnp.float32)
            freqs = t[:, None] * inv_freq[None, :]
            freqs = jnp.concatenate([freqs, freqs], axis=-1)
            base = (half_idx + 0.4 * DIM_HEAD) / (1.4 * DIM_HEAD)
            power = (t - n // 2) / float(WINDOW // 2)
            scale = base[None, :] ** power[:, None]
            scale = jnp.concatenate([scale, scale], axis=-1)
            cos, sin = (jnp.cos(freqs), jnp.sin(freqs))
            q = q * cos * scale + rotate_half(q) * sin * scale
            k = k * cos / scale + rotate_half(k) * sin / scale
            return (q, k)

        def local_attention(q, k, v):
            b, h, n, d = q.shape
            w = n // WINDOW
            bq = q.reshape(b, h, w, WINDOW, d) * QK_SCALE
            bk = k.reshape(b, h, w, WINDOW, d)
            bv = v.reshape(b, h, w, WINDOW, d)

            def look_around(t):
                p = jnp.pad(t, ((0, 0), (0, 0), (1, 0), (0, 0), (0, 0)))
                return jnp.concatenate([p[:, :, :w], p[:, :, 1:]], axis=3)
            bk, bv = (look_around(bk), look_around(bv))
            bt = jnp.arange(n).reshape(w, WINDOW)
            btp = jnp.pad(bt, ((1, 0), (0, 0)), constant_values=-1)
            btk = jnp.concatenate([btp[:w], btp[1:]], axis=1)
            sim = jnp.einsum('bhwid,bhwjd->bhwij', bq, bk)
            i = bt[:, :, None]
            j = btk[:, None, :]
            mask = (i < j) | (i > j + WINDOW) | (j == -1)
            sim = jnp.where(mask, -jnp.finfo(sim.dtype).max, sim)
            attn = jax.nn.softmax(sim, axis=-1)
            out = jnp.einsum('bhwij,bhwjd->bhwid', attn, bv)
            return out.reshape(b, h, n, d)

        def _layer(x, wqkv, qs, ksc, wo, lg, lb, w1, b1, w2, b2):
            b, n, _ = x.shape
            h = shift_token(x)
            qkv = h @ wqkv
            q, k, v = jnp.split(qkv, 3, axis=-1)
            to_heads = lambda t: t.reshape(b, n, HEADS, DIM_HEAD).transpose(0, 2, 1, 3)
            q, k, v = (to_heads(q), to_heads(k), to_heads(v))
            q = l2norm(q) * qs
            k = l2norm(k) * ksc
            q, k = rotary_xpos(q, k)
            o = local_attention(q, k, v)
            o = o.transpose(0, 2, 1, 3).reshape(b, n, INNER)
            x = x + o @ wo
            h = shift_token(x)
            mu = h.mean(-1, keepdims=True)
            var = h.var(-1, keepdims=True)
            h = (h - mu) / jnp.sqrt(var + 1e-05) * lg + lb
            h = h @ w1 + b1
            a, g = jnp.split(h, 2, axis=-1)
            h = a * jax.nn.gelu(g, approximate=False)
            x = x + h @ w2 + b2
            return x
        key = jax.random.key(seed)
        ks = jax.random.split(key, 6)
        return {'x': jax.random.normal(ks[0], (B, N, DIM), jnp.float32), 'wqkv': jax.random.normal(ks[1], (DEPTH, DIM, 3 * INNER), jnp.float32) * 0.02, 'q_scale': jnp.ones((DEPTH, DIM_HEAD), jnp.float32), 'k_scale': jnp.ones((DEPTH, DIM_HEAD), jnp.float32), 'wo': jax.random.normal(ks[2], (DEPTH, INNER, DIM), jnp.float32) * 0.02, 'ln_g': jnp.ones((DEPTH, DIM), jnp.float32), 'ln_b': jnp.zeros((DEPTH, DIM), jnp.float32), 'w1': jax.random.normal(ks[3], (DEPTH, DIM, 2 * HID), jnp.float32) * 0.02, 'b1': jnp.zeros((DEPTH, 2 * HID), jnp.float32), 'w2': jax.random.normal(ks[4], (DEPTH, HID, DIM), jnp.float32) * 0.02, 'b2': jnp.zeros((DEPTH, DIM), jnp.float32)}
    _L2_ffn_all = _L2_ffn_setup()
    _L2_ffn_in = {k: v for k, v in _L2_ffn_all.items() if k in ('wqkv', 'q_scale', 'k_scale', 'wo', 'ln_g', 'ln_b', 'w1', 'b1', 'w2', 'b2')}
    del _L2_ffn_all

    def _L3_xattn_setup():
        import jax, jax.numpy as jnp
        import numpy as np
        D_MODEL = 256
        N_HEADS = 1
        HEAD_DIM = D_MODEL // N_HEADS
        N, LEN_Q, LEN_IN = (8, 256, 1024)
        key = jax.random.key(seed)
        ks = jax.random.split(key, 7)
        s = 1.0 / np.sqrt(D_MODEL)
        return {'query': jax.random.normal(ks[0], (N, LEN_Q, D_MODEL), dtype=jnp.float32), 'input_flatten': jax.random.normal(ks[1], (N, LEN_IN, D_MODEL), dtype=jnp.float32), 'input_padding_mask': jax.random.randint(ks[2], (N, LEN_IN), 0, 2).astype(bool), 'Wq': jax.random.normal(ks[3], (D_MODEL, D_MODEL), dtype=jnp.float32) * s, 'bq': jnp.zeros((D_MODEL,), dtype=jnp.float32), 'Wk': jax.random.normal(ks[4], (D_MODEL, D_MODEL), dtype=jnp.float32) * s, 'bk': jnp.zeros((D_MODEL,), dtype=jnp.float32), 'Wo': jax.random.normal(ks[5], (D_MODEL, D_MODEL), dtype=jnp.float32) * s, 'bo': jnp.zeros((D_MODEL,), dtype=jnp.float32)}
    _L3_xattn_all = _L3_xattn_setup()
    _L3_xattn_in = {k: v for k, v in _L3_xattn_all.items() if k in ('Wq', 'bq', 'Wk', 'bk', 'Wo', 'bo')}
    del _L3_xattn_all

    def _L3_ffn_setup():
        import jax, jax.numpy as jnp
        import numpy as np
        DIM = 256
        HIDDEN = 704
        NUM_EXPERTS = 8
        TOP_K = 2
        BATCH, SEQ = (4, 512)
        key = jax.random.key(seed)
        ks = jax.random.split(key, 5)
        x = jax.random.normal(ks[0], (BATCH, SEQ, DIM), dtype=jnp.float32)
        gate_w = jax.random.normal(ks[1], (NUM_EXPERTS, DIM), dtype=jnp.float32) * 0.02
        w1 = jax.random.normal(ks[2], (NUM_EXPERTS, HIDDEN, DIM), dtype=jnp.float32) * 0.02
        w3 = jax.random.normal(ks[3], (NUM_EXPERTS, HIDDEN, DIM), dtype=jnp.float32) * 0.02
        w2 = jax.random.normal(ks[4], (NUM_EXPERTS, DIM, HIDDEN), dtype=jnp.float32) * 0.02
        return {'x': x, 'gate_w': gate_w, 'w1': w1, 'w3': w3, 'w2': w2}
    _L3_ffn_all = _L3_ffn_setup()
    _L3_ffn_in = {k: v for k, v in _L3_ffn_all.items() if k in ('gate_w', 'w1', 'w3', 'w2')}
    del _L3_ffn_all
    return {'x': x, 'ctx_1024': ctx_1024, 'mask_BxS2_bk1': mask_BxS2_bk1, 'mask_BxS2_if1': mask_BxS2_if1, 'mask_BxS2_bk0': mask_BxS2_bk0, 'L0_xattn_Wq': _L0_xattn_in['Wq'], 'L0_xattn_bq': _L0_xattn_in['bq'], 'L0_xattn_Wk': _L0_xattn_in['Wk'], 'L0_xattn_bk': _L0_xattn_in['bk'], 'L0_xattn_Wv': _L0_xattn_in['Wv'], 'L0_xattn_bv': _L0_xattn_in['bv'], 'L0_xattn_Wo': _L0_xattn_in['Wo'], 'L0_xattn_bo': _L0_xattn_in['bo'], 'L0_ffn_gate': _L0_ffn_in['gate'], 'L0_ffn_W1': _L0_ffn_in['W1'], 'L0_ffn_b1': _L0_ffn_in['b1'], 'L0_ffn_W2': _L0_ffn_in['W2'], 'L0_ffn_b2': _L0_ffn_in['b2'], 'L1_xattn_Wq': _L1_xattn_in['Wq'], 'L1_xattn_bq': _L1_xattn_in['bq'], 'L1_xattn_Wk': _L1_xattn_in['Wk'], 'L1_xattn_bk': _L1_xattn_in['bk'], 'L1_xattn_Wv': _L1_xattn_in['Wv'], 'L1_xattn_bv': _L1_xattn_in['bv'], 'L1_xattn_Wo': _L1_xattn_in['Wo'], 'L1_xattn_bo': _L1_xattn_in['bo'], 'L1_ffn_w_gate': _L1_ffn_in['w_gate'], 'L1_ffn_w_up': _L1_ffn_in['w_up'], 'L1_ffn_w_down': _L1_ffn_in['w_down'], 'L2_xattn_Wq': _L2_xattn_in['Wq'], 'L2_xattn_bq': _L2_xattn_in['bq'], 'L2_xattn_Wk': _L2_xattn_in['Wk'], 'L2_xattn_bk': _L2_xattn_in['bk'], 'L2_xattn_Wv': _L2_xattn_in['Wv'], 'L2_xattn_bv': _L2_xattn_in['bv'], 'L2_xattn_Wo': _L2_xattn_in['Wo'], 'L2_xattn_bo': _L2_xattn_in['bo'], 'L2_ffn_wqkv': _L2_ffn_in['wqkv'], 'L2_ffn_q_scale': _L2_ffn_in['q_scale'], 'L2_ffn_k_scale': _L2_ffn_in['k_scale'], 'L2_ffn_wo': _L2_ffn_in['wo'], 'L2_ffn_ln_g': _L2_ffn_in['ln_g'], 'L2_ffn_ln_b': _L2_ffn_in['ln_b'], 'L2_ffn_w1': _L2_ffn_in['w1'], 'L2_ffn_b1': _L2_ffn_in['b1'], 'L2_ffn_w2': _L2_ffn_in['w2'], 'L2_ffn_b2': _L2_ffn_in['b2'], 'L3_xattn_Wq': _L3_xattn_in['Wq'], 'L3_xattn_bq': _L3_xattn_in['bq'], 'L3_xattn_Wk': _L3_xattn_in['Wk'], 'L3_xattn_bk': _L3_xattn_in['bk'], 'L3_xattn_Wo': _L3_xattn_in['Wo'], 'L3_xattn_bo': _L3_xattn_in['bo'], 'L3_ffn_gate_w': _L3_ffn_in['gate_w'], 'L3_ffn_w1': _L3_ffn_in['w1'], 'L3_ffn_w3': _L3_ffn_in['w3'], 'L3_ffn_w2': _L3_ffn_in['w2']}

def reference(x, ctx_1024, mask_BxS2_bk1, mask_BxS2_if1, mask_BxS2_bk0, L0_xattn_Wq, L0_xattn_bq, L0_xattn_Wk, L0_xattn_bk, L0_xattn_Wv, L0_xattn_bv, L0_xattn_Wo, L0_xattn_bo, L0_ffn_gate, L0_ffn_W1, L0_ffn_b1, L0_ffn_W2, L0_ffn_b2, L1_xattn_Wq, L1_xattn_bq, L1_xattn_Wk, L1_xattn_bk, L1_xattn_Wv, L1_xattn_bv, L1_xattn_Wo, L1_xattn_bo, L1_ffn_w_gate, L1_ffn_w_up, L1_ffn_w_down, L2_xattn_Wq, L2_xattn_bq, L2_xattn_Wk, L2_xattn_bk, L2_xattn_Wv, L2_xattn_bv, L2_xattn_Wo, L2_xattn_bo, L2_ffn_wqkv, L2_ffn_q_scale, L2_ffn_k_scale, L2_ffn_wo, L2_ffn_ln_g, L2_ffn_ln_b, L2_ffn_w1, L2_ffn_b1, L2_ffn_w2, L2_ffn_b2, L3_xattn_Wq, L3_xattn_bq, L3_xattn_Wk, L3_xattn_bk, L3_xattn_Wo, L3_xattn_bo, L3_ffn_gate_w, L3_ffn_w1, L3_ffn_w3, L3_ffn_w2):
    import jax
    import jax.numpy as jnp

    def _L0_xattn_ref(query, key, value, Wq, bq, Wk, bk, Wv, bv, Wo, bo):
        import jax, jax.numpy as jnp
        import numpy as np
        import math
        B, S, E, H = (1, 512, 256, 16)
        HD = E // H
        CAUSAL_HEADS = 4
        WINDOW = 63

        def _rope_tables(seq_len, head_dim):
            inv_freq = 1.0 / 10000.0 ** (jnp.arange(0, head_dim, 2, dtype=jnp.float32) / head_dim)
            t = jnp.arange(seq_len, dtype=jnp.float32)
            freqs = t[:, None] * inv_freq[None, :]
            return (jnp.cos(freqs)[None, None], jnp.sin(freqs)[None, None])

        def _apply_rope(x, cos, sin):
            x_even = x[..., ::2]
            x_odd = x[..., 1::2]
            r_even = x_even * cos - x_odd * sin
            r_odd = x_even * sin + x_odd * cos
            return jnp.stack((r_even, r_odd), axis=-1).reshape(x.shape)
        b, s, _ = query.shape
        q = query @ Wq.T + bq
        k = key @ Wk.T + bk
        v = value @ Wv.T + bv
        q = q.reshape(b, s, H, HD).transpose(0, 2, 1, 3)
        k = k.reshape(b, s, H, HD).transpose(0, 2, 1, 3)
        v = v.reshape(b, s, H, HD).transpose(0, 2, 1, 3)
        cos, sin = _rope_tables(s, HD)
        q = _apply_rope(q, cos, sin)
        k = _apply_rope(k, cos, sin)
        scale = math.sqrt(HD)
        scores = jnp.einsum('bhqd,bhkd->bhqk', q, k) / scale
        i = jnp.arange(s)
        causal_mask = i[None, :] > i[:, None]
        allowed = (i[None, :] <= i[:, None]) & (i[None, :] >= i[:, None] - (WINDOW - 1))
        sparse_mask = ~allowed
        is_causal_head = jnp.arange(H) < CAUSAL_HEADS
        head_mask = jnp.where(is_causal_head[:, None, None], causal_mask[None], sparse_mask[None])
        neg_inf = jnp.float32(-jnp.inf)
        scores = jnp.where(head_mask[None], neg_inf, scores)
        all_masked = jnp.all(jnp.isneginf(scores), axis=-1, keepdims=True)
        scores = jnp.where(all_masked, 0.0, scores)
        attn = jax.nn.softmax(scores, axis=-1)
        out = jnp.einsum('bhqk,bhkd->bhqd', attn, v)
        out = out.transpose(0, 2, 1, 3).reshape(b, s, E)
        return out @ Wo.T + bo

    def _L0_ffn_ref(x, gate, W1, b1, W2, b2):
        import jax, jax.numpy as jnp
        import numpy as np
        B, T, D, H, E = (4, 512, 256, 512, 8)
        TOP_K = int(E * 0.25)
        raw_gate = jax.nn.softmax(jnp.einsum('btd,de->bte', x, gate), axis=-1)
        topk_scores, topk_idx = jax.lax.top_k(raw_gate, TOP_K)
        mask = jax.nn.one_hot(topk_idx, E, dtype=raw_gate.dtype).sum(axis=-2)
        gate_topk = mask * raw_gate
        gate_topk = gate_topk / jnp.maximum(gate_topk.sum(axis=-1, keepdims=True), 1e-12)
        h = jax.nn.relu(jnp.einsum('btd,edh->beth', x, W1) + b1[None, :, None, :])
        expert_out = jnp.einsum('beth,ehd->betd', h, W2) + b2[None, :, None, :]
        out = jnp.einsum('bte,betd->btd', gate_topk, expert_out)
        return out

    def _L1_xattn_ref(query, key, value, key_padding_mask, Wq, bq, Wk, bk, Wv, bv, Wo, bo):
        import jax, jax.numpy as jnp
        import numpy as np
        EPS = 1e-12

        def _l2_normalize(x, axis):
            n = jnp.sqrt(jnp.sum(x * x, axis=axis, keepdims=True))
            return x / jnp.maximum(n, EPS)
        b, n, d = query.shape
        h = 16
        dh = d // h
        q = query @ Wq.T + bq
        k = key @ Wk.T + bk
        v = value @ Wv.T + bv
        q = 1.0 + jax.nn.elu(q)
        k = 1.0 + jax.nn.elu(k)
        k = jnp.where(key_padding_mask[:, :, None], 0.0, k)
        q = q.reshape(b, n, h, dh).transpose(0, 2, 1, 3)
        k = k.reshape(b, n, h, dh).transpose(0, 2, 1, 3)
        v = v.reshape(b, n, h, dh).transpose(0, 2, 1, 3)
        q = _l2_normalize(q, axis=2)
        k = _l2_normalize(k, axis=3)
        kv = jnp.einsum('bhnd,bhne->bhde', k, v)
        out = jnp.einsum('bhnd,bhde->bhne', q, kv)
        out = out.transpose(0, 2, 1, 3).reshape(b, n, d)
        return out @ Wo.T + bo

    def _L1_ffn_ref(x, w_gate, w_up, w_down):
        import jax, jax.numpy as jnp
        import numpy as np
        HIDDEN = 256
        INNER = 1024

        def _weight_quant(w):
            scale = 1.0 / jnp.clip(jnp.mean(jnp.abs(w)), 1e-05)
            wq = jnp.clip(jnp.round(w * scale), -1.0, 1.0) / scale
            return w + jax.lax.stop_gradient(wq - w)

        def _act_quant(x):
            scale = 127.0 / jnp.clip(jnp.max(jnp.abs(x), axis=-1, keepdims=True), 1e-05)
            xq = jnp.clip(jnp.round(x * scale), -128.0, 127.0) / scale
            return x + jax.lax.stop_gradient(xq - x)

        def _bitlinear(x, w):
            return jnp.einsum('bsi,oi->bso', _act_quant(x), _weight_quant(w))
        gate = jax.nn.silu(_bitlinear(x, w_gate))
        up = _bitlinear(x, w_up)
        return _bitlinear(gate * up, w_down)

    def _L2_xattn_ref(q, k, v, mask, Wq, bq, Wk, bk, Wv, bv, Wo, bo):
        import jax, jax.numpy as jnp
        import numpy as np
        D_MODEL = 256
        N_HEADS = 16
        D_K = D_MODEL // N_HEADS
        B, L = (2, 512)

        def _dense_bf16(x, W, b):
            return jnp.matmul(x.astype(jnp.bfloat16), W.astype(jnp.bfloat16)) + b.astype(jnp.bfloat16)

        def _attention(q, k, v, mask):
            Lq, Ls, dk = (q.shape[2], k.shape[2], q.shape[3])
            scale = 1.0 / np.sqrt(dk)
            scores = jnp.einsum('bhqd,bhkd->bhqk', q, k) * scale
            causal = jnp.tril(jnp.ones((Lq, Ls), bool))
            full_mask = causal[None, None] & (mask[:, None, None, :] > 0)
            scores = jnp.where(full_mask, scores, -jnp.inf)
            p = jax.nn.softmax(scores, axis=-1)
            return jnp.einsum('bhqk,bhkd->bhqd', p, v)
        query = _dense_bf16(q, Wq, bq).astype(jnp.float32)
        key_p = _dense_bf16(k, Wk, bk).astype(jnp.float32)
        val_p = _dense_bf16(v, Wv, bv).astype(jnp.float32)
        Bb, Lt, _ = query.shape
        Ls = key_p.shape[1]
        query = query.reshape(Bb, Lt, N_HEADS, D_K).transpose(0, 2, 1, 3)
        key_p = key_p.reshape(Bb, Ls, N_HEADS, D_K).transpose(0, 2, 1, 3)
        val_p = val_p.reshape(Bb, Ls, N_HEADS, D_K).transpose(0, 2, 1, 3)
        x = _attention(query, key_p, val_p, mask)
        x = x.transpose(0, 2, 1, 3).reshape(Bb, Lt, D_MODEL)
        out = _dense_bf16(x, Wo, bo)
        return out.astype(jnp.float32)

    def _L2_ffn_ref(x, wqkv, q_scale, k_scale, wo, ln_g, ln_b, w1, b1, w2, b2):
        import jax, jax.numpy as jnp
        import numpy as np
        DIM = 256
        DEPTH = 2
        HEADS = 8
        DIM_HEAD = 64
        WINDOW = 128
        INNER = HEADS * DIM_HEAD
        HID = int(DIM * 4 * 2 / 3)
        B, N = (2, 2048)
        QK_SCALE = 8.0

        def shift_token(t):
            t1, t2 = jnp.split(t, 2, axis=-1)
            t2 = jnp.pad(t2, ((0, 0), (1, 0), (0, 0)))[:, :-1]
            return jnp.concatenate([t1, t2], axis=-1)

        def l2norm(t):
            return t / jnp.clip(jnp.linalg.norm(t, axis=-1, keepdims=True), 1e-12)

        def rotate_half(x):
            x1, x2 = jnp.split(x, 2, axis=-1)
            return jnp.concatenate([-x2, x1], axis=-1)

        def rotary_xpos(q, k):
            n = q.shape[-2]
            half_idx = jnp.arange(0, DIM_HEAD, 2, dtype=jnp.float32)
            inv_freq = 1.0 / 10000.0 ** (half_idx / DIM_HEAD)
            t = jnp.arange(n, dtype=jnp.float32)
            freqs = t[:, None] * inv_freq[None, :]
            freqs = jnp.concatenate([freqs, freqs], axis=-1)
            base = (half_idx + 0.4 * DIM_HEAD) / (1.4 * DIM_HEAD)
            power = (t - n // 2) / float(WINDOW // 2)
            scale = base[None, :] ** power[:, None]
            scale = jnp.concatenate([scale, scale], axis=-1)
            cos, sin = (jnp.cos(freqs), jnp.sin(freqs))
            q = q * cos * scale + rotate_half(q) * sin * scale
            k = k * cos / scale + rotate_half(k) * sin / scale
            return (q, k)

        def local_attention(q, k, v):
            b, h, n, d = q.shape
            w = n // WINDOW
            bq = q.reshape(b, h, w, WINDOW, d) * QK_SCALE
            bk = k.reshape(b, h, w, WINDOW, d)
            bv = v.reshape(b, h, w, WINDOW, d)

            def look_around(t):
                p = jnp.pad(t, ((0, 0), (0, 0), (1, 0), (0, 0), (0, 0)))
                return jnp.concatenate([p[:, :, :w], p[:, :, 1:]], axis=3)
            bk, bv = (look_around(bk), look_around(bv))
            bt = jnp.arange(n).reshape(w, WINDOW)
            btp = jnp.pad(bt, ((1, 0), (0, 0)), constant_values=-1)
            btk = jnp.concatenate([btp[:w], btp[1:]], axis=1)
            sim = jnp.einsum('bhwid,bhwjd->bhwij', bq, bk)
            i = bt[:, :, None]
            j = btk[:, None, :]
            mask = (i < j) | (i > j + WINDOW) | (j == -1)
            sim = jnp.where(mask, -jnp.finfo(sim.dtype).max, sim)
            attn = jax.nn.softmax(sim, axis=-1)
            out = jnp.einsum('bhwij,bhwjd->bhwid', attn, bv)
            return out.reshape(b, h, n, d)

        def _layer(x, wqkv, qs, ksc, wo, lg, lb, w1, b1, w2, b2):
            b, n, _ = x.shape
            h = shift_token(x)
            qkv = h @ wqkv
            q, k, v = jnp.split(qkv, 3, axis=-1)
            to_heads = lambda t: t.reshape(b, n, HEADS, DIM_HEAD).transpose(0, 2, 1, 3)
            q, k, v = (to_heads(q), to_heads(k), to_heads(v))
            q = l2norm(q) * qs
            k = l2norm(k) * ksc
            q, k = rotary_xpos(q, k)
            o = local_attention(q, k, v)
            o = o.transpose(0, 2, 1, 3).reshape(b, n, INNER)
            x = x + o @ wo
            h = shift_token(x)
            mu = h.mean(-1, keepdims=True)
            var = h.var(-1, keepdims=True)
            h = (h - mu) / jnp.sqrt(var + 1e-05) * lg + lb
            h = h @ w1 + b1
            a, g = jnp.split(h, 2, axis=-1)
            h = a * jax.nn.gelu(g, approximate=False)
            x = x + h @ w2 + b2
            return x
        for l in range(DEPTH):
            x = _layer(x, wqkv[l], q_scale[l], k_scale[l], wo[l], ln_g[l], ln_b[l], w1[l], b1[l], w2[l], b2[l])
        return x

    def _L3_xattn_ref(query, input_flatten, input_padding_mask, Wq, bq, Wk, bk, Wo, bo):
        import jax, jax.numpy as jnp
        import numpy as np
        D_MODEL = 256
        N_HEADS = 1
        HEAD_DIM = D_MODEL // N_HEADS
        N, LEN_Q, LEN_IN = (8, 256, 1024)
        n, len_q, _ = query.shape
        len_in = input_flatten.shape[1]
        Q = (query @ Wq.T + bq).reshape(n, len_q, N_HEADS, HEAD_DIM).transpose(0, 2, 1, 3)
        K = (input_flatten @ Wk.T + bk).reshape(n, len_in, N_HEADS, HEAD_DIM).transpose(0, 2, 1, 3)
        scores = jnp.einsum('nhqd,nhkd->nhqk', Q, K)
        scores = jnp.where(input_padding_mask[:, None, None, :], -jnp.inf, scores)
        attn = jax.nn.softmax(scores, axis=-1)
        V = jnp.broadcast_to(input_flatten[:, None], (n, N_HEADS, len_in, D_MODEL))
        out = jnp.einsum('nhql,nhld->nhqd', attn, V)
        out = out.transpose(0, 2, 1, 3).reshape(n, len_q, D_MODEL)
        return out @ Wo.T + bo

    def _L3_ffn_ref(x, gate_w, w1, w3, w2):
        import jax, jax.numpy as jnp
        import numpy as np
        DIM = 256
        HIDDEN = 704
        NUM_EXPERTS = 8
        TOP_K = 2
        BATCH, SEQ = (4, 512)
        orig_shape = x.shape
        xf = x.reshape(-1, x.shape[-1])
        T = xf.shape[0]
        E, K = (gate_w.shape[0], TOP_K)
        scores = jax.nn.softmax(xf @ gate_w.T, axis=-1)
        expert_weights, expert_indices = jax.lax.top_k(scores, K)
        expert_weights = expert_weights / jnp.sum(expert_weights, axis=-1, keepdims=True)
        x_rep = jnp.repeat(xf, K, axis=0)
        flat_idx = expert_indices.reshape(-1)
        y = jnp.zeros_like(x_rep)
        for e in range(E):
            m = (flat_idx == e)[:, None]
            xe = jnp.where(m, x_rep, 0.0)
            h = jax.nn.silu(xe @ w1[e].T) * (xe @ w3[e].T)
            out = h @ w2[e].T
            y = y + jnp.where(m, out, 0.0)
        y = jnp.sum(y.reshape(T, K, -1) * expert_weights[..., None], axis=1)
        return y.reshape(orig_shape)
    x = x + _L0_xattn_ref(_layernorm(x, axis=-1), ctx_1024, ctx_1024, L0_xattn_Wq, L0_xattn_bq, L0_xattn_Wk, L0_xattn_bk, L0_xattn_Wv, L0_xattn_bv, L0_xattn_Wo, L0_xattn_bo)
    x = x + _L0_ffn_ref(_layernorm(x, axis=-1), L0_ffn_gate, L0_ffn_W1, L0_ffn_b1, L0_ffn_W2, L0_ffn_b2)
    x = x + _L1_xattn_ref(_layernorm(x, axis=-1), ctx_1024, ctx_1024, mask_BxS2_bk1, L1_xattn_Wq, L1_xattn_bq, L1_xattn_Wk, L1_xattn_bk, L1_xattn_Wv, L1_xattn_bv, L1_xattn_Wo, L1_xattn_bo)
    x = x + _L1_ffn_ref(_layernorm(x, axis=-1), L1_ffn_w_gate, L1_ffn_w_up, L1_ffn_w_down)
    x = x + _L2_xattn_ref(_layernorm(x, axis=-1), ctx_1024, ctx_1024, mask_BxS2_if1, L2_xattn_Wq, L2_xattn_bq, L2_xattn_Wk, L2_xattn_bk, L2_xattn_Wv, L2_xattn_bv, L2_xattn_Wo, L2_xattn_bo)
    x = x + _L2_ffn_ref(_layernorm(x, axis=-1), L2_ffn_wqkv, L2_ffn_q_scale, L2_ffn_k_scale, L2_ffn_wo, L2_ffn_ln_g, L2_ffn_ln_b, L2_ffn_w1, L2_ffn_b1, L2_ffn_w2, L2_ffn_b2)
    x = x + _L3_xattn_ref(_layernorm(x, axis=-1), ctx_1024, mask_BxS2_bk0, L3_xattn_Wq, L3_xattn_bq, L3_xattn_Wk, L3_xattn_bk, L3_xattn_Wo, L3_xattn_bo)
    x = x + _L3_ffn_ref(_layernorm(x, axis=-1), L3_ffn_gate_w, L3_ffn_w1, L3_ffn_w3, L3_ffn_w2)
    return x

_drawn_inputs = setup_inputs


def setup_inputs(seed=0):
    import zlib

    import numpy as np

    out = dict(_drawn_inputs(seed))
    spreads = {'L0_ffn_b1': (0.0, 0.1),
     'L0_ffn_b2': (0.0, 0.1),
     'L2_xattn_bq': (0.0, 0.8),
     'L2_xattn_bk': (0.0, 0.8),
     'L2_xattn_bv': (0.0, 0.1),
     'L2_xattn_bo': (0.0, 0.1),
     'L2_ffn_q_scale': (1.0, 0.6),
     'L2_ffn_k_scale': (1.0, 0.6),
     'L2_ffn_ln_g': (1.0, 0.6),
     'L2_ffn_ln_b': (0.0, 0.8),
     'L2_ffn_b1': (0.0, 0.572),
     'L2_ffn_b2': (0.0, 0.1),
     'L3_xattn_bq': (0.0, 0.1),
     'L3_xattn_bk': (0.0, 0.8),
     'L3_xattn_bo': (0.0, 0.1)}
    factors = {'L0_xattn_Wq': 5.422,
     'L0_xattn_bq': 8.0,
     'L0_xattn_Wk': 6.942,
     'L0_xattn_bk': 8.0,
     'L0_xattn_bv': 2.936,
     'L1_xattn_bq': 8.0,
     'L1_xattn_Wk': 8.0,
     'L1_xattn_bk': 8.0,
     'L2_xattn_Wq': 8.0,
     'L2_xattn_Wk': 8.0,
     'L3_ffn_gate_w': 8.0,
     'L3_ffn_w1': 7.316,
     'L3_ffn_w3': 7.239,
     'L3_ffn_w2': 7.252}
    for name, (base, spread) in spreads.items():
        noise = np.random.default_rng([zlib.crc32(name.encode()), seed]).standard_normal(out[name].shape)
        drawn = base * np.exp(spread * noise) if base else spread * noise
        out[name] = jnp.asarray(drawn.astype(out[name].dtype))
    for name, factor in factors.items():
        out[name] = (out[name] * factor).astype(out[name].dtype)
    return out
```

```python
from contextlib import ExitStack

import numpy as np

import concourse.bass as bass
from concourse import mybir

ALU = mybir.AluOpType
ACT = mybir.ActivationFunctionType
F32 = mybir.dt.float32
F32R = mybir.dt.float32r
BF16 = mybir.dt.bfloat16
U8 = mybir.dt.uint8
U32 = mybir.dt.uint32
I32 = mybir.dt.int32
AX_X = mybir.AxisListType.X

P = 128
BATCH, SEQ, DIM = 8, 256, 256
TILES = BATCH * SEQ // P
KD = DIM // P
BANK = 512
CAUSAL3 = 3 * P
MASKED = -1e30
LN_EPS = 1e-5
TINY_SQ = 1e-24
EXPERTS = 8
ROUND = 12582912.0
QUANT_MIN = 1e-5


class Stage:

    def __init__(self, nc, ctx, name):
        self.nc, self.ctx, self.name = nc, ctx, name
        self.sems = []

    def sem(self, name):
        s = self.ctx.enter_context(self.nc.semaphore(f"{self.name}_{name}"))
        self.sems.append(s)
        return s

    def sb(self, name, shape, dt=F32):
        return self.ctx.enter_context(self.nc.sbuf_tensor(f"{self.name}_{name}", shape, dt))

    def ps(self, name, shape, dt=F32):
        return self.ctx.enter_context(self.nc.psum_tensor(f"{self.name}_{name}", shape, dt))

    def again(self):
        numbers = sorted(s.num for s in self.sems)
        first = numbers[0]
        for number, following in zip(numbers, numbers[1:] + [None]):
            if following != number + 1:
                self.nc.gpsimd.sem_clear(range(first, number + 1))
                first = following
        self.nc.all_engine_barrier()


def chain(eng, sem):
    count = [0]

    def link(ins):
        count[0] += 1
        ins.then_inc(sem, 1)
        eng.wait_ge(sem, count[0])

    return link


class Ring:

    def __init__(self, banks, readers):
        self.banks, self.readers, self.n = banks, readers, 0

    def claim(self, eng):
        old = self.n - len(self.banks)
        if old >= 0:
            reader = self.readers[old]
            eng.wait_ge(reader, sum(r is reader for r in self.readers[:old + 1]))
        bank = self.banks[self.n % len(self.banks)]
        self.n += 1
        return bank

    def bank(self, n):
        return self.banks[n % len(self.banks)]


def spread(ap, axis, shape):
    return ap.unsqueeze(axis).to_broadcast(shape)


class LayerNorm:

    def __init__(self, s, tiles, pieces=1):
        self.tiles, self.pieces = tiles, pieces
        self.stats = s.sb("ln_stats", [P, tiles, 6 * pieces])
        self.mv = s.sb("ln_mean_var", [P, tiles, 2])
        self.ve = s.sb("ln_var_eps", [P, tiles])
        self.rstd = s.sb("ln_rstd", [P, tiles])
        self.xn = s.sb("ln_out", [P, tiles, DIM])
        self.stats_ready = s.sem("ln_stats_ready")
        self.eps_added = s.sem("ln_eps_added")
        self.rstd_ready = s.sem("ln_rstd_ready")
        self.xn_ready = s.sem("ln_out_ready")

    def statistics(self, nc, link, parts):
        for t in range(self.tiles):
            for i, part in enumerate(parts(t)):
                ins = nc.vector.bn_stats(self.stats[:, t, 6 * i:6 * i + 6], part)
        link(ins)
        for t in range(self.tiles):
            ins = nc.vector.bn_aggr(self.mv[:, t, :], self.stats[:, t, :])
        ins.then_inc(self.stats_ready, 1)

    def root(self, nc, pool, minus_half):
        pool.wait_ge(self.stats_ready, 1)
        nc.gpsimd.tensor_scalar(self.ve[:], self.mv[:, :, 1], LN_EPS, None, ALU.add).then_inc(self.eps_added, 1)
        pool.wait_ge(self.eps_added, 1)
        nc.gpsimd.tensor_tensor(self.rstd[:], self.ve[:], minus_half[:, 0:self.tiles],
                                ALU.pow).then_inc(self.rstd_ready, 1)

    def apply(self, nc, dve, parts):
        dve.wait_ge(self.rstd_ready, 1)
        for t in range(self.tiles):
            at = 0
            for part in parts(t):
                n = part.shape[-1]
                ins = nc.vector.tensor_scalar(self.xn[:, t, at:at + n], part, self.mv[:, t, 0:1],
                                              self.rstd[:, t:t + 1], ALU.subtract, ALU.mult)
                at += n
        ins.then_inc(self.xn_ready, 1)


class Attention:

    SLOT = 2

    def __init__(self, s, heads, width, padded, dtype, max_parts, key_mask, ring_uses):
        self.H, self.D, self.HP, self.dt = heads, width, padded, dtype
        self.parts, self.key_mask = max_parts, key_mask
        self.per_chunk = P // padded
        self.chunks = heads // self.per_chunk
        self.k_first = width + key_mask
        self.k_second = self.k_first + max_parts
        self.groups = heads // self.SLOT
        self.tr_banks = self.chunks * SEQ // BANK
        self.rounds = -(-heads * (width + 1) // BANK)
        self.round_groups = self.groups // self.rounds
        self.q_rows = s.sb("q_rows", [P, 2, heads, padded], dtype)
        self.k_rows = s.sb("k_rows", [P, 2, heads, padded], dtype)
        self.v_rows = s.sb("v_rows", [P, 2, heads, width + 1])
        self.qT = s.sb("qT", [P, self.chunks, SEQ], dtype)
        self.kT = s.sb("kT", [P, self.chunks, SEQ], dtype)
        self.probs = s.sb("probs", [P, 4, self.SLOT, CAUSAL3])
        self.rsum = s.sb("rsum", [P, 2, heads])
        self.o_rows = s.sb("o_rows", [P, 2, heads, width])
        self.negmax = s.sb("negmax", [P, 2, heads]) if max_parts > 1 else None
        self.psS = s.ps("scores", [P, 4, BANK])
        self.psO = s.ps("pv", [P, 2, BANK])
        self.q_ready, self.k_ready, self.v_ready = s.sem("q_ready"), s.sem("k_ready"), s.sem("v_ready")
        self.tr_done = s.sem("tr_done")
        self.first_done, self.second_done = s.sem("first_done"), s.sem("second_done")
        self.max_taken = s.sem("max_taken")
        self.max_placed = s.sem("max_placed")
        self.exp_done, self.pv_done = s.sem("exp_done"), s.sem("pv_done")
        self.o_ready = s.sem("o_ready")

    def clear(self, nc):
        ones_from = self.k_first
        nc.vector.memset(self.q_rows[:], 0.0)
        nc.vector.memset(self.k_rows[:], 0.0)
        nc.vector.memset(self.v_rows[:], 1.0)

    def clear_ones(self, nc):
        nc.vector.memset(self.k_rows[:, :, :, self.k_first:self.k_second], 1.0)
        if self.key_mask:
            nc.vector.memset(self.q_rows[:, :, :, self.D:self.D + 1], 1.0)

    def _flip(self, nc, pe, rows, ring, ident):
        for n in range(self.tr_banks):
            bank = ring.claim(pe)
            view = bank[:] if self.dt == F32 else bank[:].bitcast(BF16)
            per = BANK // SEQ
            for i in range(per):
                c = n * per + i
                for t in range(2):
                    src = rows[:, t, c * self.per_chunk:(c + 1) * self.per_chunk, :]
                    ins = nc.tensor.transpose(view[:, i * SEQ + t * P:i * SEQ + (t + 1) * P],
                                              src.rearrange("p h d -> p (h d)"), ident[:])
            ins.then_inc(self.tr_done, 1)

    def _unflip(self, nc, act, to, ring, first_use, first_done, evacuated):
        for n in range(self.tr_banks):
            act.wait_ge(self.tr_done, first_done + n + 1)
            bank = ring.bank(first_use + n)
            view = bank[:] if self.dt == F32 else bank[:].bitcast(BF16)
            per = BANK // SEQ
            nc.scalar.copy(to[:, n * per:(n + 1) * per, :],
                           view[:, 0:BANK].rearrange("p (c t) -> p c t", c=per)).then_inc(evacuated, 1)

    def tensor(self, nc, pe, ring, ident, ident_bf, mask_q, mask_k, evacuated, before):
        nb = self.tr_banks
        pe.wait_ge(self.k_ready, 1)
        self._flip(nc, pe, self.k_rows, ring, ident)
        pe.wait_ge(self.q_ready, 1)
        self._flip(nc, pe, self.q_rows, ring, ident)
        pe.wait_ge(evacuated, before + 2 * nb)
        for g in range(self.groups):
            if g >= 2:
                pe.wait_ge(self.max_taken, g - 1)
            for i in range(self.SLOT):
                h = g * self.SLOT + i
                bank = self.psS[:, (g % 2) * self.SLOT + i, :]
                nc.tensor.matmul(bank[:, 0:CAUSAL3], ident_bf[:], mask_q(h), start=True, stop=True)
            for i in range(self.SLOT):
                h = g * self.SLOT + i
                bank = self.psS[:, (g % 2) * self.SLOT + i, :]
                c, r = h // self.per_chunk, (h % self.per_chunk) * self.HP
                K = self.k_first
                nc.tensor.matmul(bank[:, 0:P], self.qT[r:r + K, c, 0:P], self.kT[r:r + K, c, 0:P],
                                 start=False, stop=False, skip_group_check=True)
                ins = nc.tensor.matmul(bank[:, P:CAUSAL3], self.qT[r:r + K, c, P:SEQ], self.kT[r:r + K, c, :],
                                       start=False, stop=False, skip_group_check=True)
            ins.then_inc(self.first_done, 1)
        pe.wait_ge(self.max_placed, 1)
        self._flip(nc, pe, self.q_rows, ring, ident)
        pe.wait_ge(evacuated, before + 3 * nb)
        pe.wait_ge(self.v_ready, 1)
        for step in range(self.groups + 1):
            if step < self.groups:
                self._second(nc, pe, step, ident_bf, mask_k)
            if step:
                self._values(nc, pe, step - 1)

    def _second(self, nc, pe, g, ident_bf, mask_k):
        if g >= 2:
            pe.wait_ge(self.exp_done, g - 1)
        for i in range(self.SLOT):
            h = g * self.SLOT + i
            bank = self.psS[:, (g % 2) * self.SLOT + i, :]
            nc.tensor.matmul(bank[:, 0:CAUSAL3], ident_bf[:], mask_k(h), start=True, stop=True)
        for i in range(self.SLOT):
            h = g * self.SLOT + i
            bank = self.psS[:, (g % 2) * self.SLOT + i, :]
            c, r = h // self.per_chunk, (h % self.per_chunk) * self.HP
            K = self.k_second
            nc.tensor.matmul(bank[:, 0:SEQ], self.kT[r:r + K, c, 0:P], self.qT[r:r + K, c, :],
                             start=False, stop=False, skip_group_check=True)
            ins = nc.tensor.matmul(bank[:, SEQ:CAUSAL3], self.kT[r:r + K, c, P:SEQ], self.qT[r:r + K, c, P:SEQ],
                                   start=False, stop=False, skip_group_check=True)
        ins.then_inc(self.second_done, 1)

    def _values(self, nc, pe, g):
        pe.wait_ge(self.exp_done, g + 1)
        if g and g % self.round_groups == 0:
            pe.wait_ge(self.o_ready, g // self.round_groups)
        W = self.D + 1
        for i in range(self.SLOT):
            h = g * self.SLOT + i
            o = (h - (g // self.round_groups) * self.round_groups * self.SLOT) * W
            pr = self.probs[:, g % 4, i, :]
            nc.tensor.matmul(self.psO[:, 0, o:o + W], pr[:, 0:P], self.v_rows[:, 0, h, :], start=True, stop=True)
            nc.tensor.matmul(self.psO[:, 1, o:o + W], pr[:, P:SEQ], self.v_rows[:, 0, h, :], start=True, stop=False)
            ins = nc.tensor.matmul(self.psO[:, 1, o:o + W], pr[:, SEQ:CAUSAL3], self.v_rows[:, 1, h, :],
                                   start=False, stop=True)
        ins.then_inc(self.pv_done, 1)

    def scalar(self, nc, act, ring, use_k, evacuated, scale):
        nb = self.tr_banks
        self._unflip(nc, act, self.kT, ring, use_k, 0, evacuated)
        self._unflip(nc, act, self.qT, ring, use_k + nb, nb, evacuated)
        self._unflip(nc, act, self.qT, ring, use_k + 2 * nb, 2 * nb, evacuated)
        for g in range(self.groups):
            act.wait_ge(self.second_done, g + 1)
            if g >= 4:
                act.wait_ge(self.pv_done, g - 3)
            src = self.psS[:, (g % 2) * self.SLOT:(g % 2 + 1) * self.SLOT, 0:CAUSAL3]
            nc.scalar.activation(self.probs[:, g % 4, :, :], src, ACT.Exp, scale=scale).then_inc(self.exp_done, 1)

    def vector(self, nc, dve, link):
        for g in range(self.groups):
            dve.wait_ge(self.first_done, g + 1)
            for t, (a, b) in enumerate(((0, P), (P, CAUSAL3))):
                src = self.psS[:, (g % 2) * self.SLOT:(g % 2 + 1) * self.SLOT, a:b]
                h = g * self.SLOT
                to = (self.q_rows[:, t, h:h + self.SLOT, self.k_first] if self.parts == 1
                      else self.negmax[:, t, h:h + self.SLOT])
                ins = nc.vector.tensor_reduce(to, src, AX_X, ALU.max, negate=True)
            ins.then_inc(self.max_taken, 1)
        dve.wait_ge(self.max_taken, self.groups)
        if self.parts == 1:
            link(nc.vector.tensor_copy(self.rsum[:, 0, 0:1], self.q_rows[:, 0, 0, self.k_first:self.k_first + 1]))
        else:
            lead = self.q_rows[:, :, :, self.k_first]
            link(nc.vector.tensor_copy(lead, self.negmax[:]))
            link(nc.vector.tensor_tensor(self.q_rows[:, :, :, self.k_first + 1], self.negmax[:], lead, ALU.subtract))
        nc.vector.memset(self.rsum[:, 0, 0:1], 0.0).then_inc(self.max_placed, 1)
        W = self.D + 1
        per = self.round_groups * self.SLOT
        for r in range(self.rounds):
            dve.wait_ge(self.pv_done, (r + 1) * self.round_groups)
            dve.wait_ge(self.max_placed, 1)
            hs = slice(r * per, (r + 1) * per)
            for t in range(2):
                view = self.psO[:, t, 0:per * W].rearrange("p (h w) -> p h w", w=W)
                ins = nc.vector.reciprocal(self.rsum[:, t, hs], view[:, :, self.D])
            link(ins)
            for t in range(2):
                view = self.psO[:, t, 0:per * W].rearrange("p (h w) -> p h w", w=W)
                ins = nc.vector.tensor_tensor(self.o_rows[:, t, hs, :], view[:, :, 0:self.D],
                                              spread(self.rsum[:, t, hs], 2, [P, per, self.D]), ALU.mult)
            ins.then_inc(self.o_ready, 1)


def load_block(nc, s, pairs):
    landed = s.sem("loaded")
    with nc.Block() as block:
        @block.sync
        def _(sp):
            for to, src in pairs:
                sp.dma_start(to, src).then_inc(landed, 16)
            sp.wait_ge(landed, 16 * len(pairs))


def cross_attention(nc, x, C, D, layer, rounded):
    H, HD = 16, 16
    with ExitStack() as ctx:
        s = Stage(nc, ctx, f"x{layer}")
        wdt = BF16 if rounded else F32
        wq, wkv = s.sb("wq", [P, KD, DIM], wdt), s.sb("wkv", [P, KD, 2 * DIM], wdt)
        wo = s.sb("wo", [P, KD, DIM], wdt)
        bq, bkv, bo = s.sb("bq", [P, DIM], wdt), s.sb("bkv", [P, 2 * DIM], wdt), s.sb("bo", [P, DIM], wdt)
        pairs = []
        staged = []
        for to, name in ((wq, "wqT"), (wkv, "wkvT"), (wo, "woT"), (bq, "bq"), (bkv, "bkv"), (bo, "bo")):
            src = D[f"L{layer}_{name}"]
            if name[0] == "b":
                src = src.partition_broadcast(P)
            if rounded:
                raw = s.sb(f"raw_{name}", list(to.shape))
                staged.append((to, raw))
                pairs.append((raw[:], src))
            else:
                pairs.append((to[:], src))
        if rounded:
            keep = s.sb("key_mask", [P, TILES], I32)
            blocked = s.sb("blocked", [P, TILES])
            pairs.append((keep[:], D["mask_if1"]))
        load_block(nc, s, pairs)

        psA = [s.ps(f"work{i}", [P, BANK]) for i in range(2)]
        att = Attention(s, H, HD, 32, wdt, 2 if rounded else 1, 1 if rounded else 0, None)
        ln = LayerNorm(s, 2)
        xnb = s.sb("xn_bf", [P, 2, DIM], BF16) if rounded else None
        ctxT = s.sb("ctxT", [P, KD, SEQ])
        ctxTb = s.sb("ctxT_bf", [P, KD, SEQ], BF16) if rounded else ctxT
        xnT = s.sb("xnT", [P, KD, SEQ], wdt)
        oT = s.sb("oT", [P, KD, SEQ], wdt)
        ob = s.sb("o_bf", [P, 2, DIM], BF16) if rounded else None
        raw = s.sb("qk_raw", [P, 2, 2, H, HD], wdt)
        biased = s.sb("biased", [P, 2, 2, DIM], BF16) if rounded else None
        vr = s.sb("v_raw", [P, 2, DIM], BF16) if rounded else None
        rot = s.sb("rotary", [P, 2, 2, H, HD // 2]) if not rounded else None
        prod = s.sb("outproj_bf", [P, 2, DIM], BF16) if rounded else None
        sem = {n: s.sem(n) for n in ("link", "ctx_landed", "ctx_cast", "kv_done", "x_turned", "q_done", "by_act",
                                     "by_dve", "x_bf", "o_bf", "o_turned", "out_done", "bias_added", "x_ready",
                                     "weights_cast")}

        with nc.Block() as block:
            @block.vector
            def _(dve):
                link = chain(dve, sem["link"])
                for to, r in staged:
                    nc.vector.tensor_copy(to[:], r[:])
                att.clear(nc)
                link(nc.vector.memset(raw[:], 0.0))
                att.clear_ones(nc)
                if rounded:
                    link(nc.vector.tensor_scalar(blocked[:], keep[:], 0.0, MASKED, ALU.is_le, ALU.mult))
                link(nc.vector.memset(raw[:], 0.0))
        s.again()

        A, V = sem["by_act"], sem["by_dve"]
        readers = [V, V, A, V, V, A, A, A, A, A, A, A, V, V]
        USE_Q, USE_K = 3, 5
        ident = C["ident_bf"] if rounded else C["ident"]

        with nc.Fori(0, BATCH) as b:
            with nc.Block() as block:
                def parts(t):
                    return [x[:, b * 2 + t, :]]

                @block.sync
                def _(sp):
                    sp.dma_start(ctxT[:], D["ctxT"][b]).then_inc(sem["ctx_landed"], 16)

                @block.gpsimd
                def _(pool):
                    if rounded:
                        pool.wait_ge(sem["ctx_landed"], 16)
                        nc.gpsimd.tensor_copy(ctxTb[:], ctxT[:]).then_inc(sem["ctx_cast"], 1)
                    ln.root(nc, pool, C["minus_half"])
                    if not rounded:
                        pool.wait_ge(ln.xn_ready, 1)
                        for t in range(2):
                            ins = nc.gpsimd.tensor_tensor(x[:, b * 2 + t, :], x[:, b * 2 + t, :], bo[:], ALU.add)
                        ins.then_inc(sem["bias_added"], 1)

                @block.tensor
                def _(pe):
                    ring = Ring(psA, readers)
                    if rounded:
                        pe.wait_ge(sem["ctx_cast"], 1)
                    else:
                        pe.wait_ge(sem["ctx_landed"], 16)
                    for t in range(2):
                        bank = ring.claim(pe)
                        for k in range(KD):
                            ins = nc.tensor.matmul(bank[:], ctxTb[:, k, t * P:(t + 1) * P], wkv[:, k, :],
                                                   start=(k == 0), stop=(k == KD - 1))
                        ins.then_inc(sem["kv_done"], 1)
                    bank = ring.claim(pe)
                    view = bank[:].bitcast(BF16) if rounded else bank[:]
                    src = xnb if rounded else ln.xn
                    pe.wait_ge(sem["x_bf"] if rounded else ln.xn_ready, 1)
                    for k in range(KD):
                        for t in range(2):
                            ins = nc.tensor.transpose(view[:, k * SEQ + t * P:k * SEQ + (t + 1) * P],
                                                      src[:, t, k * P:(k + 1) * P], ident[:])
                    ins.then_inc(sem["x_turned"], 1)
                    pe.wait_ge(A, 1)
                    for t in range(2):
                        bank = ring.claim(pe)
                        for k in range(KD):
                            ins = nc.tensor.matmul(bank[:, 0:DIM], xnT[:, k, t * P:(t + 1) * P], wq[:, k, :],
                                                   start=(k == 0), stop=(k == KD - 1))
                        ins.then_inc(sem["q_done"], 1)
                    m = (lambda h: C["causal_q"][:]) if rounded else (lambda h: C["causal_q" if h < 4 else "window_q"][:])
                    mk = (lambda h: C["causal_k"][:]) if rounded else (lambda h: C["causal_k" if h < 4 else "window_k"][:])
                    att.tensor(nc, pe, ring, ident, C["ident_bf"], m, mk, A, 1)
                    bank = ring.claim(pe)
                    view = bank[:].bitcast(BF16) if rounded else bank[:]
                    pe.wait_ge(sem["o_bf"] if rounded else att.o_ready, 1)
                    orow = ob if rounded else att.o_rows
                    for k in range(KD):
                        for t in range(2):
                            src = (orow[:, t, k * P:(k + 1) * P] if rounded else
                                   orow[:, t, k * 8:(k + 1) * 8, :].rearrange("p h d -> p (h d)"))
                            ins = nc.tensor.transpose(view[:, k * SEQ + t * P:k * SEQ + (t + 1) * P], src, ident[:])
                    ins.then_inc(sem["o_turned"], 1)
                    pe.wait_ge(A, 8)
                    for t in range(2):
                        bank = ring.claim(pe)
                        for k in range(KD):
                            ins = nc.tensor.matmul(bank[:, 0:DIM], oT[:, k, t * P:(t + 1) * P], wo[:, k, :],
                                                   start=(k == 0), stop=(k == KD - 1))
                        ins.then_inc(sem["out_done"], 1)

                @block.scalar
                def _(act):
                    ring = Ring(psA, readers)
                    act.wait_ge(sem["x_turned"], 1)
                    view = ring.bank(2)[:].bitcast(BF16) if rounded else ring.bank(2)[:]
                    nc.scalar.copy(xnT[:], view[:, 0:KD * SEQ].rearrange("p (k t) -> p k t", k=KD)).then_inc(A, 1)
                    att.scalar(nc, act, ring, USE_K, A, 1.0 / HD ** 0.5)
                    act.wait_ge(sem["o_turned"], 1)
                    view = ring.bank(11)[:].bitcast(BF16) if rounded else ring.bank(11)[:]
                    nc.scalar.copy(oT[:], view[:, 0:KD * SEQ].rearrange("p (k t) -> p k t", k=KD)).then_inc(A, 1)

                @block.vector
                def _(dve):
                    ring = Ring(psA, readers)
                    link = chain(dve, sem["link"])
                    ln.statistics(nc, link, parts)
                    ln.apply(nc, dve, parts)
                    if rounded:
                        dve.wait_ge(ln.xn_ready, 1)
                        nc.vector.tensor_copy(xnb[:], ln.xn[:]).then_inc(sem["x_bf"], 1)
                    for t in range(2):
                        dve.wait_ge(sem["kv_done"], t + 1)
                        bank = ring.bank(t)
                        k_to = raw[:, t, 1].rearrange("p h d -> p (h d)")
                        if rounded:
                            nc.vector.tensor_copy(biased[:, t, 1, :], bank[:, 0:DIM])
                            nc.vector.tensor_copy(vr[:, t, :], bank[:, DIM:2 * DIM]).then_inc(V, 1)
                        else:
                            nc.vector.tensor_tensor(k_to, bank[:, 0:DIM], bkv[:, 0:DIM], ALU.add)
                            nc.vector.tensor_tensor(att.v_rows[:, t, :, 0:HD],
                                                    bank[:, DIM:2 * DIM].rearrange("p (h d) -> p h d", h=H),
                                                    bkv[:, DIM:2 * DIM].rearrange("p (h d) -> p h d", h=H),
                                                    ALU.add).then_inc(V, 1)
                    dve.wait_ge(V, 2)
                    if rounded:
                        for t in range(2):
                            nc.vector.tensor_tensor(att.k_rows[:, t, :, 0:HD],
                                                    biased[:, t, 1, :].rearrange("p (h d) -> p h d", h=H),
                                                    bkv[:, 0:DIM].rearrange("p (h d) -> p h d", h=H), ALU.add)
                            nc.vector.tensor_copy(att.k_rows[:, t, :, HD:HD + 1],
                                                  blocked[:, bass.ds(b * 2 + t, 1)].unsqueeze(1).to_broadcast([P, H, 1]))
                            ins = nc.vector.tensor_tensor(vr[:, t, :], vr[:, t, :], bkv[:, DIM:2 * DIM], ALU.add)
                        ins.then_inc(att.k_ready, 1)
                        dve.wait_ge(att.k_ready, 1)
                        for t in range(2):
                            ins = nc.vector.tensor_copy(att.v_rows[:, t, :, 0:HD],
                                                        vr[:, t, :].rearrange("p (h d) -> p h d", h=H))
                        ins.then_inc(att.v_ready, 1)
                    else:
                        nc.vector.memset(att.v_rows[:, :, :, HD:HD + 1], 1.0).then_inc(att.v_ready, 1)

                    def rotary(which, to, ready):
                        cos, sin = C["rope_cos"], C["rope_sin"]
                        for t in range(2):
                            even, odd = raw[:, t, which, :, 0:HD:2], raw[:, t, which, :, 1:HD:2]
                            shape = [P, H, HD // 2]
                            ct, st = spread(cos[:, t, :], 1, shape), spread(sin[:, t, :], 1, shape)
                            out_e, out_o = to[:, t, :, 0:HD:2], to[:, t, :, 1:HD:2]
                            nc.vector.tensor_tensor(rot[:, t, 0], even, st, ALU.mult)
                            nc.vector.tensor_tensor(rot[:, t, 1], odd, st, ALU.mult)
                            nc.vector.tensor_tensor(out_e, even, ct, ALU.mult)
                            link(nc.vector.tensor_tensor(out_o, odd, ct, ALU.mult))
                            nc.vector.tensor_tensor(out_e, out_e, rot[:, t, 1], ALU.subtract)
                            ins = nc.vector.tensor_tensor(out_o, out_o, rot[:, t, 0], ALU.add)
                            if t:
                                ins.then_inc(ready, 1)

                    if not rounded:
                        rotary(1, att.k_rows, att.k_ready)
                        dve.wait_ge(att.k_ready, 1)
                    for t in range(2):
                        dve.wait_ge(sem["q_done"], t + 1)
                        bank = ring.bank(USE_Q + t)
                        if rounded:
                            nc.vector.tensor_copy(biased[:, t, 0, :], bank[:, 0:DIM]).then_inc(V, 1)
                        else:
                            nc.vector.tensor_tensor(raw[:, t, 0].rearrange("p h d -> p (h d)"), bank[:, 0:DIM],
                                                    bq[:], ALU.add).then_inc(V, 1)
                    dve.wait_ge(V, 4)
                    if rounded:
                        for t in range(2):
                            ins = nc.vector.tensor_tensor(att.q_rows[:, t, :, 0:HD],
                                                          biased[:, t, 0, :].rearrange("p (h d) -> p h d", h=H),
                                                          bq[:].rearrange("p (h d) -> p h d", h=H), ALU.add)
                        ins.then_inc(att.q_ready, 1)
                    else:
                        rotary(0, att.q_rows, att.q_ready)
                    att.vector(nc, dve, link)
                    if rounded:
                        dve.wait_ge(att.o_ready, 1)
                        nc.vector.tensor_copy(ob[:], att.o_rows[:].rearrange("p t h d -> p t (h d)")).then_inc(sem["o_bf"], 1)
                    for t in range(2):
                        dve.wait_ge(sem["out_done"], t + 1)
                        bank = ring.bank(12 + t)
                        if rounded:
                            link(nc.vector.tensor_copy(prod[:, t, :], bank[:, 0:DIM]))
                            link(nc.vector.tensor_tensor(prod[:, t, :], prod[:, t, :], bo[:], ALU.add))
                            nc.vector.tensor_tensor(x[:, b * 2 + t, :], x[:, b * 2 + t, :], prod[:, t, :],
                                                    ALU.add).then_inc(V, 1)
                        else:
                            dve.wait_ge(sem["bias_added"], 1)
                            nc.vector.tensor_tensor(x[:, b * 2 + t, :], x[:, b * 2 + t, :], bank[:, 0:DIM],
                                                    ALU.add).then_inc(V, 1)
            s.again()


def turn_rows(nc, bank, rows, ident, tiles, width):
    for k in range(width // P):
        for t in range(tiles):
            at = (k * tiles + t) * P
            ins = nc.tensor.transpose(bank[:, at:at + P], rows[:, t, k * P:(k + 1) * P], ident[:])
    return ins


def linear_attention(nc, x, C, D):
    H, HD = 16, 16
    with ExitStack() as ctx:
        s = Stage(nc, ctx, "x1")
        wq, wkv, wo = s.sb("wq", [P, KD, DIM]), s.sb("wkv", [P, KD, 2 * DIM]), s.sb("wo", [P, KD, DIM])
        bq, bkv, bo = s.sb("bq", [P, KD]), s.sb("bkv", [P, 2 * DIM]), s.sb("bo", [P, DIM])
        dropped = s.sb("dropped", [P, TILES], U8)
        keep = s.sb("keep", [P, TILES])
        load_block(nc, s, [(wq[:], D["L1_wqT"]), (wkv[:], D["L1_wkvT"]), (wo[:], D["L1_woT"]),
                           (bq[:], D["L1_bq_col"]), (bkv[:], D["L1_bkv"].partition_broadcast(P)),
                           (bo[:], D["L1_bo"].partition_broadcast(P)), (dropped[:], D["mask_bk1"])])
        ps_kv = [s.ps(f"kv{t}", [P, BANK]) for t in range(2)]
        ps_x = s.ps("turned", [P, BANK])
        ps_q = [s.ps(f"q{c}", [P, BANK]) for c in range(KD)]
        ps_m = s.ps("key_value", [P, BANK])
        ps_y = [s.ps(f"out{t}", [P, BANK]) for t in range(2)]
        ln = LayerNorm(s, 2)
        ctxT, xnT = s.sb("ctxT", [P, KD, SEQ]), s.sb("xnT", [P, KD, SEQ])
        k_raw, k_neg, k_exp, k_sq = (s.sb(n, [P, 2, DIM]) for n in ("k_raw", "k_neg", "k_exp", "k_sq"))
        k_ss, k_rn = s.sb("k_ss", [P, 2 * H]), s.sb("k_rn", [P, 2 * H])
        q_raw, q_neg, q_exp, q_sq = (s.sb(n, [P, KD, SEQ]) for n in ("q_raw", "q_neg", "q_exp", "q_sq"))
        q_ss, q_rn = s.sb("q_ss", [P, KD]), s.sb("q_rn", [P, KD])
        v = s.sb("v", [P, 2, DIM])
        m = s.sb("m", [P, KD, P])
        oT = s.sb("oT", [P, KD, SEQ])
        sem = {n: s.sem(n) for n in ("link", "ctx_landed", "kv_done", "x_turned", "xnT_ready", "q_done", "k_neg",
                                     "k_exp", "k_ss", "k_bounded", "k_rn", "k_ready", "q_neg", "q_exp", "q_ready", "q_ss",
                                     "q_bounded", "q_rn", "m_done", "m_ready", "o_done", "o_ready", "y_done",
                                     "bias_added", "x_ready")}
        with nc.Block() as block:
            @block.vector
            def _(dve):
                link = chain(dve, sem["link"])
                link(nc.vector.tensor_scalar(keep[:], dropped[:], -1.0, 1.0, ALU.mult, ALU.add))
        s.again()
        with nc.Fori(0, BATCH) as b:
            with nc.Block() as block:
                def parts(t):
                    return [x[:, b * 2 + t, :]]

                @block.sync
                def _(sp):
                    sp.dma_start(ctxT[:], D["ctxT"][b]).then_inc(sem["ctx_landed"], 16)

                @block.gpsimd
                def _(pool):
                    ln.root(nc, pool, C["minus_half"])
                    pool.wait_ge(ln.xn_ready, 1)
                    for t in range(2):
                        ins = nc.gpsimd.tensor_tensor(x[:, b * 2 + t, :], x[:, b * 2 + t, :], bo[:], ALU.add)
                    ins.then_inc(sem["bias_added"], 1)
                    pool.wait_ge(sem["k_ss"], 1)
                    nc.gpsimd.tensor_scalar(k_ss[:], k_ss[:], TINY_SQ, None, ALU.max).then_inc(sem["k_bounded"], 1)
                    pool.wait_ge(sem["k_bounded"], 1)
                    nc.gpsimd.tensor_tensor(k_rn[:], k_ss[:], C["minus_half"][:, 0:2 * H], ALU.pow).then_inc(sem["k_rn"], 1)
                    pool.wait_ge(sem["q_ss"], KD)
                    nc.gpsimd.tensor_scalar(q_ss[:], q_ss[:], TINY_SQ, None, ALU.max).then_inc(sem["q_bounded"], 1)
                    pool.wait_ge(sem["q_bounded"], 1)
                    nc.gpsimd.tensor_tensor(q_rn[:], q_ss[:], C["minus_half"][:, 0:KD], ALU.pow).then_inc(sem["q_rn"], 1)

                @block.tensor
                def _(pe):
                    pe.wait_ge(sem["ctx_landed"], 16)
                    for t in range(2):
                        for k in range(KD):
                            ins = nc.tensor.matmul(ps_kv[t][:], ctxT[:, k, t * P:(t + 1) * P], wkv[:, k, :],
                                                   start=(k == 0), stop=(k == KD - 1))
                        ins.then_inc(sem["kv_done"], 1)
                    pe.wait_ge(ln.xn_ready, 1)
                    turn_rows(nc, ps_x, ln.xn, C["ident"], 2, DIM).then_inc(sem["x_turned"], 1)
                    pe.wait_ge(sem["xnT_ready"], 1)
                    for c in range(KD):
                        for k in range(KD):
                            ins = nc.tensor.matmul(ps_q[c][:, 0:SEQ], wq[:, k, c * P:(c + 1) * P], xnT[:, k, :],
                                                   start=(k == 0), stop=(k == KD - 1))
                        ins.then_inc(sem["q_done"], 1)
                    pe.wait_ge(sem["k_ready"], 1)
                    for c in range(KD):
                        for t in range(2):
                            ins = nc.tensor.matmul(ps_m[:, c * P:(c + 1) * P], k_exp[:, t, c * P:(c + 1) * P],
                                                   v[:, t, c * P:(c + 1) * P], start=(t == 0), stop=(t == 1))
                    ins.then_inc(sem["m_done"], 1)
                    pe.wait_ge(sem["m_ready"], 1)
                    for c in range(KD):
                        ins = nc.tensor.matmul(ps_q[c][:, 0:SEQ], m[:, c, :], q_exp[:, c, :], start=True, stop=True)
                        ins.then_inc(sem["o_done"], 1)
                    pe.wait_ge(sem["o_ready"], KD)
                    for t in range(2):
                        for k in range(KD):
                            ins = nc.tensor.matmul(ps_y[t][:, 0:DIM], oT[:, k, t * P:(t + 1) * P], wo[:, k, :],
                                                   start=(k == 0), stop=(k == KD - 1))
                        ins.then_inc(sem["y_done"], 1)

                @block.scalar
                def _(act):
                    act.wait_ge(sem["k_neg"], 1)
                    nc.scalar.activation(k_exp[:], k_neg[:], ACT.Exp).then_inc(sem["k_exp"], 1)
                    act.wait_ge(sem["x_turned"], 1)
                    nc.scalar.copy(xnT[:], ps_x[:].rearrange("p (k t) -> p k t", k=KD)).then_inc(sem["xnT_ready"], 1)
                    act.wait_ge(sem["q_neg"], 1)
                    nc.scalar.activation(q_exp[:], q_neg[:], ACT.Exp).then_inc(sem["q_exp"], 1)
                    act.wait_ge(sem["q_ready"], 1)
                    for c in range(KD):
                        nc.scalar.activation(q_sq[:, c, :], q_exp[:, c, :], ACT.Square,
                                             accum_out=q_ss[:, c:c + 1]).then_inc(sem["q_ss"], 1)
                    for c in range(KD):
                        act.wait_ge(sem["o_done"], c + 1)
                        nc.scalar.copy(oT[:, c, :], ps_q[c][:, 0:SEQ]).then_inc(sem["o_ready"], 1)

                @block.vector
                def _(dve):
                    link = chain(dve, sem["link"])
                    ln.statistics(nc, link, parts)
                    ln.apply(nc, dve, parts)
                    for t in range(2):
                        dve.wait_ge(sem["kv_done"], t + 1)
                        nc.vector.tensor_tensor(k_raw[:, t, :], ps_kv[t][:, 0:DIM], bkv[:, 0:DIM], ALU.add)
                        ins = nc.vector.tensor_tensor(v[:, t, :], ps_kv[t][:, DIM:2 * DIM], bkv[:, DIM:2 * DIM], ALU.add)
                    link(ins)
                    nc.vector.tensor_scalar(k_neg[:], k_raw[:], 0.0, None, ALU.min).then_inc(sem["k_neg"], 1)
                    dve.wait_ge(sem["k_exp"], 1)
                    link(nc.vector.scalar_tensor_tensor(k_exp[:], k_raw[:], 0.0, k_exp[:], ALU.max, ALU.add))
                    for t in range(2):
                        ins = nc.vector.tensor_scalar(k_exp[:, t, :], k_exp[:, t, :], keep[:, bass.ds(b * 2 + t, 1)], None, ALU.mult)
                    link(ins)
                    link(nc.vector.tensor_tensor(k_sq[:], k_exp[:], k_exp[:], ALU.mult))
                    nc.vector.tensor_reduce(k_ss[:], k_sq[:].rearrange("p t (h d) -> p (t h) d", h=H), AX_X,
                                            ALU.add).then_inc(sem["k_ss"], 1)
                    for c in range(KD):
                        dve.wait_ge(sem["q_done"], c + 1)
                        ins = nc.vector.tensor_scalar(q_raw[:, c, :], ps_q[c][:, 0:SEQ], bq[:, c:c + 1], None, ALU.add)
                    link(ins)
                    nc.vector.tensor_scalar(q_neg[:], q_raw[:], 0.0, None, ALU.min).then_inc(sem["q_neg"], 1)
                    dve.wait_ge(sem["k_rn"], 1)
                    heads = k_exp[:].rearrange("p t (h d) -> p (t h) d", h=H)
                    nc.vector.tensor_tensor(heads, heads, spread(k_rn[:], 2, [P, 2 * H, HD]),
                                            ALU.mult).then_inc(sem["k_ready"], 1)
                    dve.wait_ge(sem["q_exp"], 1)
                    nc.vector.scalar_tensor_tensor(q_exp[:], q_raw[:], 0.0, q_exp[:], ALU.max,
                                                   ALU.add).then_inc(sem["q_ready"], 1)
                    dve.wait_ge(sem["m_done"], 1)
                    dve.wait_ge(sem["q_rn"], 1)
                    for c in range(KD):
                        ins = nc.vector.scalar_tensor_tensor(m[:, c, :], ps_m[:, c * P:(c + 1) * P], q_rn[:, c:c + 1],
                                                             C["head_blocks"][:], ALU.mult, ALU.mult)
                    ins.then_inc(sem["m_ready"], 1)
                    dve.wait_ge(sem["bias_added"], 1)
                    for t in range(2):
                        dve.wait_ge(sem["y_done"], t + 1)
                        nc.vector.tensor_tensor(x[:, b * 2 + t, :], x[:, b * 2 + t, :], ps_y[t][:, 0:DIM],
                                                ALU.add).then_inc(sem["x_ready"], 1)
            s.again()


def memory_attention(nc, x, C, D):
    with ExitStack() as ctx:
        s = Stage(nc, ctx, "x3")
        wq, wk, wo = (s.sb(n, [P, KD, DIM]) for n in ("wq", "wk", "wo"))
        bq, bk, bo = s.sb("bq", [P, KD]), s.sb("bk", [P, KD]), s.sb("bo", [P, DIM])
        load_block(nc, s, [(wq[:], D["L3_wqT"]), (wk[:], D["L3_wkT"]), (wo[:], D["L3_woT"]),
                           (bq[:], D["L3_bq_col"]), (bk[:], D["L3_bk_col"]),
                           (bo[:], D["L3_bo"].partition_broadcast(P))])
        ps_k = s.ps("k", [P, KD * SEQ])
        ps_x = s.ps("turned", [P, BANK])
        ps_q = s.ps("q", [P, KD * SEQ])
        ps_s = [s.ps(f"scores{t}", [P, BANK]) for t in range(2)]
        ps_p = s.ps("probs_turned", [P, BANK])
        ps_o = s.ps("o", [P, KD * SEQ])
        ps_y = s.ps("out", [P, BANK])
        ln = LayerNorm(s, 2)
        ctxT, xnT = s.sb("ctxT", [P, KD, SEQ]), s.sb("xnT", [P, KD, SEQ])
        ctx_rows = s.sb("ctx_rows", [P, 2, DIM])
        masked, mrow, ones = s.sb("masked", [1, SEQ], U8), s.sb("mask_row", [1, SEQ]), s.sb("ones", [1, P])
        kT, qT = s.sb("kT", [P, KD, SEQ]), s.sb("qT", [P, KD, SEQ])
        negmax, rsum, rinv = s.sb("negmax", [P, 2]), s.sb("rsum", [P, 2]), s.sb("rinv", [P, 2])
        probs, pT, oT = s.sb("probs", [P, 2, SEQ]), s.sb("pT", [P, 2, SEQ]), s.sb("oT", [P, KD, SEQ])
        sem = {n: s.sem(n) for n in ("link", "ctx_landed", "rows_landed", "mask_landed", "mask_ready", "k_done",
                                     "kT_ready", "x_turned", "xnT_ready", "q_done", "qT_ready", "s_done",
                                     "max_ready", "exp_done", "p_ready", "p_turned", "pT_ready", "o_done",
                                     "oT_ready", "y_done", "bias_added", "x_ready")}
        with nc.Fori(0, BATCH) as b:
            with nc.Block() as block:
                def parts(t):
                    return [x[:, b * 2 + t, :]]

                @block.sync
                def _(sp):
                    sp.dma_start(ctxT[:], D["ctxT"][b]).then_inc(sem["ctx_landed"], 16)
                    sp.dma_start(masked[:], D["mask_bk0"][bass.ds(b, 1), :]).then_inc(sem["mask_landed"], 16)
                    sp.dma_start(ctx_rows[:], D["ctx"][b]).then_inc(sem["rows_landed"], 16)

                @block.gpsimd
                def _(pool):
                    ln.root(nc, pool, C["minus_half"])
                    pool.wait_ge(ln.xn_ready, 1)
                    for t in range(2):
                        ins = nc.gpsimd.tensor_tensor(x[:, b * 2 + t, :], x[:, b * 2 + t, :], bo[:], ALU.add)
                    ins.then_inc(sem["bias_added"], 1)

                @block.tensor
                def _(pe):
                    pe.wait_ge(sem["ctx_landed"], 16)
                    for c in range(KD):
                        for k in range(KD):
                            ins = nc.tensor.matmul(ps_k[:, c * SEQ:(c + 1) * SEQ], wk[:, k, c * P:(c + 1) * P],
                                                   ctxT[:, k, :], start=(k == 0), stop=(k == KD - 1))
                    ins.then_inc(sem["k_done"], 1)
                    pe.wait_ge(ln.xn_ready, 1)
                    turn_rows(nc, ps_x, ln.xn, C["ident"], 2, DIM).then_inc(sem["x_turned"], 1)
                    pe.wait_ge(sem["xnT_ready"], 1)
                    for c in range(KD):
                        for k in range(KD):
                            ins = nc.tensor.matmul(ps_q[:, c * SEQ:(c + 1) * SEQ], wq[:, k, c * P:(c + 1) * P],
                                                   xnT[:, k, :], start=(k == 0), stop=(k == KD - 1))
                    ins.then_inc(sem["q_done"], 1)
                    pe.wait_ge(sem["mask_ready"], 1)
                    pe.wait_ge(sem["kT_ready"], KD)
                    pe.wait_ge(sem["qT_ready"], KD)
                    for t in range(2):
                        nc.tensor.matmul(ps_s[t][:, 0:SEQ], ones[:], mrow[:], start=True, stop=False)
                        for c in range(KD):
                            ins = nc.tensor.matmul(ps_s[t][:, 0:SEQ], qT[:, c, t * P:(t + 1) * P], kT[:, c, :],
                                                   start=False, stop=(c == KD - 1))
                        ins.then_inc(sem["s_done"], 1)
                    pe.wait_ge(sem["p_ready"], 2)
                    turn_rows(nc, ps_p, probs, C["ident"], 2, SEQ).then_inc(sem["p_turned"], 1)
                    pe.wait_ge(sem["pT_ready"], 1)
                    pe.wait_ge(sem["rows_landed"], 16)
                    for c in range(KD):
                        for k in range(2):
                            ins = nc.tensor.matmul(ps_o[:, c * SEQ:(c + 1) * SEQ], ctx_rows[:, k, c * P:(c + 1) * P],
                                                   pT[:, k, :], start=(k == 0), stop=(k == 1))
                    ins.then_inc(sem["o_done"], 1)
                    pe.wait_ge(sem["oT_ready"], 1)
                    for t in range(2):
                        for k in range(KD):
                            ins = nc.tensor.matmul(ps_y[:, t * DIM:(t + 1) * DIM], oT[:, k, t * P:(t + 1) * P],
                                                   wo[:, k, :], start=(k == 0), stop=(k == KD - 1))
                    ins.then_inc(sem["y_done"], 1)

                @block.scalar
                def _(act):
                    act.wait_ge(sem["k_done"], 1)
                    for c in range(KD):
                        nc.scalar.activation(kT[:, c, :], ps_k[:, c * SEQ:(c + 1) * SEQ], ACT.Identity,
                                             bias=bk[:, c:c + 1]).then_inc(sem["kT_ready"], 1)
                    act.wait_ge(sem["x_turned"], 1)
                    nc.scalar.copy(xnT[:], ps_x[:].rearrange("p (k t) -> p k t", k=KD)).then_inc(sem["xnT_ready"], 1)
                    act.wait_ge(sem["q_done"], 1)
                    for c in range(KD):
                        nc.scalar.activation(qT[:, c, :], ps_q[:, c * SEQ:(c + 1) * SEQ], ACT.Identity,
                                             bias=bq[:, c:c + 1]).then_inc(sem["qT_ready"], 1)
                    for t in range(2):
                        act.wait_ge(sem["max_ready"], t + 1)
                        nc.scalar.activation(probs[:, t, :], ps_s[t][:, 0:SEQ], ACT.Exp, bias=negmax[:, t:t + 1],
                                             accum_out=rsum[:, t:t + 1]).then_inc(sem["exp_done"], 1)
                    act.wait_ge(sem["p_turned"], 1)
                    nc.scalar.copy(pT[:], ps_p[:].rearrange("p (k t) -> p k t", k=2)).then_inc(sem["pT_ready"], 1)
                    act.wait_ge(sem["o_done"], 1)
                    nc.scalar.copy(oT[:], ps_o[:].rearrange("p (k t) -> p k t", k=KD)).then_inc(sem["oT_ready"], 1)

                @block.vector
                def _(dve):
                    link = chain(dve, sem["link"])
                    ln.statistics(nc, link, parts)
                    ln.apply(nc, dve, parts)
                    dve.wait_ge(sem["mask_landed"], 16)
                    nc.vector.memset(ones[:], 1.0)
                    nc.vector.tensor_scalar(mrow[:], masked[:], MASKED, None, ALU.mult).then_inc(sem["mask_ready"], 1)
                    for t in range(2):
                        dve.wait_ge(sem["s_done"], t + 1)
                        nc.vector.tensor_reduce(negmax[:, t:t + 1], ps_s[t][:, 0:SEQ], AX_X, ALU.max,
                                                negate=True).then_inc(sem["max_ready"], 1)
                    for t in range(2):
                        dve.wait_ge(sem["exp_done"], t + 1)
                        link(nc.vector.reciprocal(rinv[:, t:t + 1], rsum[:, t:t + 1]))
                        nc.vector.tensor_scalar(probs[:, t, :], probs[:, t, :], rinv[:, t:t + 1], None,
                                                ALU.mult).then_inc(sem["p_ready"], 1)
                    dve.wait_ge(sem["bias_added"], 1)
                    dve.wait_ge(sem["y_done"], 1)
                    for t in range(2):
                        nc.vector.tensor_tensor(x[:, b * 2 + t, :], x[:, b * 2 + t, :], ps_y[:, t * DIM:(t + 1) * DIM],
                                                ALU.add).then_inc(sem["x_ready"], 1)
            s.again()


def mixture(nc, x, C, D, layer):
    gated = layer == 3
    FT = -(-(704 if gated else 512) // P)
    HID = FT * P
    CHUNK = 4
    CHUNKS = TILES // CHUNK
    TOK = CHUNK * P
    ups = 2 if gated else 1
    up_at = [0, KD * HID]
    b1_at = KD * HID
    down_at = ups * KD * HID + (0 if gated else FT)
    size = down_at + FT * DIM
    with ExitStack() as ctx:
        s = Stage(nc, ctx, f"f{layer}")
        gate = s.sb("gate", [P, KD, EXPERTS])
        iota = C["iota8"]
        w_all = s.sb("w_all", [P, TILES, EXPERTS])
        xH, xL = (s.sb(n, [P, KD, TILES * P], F32R) for n in ("x_high", "x_low"))
        pairs = [(gate[:], D[f"L{layer}_gate"])]
        if not gated:
            b2 = s.sb("b2", [EXPERTS, DIM])
            pairs.append((b2[:], D["L0_b2"]))
        load_block(nc, s, pairs)

        with ExitStack() as front:
            g = Stage(nc, front, f"g{layer}")
            ln = LayerNorm(g, CHUNK)
            part = g.sb("xnT_part", [P, KD, TOK])
            ps_x = [g.ps(f"turned{k}", [P, BANK]) for k in range(KD)]
            ps_g = g.ps("logits", [P, CHUNK * EXPERTS])
            ps_w = g.ps("w_turned", [EXPERTS, TOK])
            ps_y = [g.ps(f"bias{t}", [P, DIM]) for t in range(CHUNK)]
            logit, prob, chosen, hot = (g.sb(n, [P, CHUNK, EXPERTS]) for n in ("logit", "prob", "chosen", "hot"))
            top, index, index_f = g.sb("top", [P, CHUNK, 8]), g.sb("index", [P, CHUNK, 8], U32), g.sb("index_f", [P, CHUNK, 8])
            peak, total, inv = g.sb("peak", [P, CHUNK]), g.sb("total", [P, CHUNK]), g.sb("inv", [P, CHUNK])
            gates = g.sb("gates", [P, CHUNK, EXPERTS])
            wT = g.sb("wT", [EXPERTS, TOK])
            sem = {n: g.sem(n) for n in ("link", "x_turned", "part_ready", "high_kept", "low_kept", "logits_done", "shifted", "exp_done",
                                         "gates_ready", "w_turned", "wT_ready", "bias_done", "x_ready")}
            with nc.Fori(0, CHUNKS) as c:
                with nc.Block() as block:
                    def parts(t):
                        return [x[:, c * CHUNK + t, :]]

                    @block.gpsimd
                    def _(pool):
                        ln.root(nc, pool, C["minus_half"])
                        pool.wait_ge(sem["part_ready"], KD)
                        high, low = (a[:, :, bass.ds(c * TOK, TOK)] for a in (xH, xL))
                        nc.gpsimd.tensor_copy(high, part[:]).then_inc(sem["high_kept"], 1)
                        pool.wait_ge(sem["high_kept"], 1)
                        nc.gpsimd.tensor_tensor(low, part[:], high.bitcast(F32), ALU.subtract).then_inc(sem["low_kept"], 1)

                    @block.tensor
                    def _(pe):
                        pe.wait_ge(ln.xn_ready, 1)
                        for k in range(KD):
                            for t in range(CHUNK):
                                ins = nc.tensor.transpose(ps_x[k][:, t * P:(t + 1) * P], ln.xn[:, t, k * P:(k + 1) * P],
                                                          C["ident"][:])
                            ins.then_inc(sem["x_turned"], 1)
                        pe.wait_ge(sem["part_ready"], KD)
                        for t in range(CHUNK):
                            for k in range(KD):
                                ins = nc.tensor.matmul(ps_g[:, t * EXPERTS:(t + 1) * EXPERTS],
                                                       part[:, k, t * P:(t + 1) * P], gate[:, k, :],
                                                       start=(k == 0), stop=(k == KD - 1))
                        ins.then_inc(sem["logits_done"], 1)
                        if not gated:
                            pe.wait_ge(sem["gates_ready"], 1)
                            for t in range(CHUNK):
                                ins = nc.tensor.transpose(ps_w[:, t * P:(t + 1) * P], gates[:, t, :], C["ident"][:])
                            ins.then_inc(sem["w_turned"], 1)
                            pe.wait_ge(sem["wT_ready"], 1)
                            for t in range(CHUNK):
                                nc.tensor.matmul(ps_y[t][:], wT[:, t * P:(t + 1) * P], b2[:], start=True,
                                                 stop=True).then_inc(sem["bias_done"], 1)

                    @block.scalar
                    def _(act):
                        for k in range(KD):
                            act.wait_ge(sem["x_turned"], k + 1)
                            nc.scalar.copy(part[:, k, :], ps_x[k][:]).then_inc(sem["part_ready"], 1)
                        act.wait_ge(sem["shifted"], 1)
                        nc.scalar.activation(prob[:], logit[:], ACT.Exp).then_inc(sem["exp_done"], 1)
                        if not gated:
                            act.wait_ge(sem["w_turned"], 1)
                            nc.scalar.copy(wT[:], ps_w[:]).then_inc(sem["wT_ready"], 1)

                    @block.vector
                    def _(dve):
                        link = chain(dve, sem["link"])
                        ln.statistics(nc, link, parts)
                        ln.apply(nc, dve, parts)
                        shape = [P, CHUNK, EXPERTS]
                        dve.wait_ge(sem["logits_done"], 1)
                        lg = ps_g[:].rearrange("p (t e) -> p t e", e=EXPERTS)
                        link(nc.vector.tensor_reduce(peak[:], lg, AX_X, ALU.max))
                        nc.vector.tensor_tensor(logit[:], lg, spread(peak[:], 2, shape), ALU.subtract).then_inc(sem["shifted"], 1)
                        dve.wait_ge(sem["exp_done"], 1)
                        link(nc.vector.tensor_reduce(total[:], prob[:], AX_X, ALU.add))
                        link(nc.vector.reciprocal(inv[:], total[:]))
                        link(nc.vector.tensor_tensor(prob[:], prob[:], spread(inv[:], 2, shape), ALU.mult))
                        for t in range(CHUNK):
                            ins = nc.vector.max(top[:, t, :], prob[:, t, :])
                        link(ins)
                        for t in range(CHUNK):
                            ins = nc.vector.max_index(index[:, t, :], top[:, t, :], prob[:, t, :])
                        link(ins)
                        link(nc.vector.tensor_copy(index_f[:], index[:]))
                        every = iota[:].unsqueeze(1).to_broadcast(shape)
                        nc.vector.tensor_tensor(chosen[:], every, index_f[:, :, 0:1].to_broadcast(shape), ALU.is_equal)
                        link(nc.vector.tensor_tensor(hot[:], every, index_f[:, :, 1:2].to_broadcast(shape), ALU.is_equal))
                        link(nc.vector.tensor_tensor(chosen[:], chosen[:], hot[:], ALU.add))
                        link(nc.vector.tensor_tensor(chosen[:], chosen[:], prob[:], ALU.mult))
                        link(nc.vector.tensor_reduce(total[:], chosen[:], AX_X, ALU.add))
                        if not gated:
                            link(nc.vector.tensor_scalar(total[:], total[:], 1e-12, None, ALU.max))
                        link(nc.vector.reciprocal(inv[:], total[:]))
                        nc.vector.tensor_tensor(gates[:], chosen[:], spread(inv[:], 2, shape), ALU.mult).then_inc(sem["gates_ready"], 1)
                        dve.wait_ge(sem["gates_ready"], 1)
                        link(nc.vector.tensor_copy(w_all[:, bass.ds(c * CHUNK, CHUNK), :], gates[:]))
                        if not gated:
                            for t in range(CHUNK):
                                dve.wait_ge(sem["bias_done"], t + 1)
                                nc.vector.tensor_tensor(x[:, c * CHUNK + t, :], x[:, c * CHUNK + t, :], ps_y[t][:],
                                                        ALU.add).then_inc(sem["x_ready"], 1)
                g.again()

        PAIR = 2
        STEPS = PAIR * CHUNKS
        raw = s.sb("weights_raw", [P, size])
        wH = [s.sb(f"weights_high{i}", [P, size], F32R) for i in range(PAIR)]
        wL = [s.sb(f"weights_low{i}", [P, size], F32R) for i in range(PAIR)]
        b1 = [s.sb(f"bias1_{i}", [P, FT]) for i in range(PAIR)] if not gated else None
        wcur = s.sb("gates_now", [P, TILES, PAIR])
        full = s.sb("hidden_full", [P, 2, TOK])
        hH, hL = (s.sb(n, [P, 2, FT, TOK], F32R) for n in ("hidden_high", "hidden_low"))
        silu = s.sb("silu", [P, 2, TOK]) if gated else None
        slots = 2 if gated else 4
        psU = [[s.ps(f"up{i}_{u}", [P, BANK]) for u in range(ups)] for i in range(slots)]
        psD = [s.ps(f"down{i}", [P, DIM]) for i in range(4)]
        landed, high_done, split_done = s.sem("landed"), s.sem("high_done"), s.sem("split_done")
        gates_now, up_done, silu_done = s.sem("gates_now"), s.sem("up_done"), s.sem("silu_done")
        full_ready, high_ready, hidden_ready = s.sem("full_ready"), s.sem("high_ready"), s.sem("hidden_ready")
        down_done, added = s.sem("down_done"), s.sem("added")
        b1_of = slice(b1_at, b1_at + FT)

        def split_weights(pool, to, times):
            nc.gpsimd.tensor_copy(wH[to][:], raw[:]).then_inc(high_done, 1)
            if not gated:
                nc.gpsimd.tensor_copy(b1[to][:], raw[:, b1_of])
            pool.wait_ge(high_done, times)
            nc.gpsimd.tensor_tensor(wL[to][:], raw[:], wH[to][:].bitcast(F32), ALU.subtract).then_inc(split_done, 1)

        with nc.Block() as block:
            @block.sync
            def _(sp):
                sp.dma_start(raw[:], D[f"L{layer}_experts"][0]).then_inc(landed, 16)

            @block.gpsimd
            def _(pool):
                pool.wait_ge(landed, 16)
                split_weights(pool, 0, 1)
        s.again()
        with nc.Fori(0, EXPERTS // PAIR) as pair:
            with nc.Block() as block:
                @block.sync
                def _(sp):
                    sp.dma_start(raw[:], D[f"L{layer}_experts"][pair * PAIR + 1]).then_inc(landed, 16)
                    sp.wait_ge(split_done, 1)
                    sp.dma_start(raw[:], D[f"L{layer}_experts"][pair * PAIR + 2]).then_inc(landed, 16)

                @block.gpsimd
                def _(pool):
                    pool.wait_ge(landed, 16)
                    split_weights(pool, 1, 1)
                    pool.wait_ge(landed, 32)
                    pool.wait_ge(down_done, CHUNKS * CHUNK)
                    split_weights(pool, 0, 2)

                @block.tensor
                def _(pe):
                    def up(step):
                        e, c = divmod(step, CHUNKS)
                        if step == CHUNKS:
                            pe.wait_ge(split_done, 1)
                        for f in range(FT):
                            n = step * FT + f
                            if n >= slots:
                                pe.wait_ge(full_ready, n - slots + 1)
                            for u in range(ups):
                                for k in range(KD):
                                    at = up_at[u] + k * HID + f * P
                                    tok = slice(c * TOK, (c + 1) * TOK)
                                    for i, (a, m) in enumerate(((wH, xH), (wH, xL), (wL, xH))):
                                        ins = nc.tensor.matmul(psU[n % slots][u][:], a[e][:, at:at + P], m[:, k, tok],
                                                               start=(k == 0 and i == 0), stop=(k == KD - 1 and i == 2))
                            ins.then_inc(up_done, 1)

                    def down(step):
                        e, c = divmod(step, CHUNKS)
                        pe.wait_ge(hidden_ready, (step + 1) * FT)
                        for t in range(CHUNK):
                            n = step * CHUNK + t
                            if n >= len(psD):
                                pe.wait_ge(added, n - len(psD) + 1)
                            for f in range(FT):
                                at = down_at + f * DIM
                                for i, (h, m) in enumerate(((hH, wH), (hH, wL), (hL, wH))):
                                    ins = nc.tensor.matmul(psD[n % len(psD)][:], h[:, step % 2, f, t * P:(t + 1) * P],
                                                           m[e][:, at:at + DIM], start=(f == 0 and i == 0),
                                                           stop=(f == FT - 1 and i == 2))
                            ins.then_inc(down_done, 1)

                    for step in range(STEPS + 1):
                        if step < STEPS:
                            up(step)
                        if step:
                            down(step - 1)

                @block.scalar
                def _(act):
                    def high(n):
                        step, f = divmod(n, FT)
                        if step >= 2:
                            act.wait_ge(down_done, (step - 1) * CHUNK)
                        act.wait_ge(full_ready, n + 1)
                        nc.scalar.copy(hH[:, step % 2, f, :], full[:, n % 2, :]).then_inc(high_ready, 1)

                    for n in range(STEPS * FT + 1):
                        if n < STEPS * FT:
                            act.wait_ge(up_done, n + 1)
                            if gated:
                                if n >= 2:
                                    act.wait_ge(full_ready, n - 1)
                                nc.scalar.activation(silu[:, n % 2, :], psU[n % slots][0][:],
                                                     ACT.Silu).then_inc(silu_done, 1)
                            else:
                                if n >= 2:
                                    act.wait_ge(hidden_ready, n - 1)
                                nc.scalar.activation(full[:, n % 2, :], psU[n % slots][0][:], ACT.Relu,
                                                     bias=b1[n // FT // CHUNKS][:, n % FT:n % FT + 1]).then_inc(full_ready, 1)
                        if n:
                            high(n - 1)

                @block.vector
                def _(dve):
                    nc.vector.tensor_copy(wcur[:], w_all[:, :, bass.ds(pair * PAIR, PAIR)]).then_inc(gates_now, 1)
                    dve.wait_ge(gates_now, 1)

                    def product(n):
                        dve.wait_ge(silu_done, n + 1)
                        if n >= 2:
                            dve.wait_ge(hidden_ready, n - 1)
                        nc.vector.tensor_tensor(full[:, n % 2, :], psU[n % slots][1][:], silu[:, n % 2, :],
                                                ALU.mult).then_inc(full_ready, 1)

                    def low(n):
                        step, f = divmod(n, FT)
                        dve.wait_ge(high_ready, n + 1)
                        nc.vector.tensor_tensor(hL[:, step % 2, f, :], full[:, n % 2, :],
                                                hH[:, step % 2, f, :].bitcast(F32), ALU.subtract).then_inc(hidden_ready, 1)

                    def add(n):
                        step, t = divmod(n, CHUNK)
                        e, c = divmod(step, CHUNKS)
                        dve.wait_ge(down_done, n + 1)
                        if n >= CHUNKS * CHUNK:
                            dve.wait_ge(added, n - CHUNKS * CHUNK + 1)
                        tile = c * CHUNK + t
                        nc.vector.scalar_tensor_tensor(x[:, tile, :], psD[n % len(psD)][:], wcur[:, tile, e:e + 1],
                                                       x[:, tile, :], ALU.mult, ALU.add).then_inc(added, 1)

                    for step in range(STEPS + 1):
                        if step < STEPS:
                            for f in range(FT):
                                n = step * FT + f
                                if gated:
                                    product(n)
                                    if n:
                                        low(n - 1)
                                else:
                                    low(n)
                        if gated and step == STEPS:
                            low(STEPS * FT - 1)
                        if step:
                            for t in range(CHUNK):
                                add((step - 1) * CHUNK + t)
            s.again()


def quantised_ffn(nc, x, C, D):
    INNER = 1024
    KI = INNER // P
    T = 4
    HALF = INNER // BANK
    with ExitStack() as ctx:
        s = Stage(nc, ctx, "f1")
        wg, wu, wd = s.sb("wg", [P, KD * INNER], BF16), s.sb("wu", [P, KD * INNER], BF16), s.sb("wd", [P, KI * DIM], BF16)
        mean, inv_mean = s.sb("mean", [P, 3]), s.sb("inv_mean", [P, 3])
        with ExitStack() as setup:
            g = Stage(nc, setup, "q1")
            raws = [g.sb(f"raw{i}", [P, KD * INNER]) for i in range(3)]
            sums, ones = g.sb("sums", [P, 3]), g.sb("ones", [P, P])
            ps_sum = g.ps("sum", [P, 3])
            link_sem, sums_ready, sum_done = g.sem("link"), g.sem("sums_ready"), g.sem("sum_done")
            load_block(nc, g, [(raws[i][:], D[f"L1_w_{n}"]) for i, n in enumerate(("gate", "up", "down"))])
            with nc.Block() as block:
                @block.tensor
                def _(pe):
                    pe.wait_ge(sums_ready, 1)
                    nc.tensor.matmul(ps_sum[:], ones[:], sums[:], start=True, stop=True).then_inc(sum_done, 1)

                @block.vector
                def _(dve):
                    link = chain(dve, link_sem)
                    nc.vector.memset(ones[:], 1.0)
                    for i in range(3):
                        ins = nc.vector.tensor_reduce(sums[:, i:i + 1], raws[i][:], AX_X, ALU.add,
                                                      apply_absolute_value=True)
                    ins.then_inc(sums_ready, 1)
                    dve.wait_ge(sum_done, 1)
                    link(nc.vector.tensor_scalar(mean[:], ps_sum[:], 1.0 / (INNER * DIM), QUANT_MIN, ALU.mult, ALU.max))
                    link(nc.vector.reciprocal(inv_mean[:], mean[:]))
                    for i, w in enumerate((wg, wu, wd)):
                        r = raws[i]
                        link(nc.vector.tensor_scalar(r[:], r[:], inv_mean[:, i:i + 1], 1.0, ALU.mult, ALU.min))
                        link(nc.vector.tensor_scalar(r[:], r[:], -1.0, ROUND, ALU.max, ALU.add))
                        link(nc.vector.tensor_scalar(w[:], r[:], -ROUND, None, ALU.add))
            g.again()
        ln = LayerNorm(s, T)
        psT = [s.ps(f"turned{i}", [P, 2 * BANK], BF16) for i in range(2)]
        psG = [s.ps(f"gate{i}", [P, BANK]) for i in range(2)]
        psU = [s.ps(f"up{i}", [P, BANK]) for i in range(2)]
        psD = [s.ps(f"down{i}", [P, DIM]) for i in range(2)]
        peak, speed = s.sb("peak", [P, T]), s.sb("quant_scale", [P, T])
        gs, us = s.sb("gate_scale", [P, T]), s.sb("up_scale", [P, T])
        v = s.sb("rounding", [P, T, DIM])
        xq, xqT = s.sb("xq", [P, T, DIM], BF16), s.sb("xqT", [P, KD, T * P], BF16)
        sg = s.sb("silu", [P, 2, BANK])
        h = s.sb("h", [P, 2, INNER])
        hpeak, hspeed, hs = s.sb("h_peak", [P, T]), s.sb("h_quant_scale", [P, T]), s.sb("down_scale", [P, T])
        hq, hqT = s.sb("hq", [P, 2, INNER], BF16), s.sb("hqT", [P, 2, KI, P], BF16)
        sem = {n: s.sem(n) for n in ("link", "xq_ready", "x_turned", "xqT_ready", "up_done", "silu_done", "h_ready",
                                     "h_rounded", "hq_ready", "h_turned", "hqT_ready", "down_done", "x_ready")}
        with nc.Fori(0, TILES // T) as c:
            with nc.Block() as block:
                def parts(t):
                    return [x[:, c * T + t, :]]

                @block.gpsimd
                def _(pool):
                    ln.root(nc, pool, C["minus_half"])

                @block.tensor
                def _(pe):
                    pe.wait_ge(sem["xq_ready"], 1)
                    for k in range(KD):
                        for t in range(T):
                            at = (k * T + t) * P
                            ins = nc.tensor.transpose(psT[0][:, at:at + P], xq[:, t, k * P:(k + 1) * P], C["ident_bf"][:])
                    ins.then_inc(sem["x_turned"], 1)
                    pe.wait_ge(sem["xqT_ready"], 1)

                    def gate_up(t):
                        for n in range(HALF):
                            u = t * HALF + n
                            if u >= 2:
                                pe.wait_ge(sem["h_ready"], u - 1)
                            for w, ps in ((wg, psG), (wu, psU)):
                                for k in range(KD):
                                    at = k * INNER + n * BANK
                                    ins = nc.tensor.matmul(ps[u % 2][:], xqT[:, k, t * P:(t + 1) * P],
                                                           w[:, at:at + BANK], start=(k == 0), stop=(k == KD - 1))
                            ins.then_inc(sem["up_done"], 1)

                    def down(t):
                        pe.wait_ge(sem["hq_ready"], t + 1)
                        if t >= 1:
                            pe.wait_ge(sem["hqT_ready"], t)
                        for k in range(KI):
                            ins = nc.tensor.transpose(psT[1][:, k * P:(k + 1) * P], hq[:, t % 2, k * P:(k + 1) * P],
                                                      C["ident_bf"][:])
                        ins.then_inc(sem["h_turned"], 1)
                        pe.wait_ge(sem["hqT_ready"], t + 1)
                        if t >= 2:
                            pe.wait_ge(sem["x_ready"], t - 1)
                        for k in range(KI):
                            ins = nc.tensor.matmul(psD[t % 2][:], hqT[:, t % 2, k, :], wd[:, k * DIM:(k + 1) * DIM],
                                                   start=(k == 0), stop=(k == KI - 1))
                        ins.then_inc(sem["down_done"], 1)

                    for t in range(T + 1):
                        if t < T:
                            gate_up(t)
                        if t:
                            down(t - 1)

                @block.scalar
                def _(act):
                    act.wait_ge(sem["x_turned"], 1)
                    nc.scalar.copy(xqT[:], psT[0][:].rearrange("p (k t) -> p k t", k=KD)).then_inc(sem["xqT_ready"], 1)
                    for t in range(T + 1):
                        if t < T:
                            for n in range(HALF):
                                u = t * HALF + n
                                act.wait_ge(sem["up_done"], u + 1)
                                if u >= 2:
                                    act.wait_ge(sem["h_ready"], u - 1)
                                nc.scalar.activation(sg[:, u % 2, :], psG[u % 2][:], ACT.Silu,
                                                     scale=gs[:, t:t + 1]).then_inc(sem["silu_done"], 1)
                        if t:
                            act.wait_ge(sem["h_turned"], t)
                            if t >= 3:
                                act.wait_ge(sem["down_done"], t - 2)
                            nc.scalar.copy(hqT[:, (t - 1) % 2, :, :],
                                           psT[1][:].rearrange("p (k t) -> p k t", k=KI)).then_inc(sem["hqT_ready"], 1)

                @block.vector
                def _(dve):
                    link = chain(dve, sem["link"])
                    ln.statistics(nc, link, parts)
                    ln.apply(nc, dve, parts)
                    dve.wait_ge(ln.xn_ready, 1)
                    link(nc.vector.tensor_reduce(peak[:], ln.xn[:], AX_X, ALU.max, apply_absolute_value=True))
                    link(nc.vector.tensor_scalar(peak[:], peak[:], QUANT_MIN, None, ALU.max))
                    link(nc.vector.reciprocal(speed[:], peak[:]))
                    nc.vector.tensor_scalar(gs[:], peak[:], mean[:, 0:1], 1.0 / 127.0, ALU.mult, ALU.mult)
                    nc.vector.tensor_scalar(us[:], peak[:], mean[:, 1:2], 1.0 / 127.0, ALU.mult, ALU.mult)
                    link(nc.vector.tensor_scalar(speed[:], speed[:], 127.0, None, ALU.mult))
                    for t in range(T):
                        ins = nc.vector.tensor_scalar(v[:, t, :], ln.xn[:, t, :], speed[:, t:t + 1], 127.0, ALU.mult, ALU.min)
                    link(ins)
                    link(nc.vector.tensor_scalar(v[:], v[:], -128.0, ROUND, ALU.max, ALU.add))
                    nc.vector.tensor_scalar(xq[:], v[:], -ROUND, None, ALU.add).then_inc(sem["xq_ready"], 1)

                    def product(t):
                        for n in range(HALF):
                            u = t * HALF + n
                            dve.wait_ge(sem["silu_done"], u + 1)
                            nc.vector.scalar_tensor_tensor(h[:, t % 2, n * BANK:(n + 1) * BANK], psU[u % 2][:],
                                                           us[:, t:t + 1], sg[:, u % 2, :], ALU.mult,
                                                           ALU.mult).then_inc(sem["h_ready"], 1)

                    def quantise(t):
                        hh, at = h[:, t % 2, :], slice(t, t + 1)
                        dve.wait_ge(sem["h_ready"], (t + 1) * HALF)
                        link(nc.vector.tensor_reduce(hpeak[:, at], hh, AX_X, ALU.max, apply_absolute_value=True))
                        link(nc.vector.tensor_scalar(hpeak[:, at], hpeak[:, at], QUANT_MIN, None, ALU.max))
                        link(nc.vector.reciprocal(hspeed[:, at], hpeak[:, at]))
                        nc.vector.tensor_scalar(hs[:, at], hpeak[:, at], mean[:, 2:3], 1.0 / 127.0, ALU.mult, ALU.mult)
                        link(nc.vector.tensor_scalar(hspeed[:, at], hspeed[:, at], 127.0, None, ALU.mult))
                        link(nc.vector.tensor_scalar(hh, hh, hspeed[:, at], 127.0, ALU.mult, ALU.min))
                        link(nc.vector.tensor_scalar(hh, hh, -128.0, ROUND, ALU.max, ALU.add))
                        if t >= 2:
                            dve.wait_ge(sem["h_turned"], t - 1)
                        nc.vector.tensor_scalar(hq[:, t % 2, :], hh, -ROUND, None, ALU.add).then_inc(sem["hq_ready"], 1)

                    def add(t):
                        dve.wait_ge(sem["down_done"], t + 1)
                        nc.vector.scalar_tensor_tensor(x[:, c * T + t, :], psD[t % 2][:], hs[:, t:t + 1],
                                                       x[:, c * T + t, :], ALU.mult, ALU.add).then_inc(sem["x_ready"], 1)

                    for t in range(T + 1):
                        if t < T:
                            product(t)
                            if t >= 2:
                                dve.wait_ge(sem["hq_ready"], t - 1)
                            quantise(t)
                        if t:
                            add(t - 1)
            s.again()


def shift_rows(nc, s, y, shifted, sem):
    with nc.Block() as block:
        @block.sync
        def _(sp):
            sp.dma_start(shifted[1:P, :, :], y[0:P - 1, :, P:DIM]).then_inc(sem, 16)
            sp.dma_start(shifted[0:1, 1:TILES:2, :], y[P - 1:P, 0:TILES:2, P:DIM]).then_inc(sem, 16)
            sp.wait_ge(sem, 32)
    s.again()


def local_attention_block(nc, x, C, D):
    DEPTH, H, HD, HID = 2, 8, 64, 682
    INNER = H * HD
    with ExitStack() as ctx:
        s = Stage(nc, ctx, "f2")
        y, shifted = s.sb("y", [P, TILES, DIM]), s.sb("shifted", [P, TILES, P])
        set_done, shift_landed = s.sem("set_done"), s.sem("shift_landed")
        T = 4
        with nc.Block() as block:
            @block.vector
            def _(dve):
                nc.vector.memset(shifted[:], 0.0).then_inc(set_done, 1)
                dve.wait_ge(set_done, 1)
        s.again()
        with ExitStack() as front:
            g = Stage(nc, front, "n2")
            ln = LayerNorm(g, T)
            link_sem, copied = g.sem("link"), g.sem("copied")
            with nc.Fori(0, TILES // T) as c:
                with nc.Block() as block:
                    def parts(t):
                        return [x[:, c * T + t, :]]

                    @block.gpsimd
                    def _(pool):
                        ln.root(nc, pool, C["minus_half"])

                    @block.scalar
                    def _(act):
                        act.wait_ge(ln.xn_ready, 1)
                        nc.scalar.copy(y[:, bass.ds(c * T, T), :], ln.xn[:]).then_inc(copied, 1)

                    @block.vector
                    def _(dve):
                        link = chain(dve, link_sem)
                        ln.statistics(nc, link, parts)
                        ln.apply(nc, dve, parts)
                g.again()
        with nc.Fori(0, DEPTH) as layer:
            shift_rows(nc, s, y, shifted, shift_landed)
            local_attention(nc, C, D, y, shifted, layer, H, HD)
            shift_rows(nc, s, y, shifted, shift_landed)
            gelu_ffn(nc, C, D, y, shifted, layer, HID)
        with nc.Block() as block:
            @block.vector
            def _(dve):
                nc.vector.tensor_tensor(x[:], x[:], y[:], ALU.add).then_inc(set_done, 1)
                dve.wait_ge(set_done, 1)
        s.again()


def local_attention(nc, C, D, y, shifted, layer, H, HD):
    INNER = H * HD
    KI = INNER // P
    with ExitStack() as ctx:
        s = Stage(nc, ctx, "a2")
        wqkv, wo = s.sb("wqkv", [P, KD, 3 * INNER]), s.sb("wo", [P, KI, DIM])
        scale = s.sb("scale", [P, 4, HD])
        tables = s.sb("tables", [P, 2, 2, 2, HD])
        psA = [s.ps(f"work{i}", [P, BANK]) for i in range(2)]
        att = Attention(s, H, HD, P, F32, 1, 0, None)
        link0 = s.sem("tables_link")
        load_block(nc, s, [(wqkv[:], D["L2_wqkv"][layer]), (wo[:], D["L2_wo"][layer]),
                           (scale[:], D["L2_qk_scale"][layer].partition_broadcast(P))])
        with nc.Block() as block:
            @block.vector
            def _(dve):
                link = chain(dve, link0)
                for w, which in enumerate(("q", "k")):
                    for f, fn in enumerate(("cos", "sin")):
                        ins = nc.vector.tensor_tensor(tables[:, w, f], C[f"xpos_{fn}_{which}"][:],
                                                      spread(scale[:, 2 * w + f, :], 1, [P, 2, HD]), ALU.mult)
                link(ins)
                att.clear(nc)
                link(nc.vector.memset(att.rsum[:], 0.0))
                att.clear_ones(nc)
                link(nc.vector.memset(att.rsum[:], 0.0))
        s.again()
        h = s.sb("h", [P, 2, DIM])
        hT = s.sb("hT", [P, KD, SEQ])
        raw = s.sb("raw", [P, 2, 2, INNER])
        sq = s.sb("squares", [P, 2, 2, INNER])
        ss, rn = s.sb("sum_squares", [P, 2, 2 * H]), s.sb("inv_norm", [P, 2, 2 * H])
        rot = s.sb("rotated", [P, 2, H, HD])
        oT = s.sb("oT", [P, KI, SEQ])
        sem = {n: s.sem(n) for n in ("link", "h_ready", "h_turned", "qkv_done", "by_act", "by_dve", "squared",
                                     "ss_ready", "bounded", "rn_ready", "o_turned", "out_done")}
        A, V = sem["by_act"], sem["by_dve"]
        QKV = 6
        core = 3 * att.tr_banks
        turn_o = KI * SEQ // BANK
        readers = [A] * (1 + QKV + core + turn_o) + [V, V]
        USE_K = 1 + QKV
        USE_O = USE_K + core
        with nc.Fori(0, BATCH) as b:
            with nc.Block() as block:
                @block.gpsimd
                def _(pool):
                    nc.gpsimd.tensor_copy(h[:, :, 0:P], y[:, bass.ds(b * 2, 2), 0:P])
                    nc.gpsimd.tensor_copy(h[:, :, P:DIM], shifted[:, bass.ds(b * 2, 2), :]).then_inc(sem["h_ready"], 1)
                    for w in range(2):
                        pool.wait_ge(sem["ss_ready"], w + 1)
                        nc.gpsimd.tensor_scalar(ss[:, w, :], ss[:, w, :], TINY_SQ, None, ALU.max).then_inc(sem["bounded"], 1)
                        pool.wait_ge(sem["bounded"], w + 1)
                        nc.gpsimd.tensor_tensor(rn[:, w, :], ss[:, w, :], C["minus_half"][:, 0:2 * H],
                                                ALU.pow).then_inc(sem["rn_ready"], 1)

                @block.tensor
                def _(pe):
                    ring = Ring(psA, readers)
                    pe.wait_ge(sem["h_ready"], 1)
                    turn_rows(nc, ring.claim(pe), h, C["ident"], 2, DIM).then_inc(sem["h_turned"], 1)
                    pe.wait_ge(A, 1)
                    for part in (1, 0, 2):
                        for t in range(2):
                            bank = ring.claim(pe)
                            for k in range(KD):
                                ins = nc.tensor.matmul(bank[:], hT[:, k, t * P:(t + 1) * P],
                                                       wqkv[:, k, part * INNER:(part + 1) * INNER],
                                                       start=(k == 0), stop=(k == KD - 1))
                            ins.then_inc(sem["qkv_done"], 1)
                    local_q, local_k = (lambda h: C["local_q"][:]), (lambda h: C["local_k"][:])
                    att.tensor(nc, pe, ring, C["ident"], C["ident_bf"], local_q, local_k, A, 1 + QKV)
                    pe.wait_ge(att.o_ready, att.rounds)
                    for n in range(turn_o):
                        bank = ring.claim(pe)
                        for i in range(2):
                            k = n * 2 + i
                            for t in range(2):
                                src = att.o_rows[:, t, 2 * k:2 * k + 2, :].rearrange("p h d -> p (h d)")
                                ins = nc.tensor.transpose(bank[:, (i * 2 + t) * P:(i * 2 + t + 1) * P], src, C["ident"][:])
                        ins.then_inc(sem["o_turned"], 1)
                    pe.wait_ge(A, USE_O + turn_o)
                    for t in range(2):
                        bank = ring.claim(pe)
                        for k in range(KI):
                            ins = nc.tensor.matmul(bank[:, 0:DIM], oT[:, k, t * P:(t + 1) * P], wo[:, k, :],
                                                   start=(k == 0), stop=(k == KI - 1))
                        ins.then_inc(sem["out_done"], 1)

                @block.scalar
                def _(act):
                    ring = Ring(psA, readers)
                    act.wait_ge(sem["h_turned"], 1)
                    nc.scalar.copy(hT[:], ring.bank(0)[:].rearrange("p (k t) -> p k t", k=KD)).then_inc(A, 1)
                    for w in range(2):
                        for t in range(2):
                            n = w * 2 + t
                            act.wait_ge(sem["qkv_done"], n + 1)
                            nc.scalar.copy(raw[:, w, t, :], ring.bank(1 + n)[:]).then_inc(A, 1)
                            act.wait_ge(A, n + 2)
                            nc.scalar.activation(sq[:, w, t, :], raw[:, w, t, :], ACT.Square).then_inc(sem["squared"], 1)
                    for t in range(2):
                        act.wait_ge(sem["qkv_done"], 5 + t)
                        ins = nc.scalar.copy(att.v_rows[:, t, :, 0:HD],
                                             ring.bank(5 + t)[:].rearrange("p (h d) -> p h d", h=H)).then_inc(A, 1)
                    att.scalar(nc, act, ring, USE_K, A, 8.0)
                    for n in range(turn_o):
                        act.wait_ge(sem["o_turned"], n + 1)
                        nc.scalar.copy(oT[:, 2 * n:2 * n + 2, :],
                                       ring.bank(USE_O + n)[:].rearrange("p (k t) -> p k t", k=2)).then_inc(A, 1)

                @block.vector
                def _(dve):
                    ring = Ring(psA, readers)
                    link = chain(dve, sem["link"])
                    nc.vector.memset(att.v_rows[:, :, :, HD:HD + 1], 1.0).then_inc(att.v_ready, 1)
                    for w, (to, ready) in enumerate(((att.k_rows, att.k_ready), (att.q_rows, att.q_ready))):
                        dve.wait_ge(sem["squared"], 2 * w + 2)
                        nc.vector.tensor_reduce(ss[:, w, :], sq[:, w].rearrange("p t (h d) -> p (t h) d", h=H), AX_X,
                                                ALU.add).then_inc(sem["ss_ready"], 1)
                        dve.wait_ge(sem["rn_ready"], w + 1)
                        rows = raw[:, w].rearrange("p t (h d) -> p (t h) d", h=H)
                        link(nc.vector.tensor_tensor(rows, rows, spread(rn[:, w, :], 2, [P, 2 * H, HD]), ALU.mult))
                        for t in range(2):
                            r = raw[:, w, t, :].rearrange("p (h d) -> p h d", h=H)
                            cos, sin = tables[:, 1 - w, 0, t, :], tables[:, 1 - w, 1, t, :]
                            half = HD // 2
                            nc.vector.tensor_tensor(rot[:, t, :, 0:half], r[:, :, half:HD],
                                                    spread(sin[:, 0:half], 1, [P, H, half]), ALU.mult)
                            nc.vector.tensor_tensor(rot[:, t, :, half:HD], r[:, :, 0:half],
                                                    spread(sin[:, half:HD], 1, [P, H, half]), ALU.mult)
                            ins = nc.vector.tensor_tensor(to[:, t, :, 0:HD], r, spread(cos, 1, [P, H, HD]), ALU.mult)
                        link(ins)
                        ins = nc.vector.tensor_tensor(to[:, :, :, 0:HD], to[:, :, :, 0:HD], rot[:], ALU.add)
                        ins.then_inc(ready, 1)
                        dve.wait_ge(ready, 1)
                    att.vector(nc, dve, link)
                    for t in range(2):
                        dve.wait_ge(sem["out_done"], t + 1)
                        nc.vector.tensor_tensor(y[:, b * 2 + t, :], y[:, b * 2 + t, :],
                                                ring.bank(USE_O + turn_o + t)[:, 0:DIM], ALU.add).then_inc(V, 1)
            s.again()


def gelu_ffn(nc, C, D, y, shifted, layer, HID):
    FT = -(-HID // P)
    rows = [min(P, HID - f * P) for f in range(FT)]
    T = 4
    TOK = T * P
    with ExitStack() as ctx:
        s = Stage(nc, ctx, "g2")
        w1, w2 = s.sb("w1", [P, KD, 2 * HID]), s.sb("w2", [P, FT, DIM])
        b1, b2 = s.sb("b1", [P, 2, FT]), s.sb("b2", [P, DIM])
        gain, bias = s.sb("ln_gain", [P, KD]), s.sb("ln_bias", [P, KD])
        load_block(nc, s, [(w1[:], D["L2_w1"][layer]), (w2[:], D["L2_w2"][layer]), (b1[:], D["L2_b1"][layer]),
                           (b2[:], D["L2_b2"][layer].partition_broadcast(P)), (gain[:], D["L2_ln_g"][layer]),
                           (bias[:], D["L2_ln_b"][layer])])
        s.again()
        ln = LayerNorm(s, T, 2)
        ps_x = [s.ps(f"turned{k}", [P, BANK]) for k in range(KD)]
        psU = [[s.ps(f"up{i}_{u}", [P, BANK]) for u in range(2)] for i in range(2)]
        psD = [s.ps(f"down{i}", [P, DIM]) for i in range(2)]
        hT = s.sb("hT", [P, KD, TOK])
        gelu = s.sb("gelu", [P, 2, TOK])
        hidden = s.sb("hidden", [P, FT, TOK])
        sem = {n: s.sem(n) for n in ("link", "x_turned", "hT_ready", "up_done", "gelu_done", "hidden_ready",
                                     "down_done", "bias_added", "y_ready")}
        with nc.Fori(0, TILES // T) as c:
            with nc.Block() as block:
                def parts(t):
                    return [y[:, c * T + t, 0:P], shifted[:, c * T + t, :]]

                @block.gpsimd
                def _(pool):
                    ln.root(nc, pool, C["minus_half"])
                    pool.wait_ge(ln.xn_ready, 1)
                    for t in range(T):
                        ins = nc.gpsimd.tensor_tensor(y[:, c * T + t, :], y[:, c * T + t, :], b2[:], ALU.add)
                    ins.then_inc(sem["bias_added"], 1)

                @block.tensor
                def _(pe):
                    pe.wait_ge(ln.xn_ready, 1)
                    for k in range(KD):
                        for t in range(T):
                            ins = nc.tensor.transpose(ps_x[k][:, t * P:(t + 1) * P], ln.xn[:, t, k * P:(k + 1) * P],
                                                      C["ident"][:])
                        ins.then_inc(sem["x_turned"], 1)
                    pe.wait_ge(sem["hT_ready"], KD)
                    for f in range(FT):
                        if f >= 2:
                            pe.wait_ge(sem["hidden_ready"], f - 1)
                        for u in (1, 0):
                            for k in range(KD):
                                at = u * HID + f * P
                                ins = nc.tensor.matmul(psU[f % 2][u][0:rows[f], :], w1[:, k, at:at + rows[f]], hT[:, k, :],
                                                       start=(k == 0), stop=(k == KD - 1))
                        ins.then_inc(sem["up_done"], 1)
                    pe.wait_ge(sem["hidden_ready"], FT)
                    for t in range(T):
                        if t >= 2:
                            pe.wait_ge(sem["y_ready"], t - 1)
                        for f in range(FT):
                            ins = nc.tensor.matmul(psD[t % 2][:], hidden[0:rows[f], f, t * P:(t + 1) * P],
                                                   w2[0:rows[f], f, :], start=(f == 0), stop=(f == FT - 1))
                        ins.then_inc(sem["down_done"], 1)

                @block.scalar
                def _(act):
                    for k in range(KD):
                        act.wait_ge(sem["x_turned"], k + 1)
                        nc.scalar.activation(hT[:, k, :], ps_x[k][:], ACT.Identity, bias=bias[:, k:k + 1],
                                             scale=gain[:, k:k + 1]).then_inc(sem["hT_ready"], 1)
                    for f in range(FT):
                        act.wait_ge(sem["up_done"], f + 1)
                        if f >= 2:
                            act.wait_ge(sem["hidden_ready"], f - 1)
                        nc.scalar.activation(gelu[0:rows[f], f % 2, :], psU[f % 2][1][0:rows[f], :], ACT.Gelu,
                                             bias=b1[0:rows[f], 1, f:f + 1]).then_inc(sem["gelu_done"], 1)

                @block.vector
                def _(dve):
                    link = chain(dve, sem["link"])
                    ln.statistics(nc, link, parts)
                    ln.apply(nc, dve, parts)
                    for f in range(FT):
                        dve.wait_ge(sem["gelu_done"], f + 1)
                        nc.vector.scalar_tensor_tensor(hidden[0:rows[f], f, :], psU[f % 2][0][0:rows[f], :],
                                                       b1[0:rows[f], 0, f:f + 1], gelu[0:rows[f], f % 2, :], ALU.add,
                                                       ALU.mult).then_inc(sem["hidden_ready"], 1)
                    dve.wait_ge(sem["bias_added"], 1)
                    for t in range(T):
                        dve.wait_ge(sem["down_done"], t + 1)
                        nc.vector.tensor_tensor(y[:, c * T + t, :], y[:, c * T + t, :], psD[t % 2][:],
                                                ALU.add).then_inc(sem["y_ready"], 1)
            s.again()


def constants():
    bf = mybir.dt.np(BF16)
    p = np.arange(P)
    c = {}
    c["ident"] = np.eye(P, dtype=np.float32)
    c["ident_bf"] = np.eye(P).astype(bf)

    def masks(allowed):
        q, k = p[:, None], p[None, :]
        by_q = np.concatenate([allowed(q, k), allowed(q + P, k), allowed(q + P, k + P)], 1)
        by_k = np.concatenate([allowed(q, k).T, allowed(q + P, k).T, allowed(q + P, k + P).T], 1)
        return [np.where(m, 0.0, MASKED).astype(bf) for m in (by_q, by_k)]

    c["causal_q"], c["causal_k"] = masks(lambda q, k: k <= q)
    c["window_q"], c["window_k"] = masks(lambda q, k: (k <= q) & (k >= q - 62))
    c["local_q"], c["local_k"] = masks(lambda q, k: (k <= q) & (q <= k + P))
    c["head_blocks"] = (p[:, None] // 16 == p[None, :] // 16).astype(np.float32)
    c["iota8"] = np.tile(np.arange(EXPERTS, dtype=np.float32), (P, 1))
    t = np.arange(SEQ, dtype=np.float32)

    def by_token(a):
        return np.ascontiguousarray(a.reshape(2, P, -1).transpose(1, 0, 2)).astype(np.float32)

    inv = (1.0 / np.float32(10000.0) ** (np.arange(0, 16, 2, dtype=np.float32) / 16)).astype(np.float32)
    f = t[:, None] * inv[None, :]
    c["rope_cos"], c["rope_sin"] = by_token(np.cos(f)), by_token(np.sin(f))
    half = np.arange(0, 64, 2, dtype=np.float32)
    inv = (1.0 / np.float32(10000.0) ** (half / 64)).astype(np.float32)
    f = t[:, None] * inv[None, :]
    f = np.concatenate([f, f], -1)
    base = (half + np.float32(0.4 * 64)) / np.float32(1.4 * 64)
    scale = base[None, :] ** ((t - SEQ // 2) / np.float32(64.0))[:, None]
    scale = np.concatenate([scale, scale], -1)
    sign = np.where(np.arange(64) < 32, -1.0, 1.0).astype(np.float32)
    c["xpos_cos_q"], c["xpos_sin_q"] = by_token(np.cos(f) * scale), by_token(np.sin(f) * scale * sign)
    c["xpos_cos_k"], c["xpos_sin_k"] = by_token(np.cos(f) / scale), by_token(np.sin(f) / scale * sign)
    return c


def chunks(w):
    return w.reshape(-1, P, w.shape[1]).transpose(1, 0, 2)


def layouts(i):
    d = {"x": i["x"].reshape(TILES, P, DIM).transpose(1, 0, 2)}
    d["ctxT"] = i["ctx_1024"].reshape(BATCH, SEQ, KD, P).transpose(0, 3, 2, 1)
    d["ctx"] = i["ctx_1024"].reshape(BATCH, 2, P, DIM).transpose(0, 2, 1, 3)
    d["mask_if1"] = i["mask_BxS2_if1"].reshape(TILES, P).T
    d["mask_bk1"] = i["mask_BxS2_bk1"].reshape(TILES, P).T
    d["mask_bk0"] = i["mask_BxS2_bk0"]
    for l in (0, 1, 2):
        n = f"L{l}_xattn_"
        d[f"L{l}_wqT"] = chunks(i[n + "Wq"].T if l < 2 else i[n + "Wq"])
        d[f"L{l}_wkvT"] = chunks(np.concatenate([i[n + "Wk"].T, i[n + "Wv"].T] if l < 2 else
                                                [i[n + "Wk"], i[n + "Wv"]], 1))
        d[f"L{l}_woT"] = chunks(i[n + "Wo"].T if l < 2 else i[n + "Wo"])
        d[f"L{l}_bq"], d[f"L{l}_bo"] = i[n + "bq"], i[n + "bo"]
        d[f"L{l}_bkv"] = np.concatenate([i[n + "bk"], i[n + "bv"]])
    d["L1_bq_col"] = i["L1_xattn_bq"].reshape(KD, P).T
    for w in ("q", "k", "o"):
        d[f"L3_w{w}T"] = chunks(i[f"L3_xattn_W{w}"].T)
    d["L3_bq_col"], d["L3_bk_col"] = i["L3_xattn_bq"].reshape(KD, P).T, i["L3_xattn_bk"].reshape(KD, P).T
    d["L3_bo"] = i["L3_xattn_bo"]
    d["L0_gate"], d["L3_gate"] = chunks(i["L0_ffn_gate"]), chunks(i["L3_ffn_gate_w"].T)
    d["L0_b2"] = i["L0_ffn_b2"]

    def rows_of(w):
        e, k, n = w.shape
        w = np.concatenate([w, np.zeros((e, -k % P, n), w.dtype)], 1)
        return w.reshape(e, -1, P, n).transpose(0, 2, 1, 3).reshape(e, P, -1)

    def wrapped(parts):
        a = np.concatenate(parts, 2)
        return np.concatenate([a, a[:1]], 0)

    d["L0_experts"] = wrapped([rows_of(i["L0_ffn_W1"]), i["L0_ffn_b1"].reshape(EXPERTS, -1, P).transpose(0, 2, 1),
                               rows_of(i["L0_ffn_W2"])])

    def padded(w):
        e, h, k = w.shape
        return np.concatenate([w, np.zeros((e, -h % P, k), w.dtype)], 1).transpose(0, 2, 1)

    d["L3_experts"] = wrapped([rows_of(padded(i["L3_ffn_w1"])), rows_of(padded(i["L3_ffn_w3"])),
                               rows_of(i["L3_ffn_w2"].transpose(0, 2, 1))])
    for n in ("gate", "up", "down"):
        d[f"L1_w_{n}"] = rows_of(i[f"L1_ffn_w_{n}"].T[None])[0]
    n = "L2_ffn_"
    depth = i[n + "wqkv"].shape[0]
    hid = i[n + "w2"].shape[1]

    def by_layer(f):
        return np.stack([f(l) for l in range(depth)])

    d["L2_wqkv"] = by_layer(lambda l: chunks(i[n + "wqkv"][l]))
    d["L2_wo"] = by_layer(lambda l: chunks(i[n + "wo"][l]))
    d["L2_w1"] = by_layer(lambda l: chunks(i[n + "w1"][l]))
    d["L2_w2"] = rows_of(i[n + "w2"]).reshape(depth, P, -1, DIM)
    b1 = i[n + "b1"].reshape(depth, 2, hid)
    b1 = np.concatenate([b1, np.zeros((depth, 2, -hid % P), b1.dtype)], 2)
    d["L2_b1"] = b1.reshape(depth, 2, -1, P).transpose(0, 3, 1, 2)
    d["L2_b2"] = i[n + "b2"]
    d["L2_ln_g"], d["L2_ln_b"] = (i[n + v].reshape(depth, KD, P).transpose(0, 2, 1) for v in ("ln_g", "ln_b"))
    qs, ks = i[n + "q_scale"], i[n + "k_scale"]
    d["L2_qk_scale"] = np.stack([qs, np.concatenate([qs[:, 32:], qs[:, :32]], 1),
                                 ks, np.concatenate([ks[:, 32:], ks[:, :32]], 1)], 1)
    return d


STAGES = [
    ("L0x", lambda nc, x, C, D: cross_attention(nc, x, C, D, 0, False)),
    ("L0f", lambda nc, x, C, D: mixture(nc, x, C, D, 0)),
    ("L1x", linear_attention),
    ("L1f", quantised_ffn),
    ("L2x", lambda nc, x, C, D: cross_attention(nc, x, C, D, 2, True)),
    ("L2f", local_attention_block),
    ("L3x", memory_attention),
    ("L3f", lambda nc, x, C, D: mixture(nc, x, C, D, 3)),
]


def program(nc, D, out, const_inputs, stages):
    with ExitStack() as ctx:
        s = Stage(nc, ctx, "all")
        x = s.sb("x", [P, TILES, DIM])
        C = {}
        pairs = [(x[:], D["x"])]
        for name, src in const_inputs.items():
            C[name] = s.sb(name, list(src.shape), src.dtype)
            pairs.append((C[name][:], src))
        C["minus_half"] = s.sb("minus_half", [P, 2 * TILES])
        set_done = s.sem("set_done")
        stored = s.sem("stored")
        load_block(nc, s, pairs)
        with nc.Block() as block:
            @block.vector
            def _(dve):
                nc.vector.memset(C["minus_half"][:], -0.5).then_inc(set_done, 1)
                dve.wait_ge(set_done, 1)
        for _, stage in stages:
            stage(nc, x, C, D)
        with nc.Block() as block:
            @block.sync
            def _(sp):
                sp.dma_start(out, x[:]).then_inc(stored, 16)
                sp.wait_ge(stored, 16)


def kernel(**inputs):
    import concourse.bacc as bacc
    from concourse.bass_utils import run_bass_kernel_spmd

    nc = bacc.Bacc("TRN2", target_bir_lowering=False, num_devices=1)
    arrays, aps = {}, []
    for group in (layouts(inputs), constants()):
        made = {}
        for name, a in group.items():
            a = np.ascontiguousarray(a)
            arrays[f"in_{name}"] = a
            kind = U8 if a.dtype == bool else mybir.dt.from_np(a.dtype)
            made[name] = nc.dram_tensor(f"in_{name}", a.shape, kind, kind="ExternalInput").ap()
        aps.append(made)
    out = nc.dram_tensor("out_x", (P, TILES, DIM), F32, kind="ExternalOutput").ap()
    program(nc, aps[0], out, aps[1], STAGES)
    r = run_bass_kernel_spmd(nc, [arrays], core_ids=[0])
    y = r.results[0]["out_x"]
    return y.transpose(1, 0, 2).reshape(BATCH, SEQ, DIM)
```

```python
from contextlib import ExitStack

import numpy as np

import concourse.bass as bass
from concourse import mybir

ALU = mybir.AluOpType
ACT = mybir.ActivationFunctionType
F32 = mybir.dt.float32
F32R = mybir.dt.float32r
BF16 = mybir.dt.bfloat16
U8 = mybir.dt.uint8
U32 = mybir.dt.uint32
I32 = mybir.dt.int32
AX_X = mybir.AxisListType.X

P = 128
BATCH, SEQ, DIM = 8, 256, 256
TILES = BATCH * SEQ // P
KD = DIM // P
BANK = 512
CAUSAL3 = 3 * P
MASKED = -1e30
LN_EPS = 1e-5
TINY_SQ = 1e-24
EXPERTS = 8
ROUND = 12582912.0
QUANT_MIN = 1e-5


class Stage:

    def __init__(self, nc, ctx, name):
        self.nc, self.ctx, self.name = nc, ctx, name
        self.sems = []

    def sem(self, name):
        s = self.ctx.enter_context(self.nc.semaphore(f"{self.name}_{name}"))
        self.sems.append(s)
        return s

    def sb(self, name, shape, dt=F32):
        return self.ctx.enter_context(self.nc.sbuf_tensor(f"{self.name}_{name}", shape, dt))

    def ps(self, name, shape, dt=F32):
        return self.ctx.enter_context(self.nc.psum_tensor(f"{self.name}_{name}", shape, dt))

    def again(self):
        numbers = sorted(s.num for s in self.sems)
        first = numbers[0]
        for number, following in zip(numbers, numbers[1:] + [None]):
            if following != number + 1:
                self.nc.gpsimd.sem_clear(range(first, number + 1))
                first = following
        self.nc.all_engine_barrier()


def chain(eng, sem):
    count = [0]

    def link(ins):
        count[0] += 1
        ins.then_inc(sem, 1)
        eng.wait_ge(sem, count[0])

    return link


class Ring:

    def __init__(self, banks, readers):
        self.banks, self.readers, self.n = banks, readers, 0

    def claim(self, eng):
        old = self.n - len(self.banks)
        if old >= 0:
            reader = self.readers[old]
            eng.wait_ge(reader, sum(r is reader for r in self.readers[:old + 1]))
        bank = self.banks[self.n % len(self.banks)]
        self.n += 1
        return bank

    def bank(self, n):
        return self.banks[n % len(self.banks)]


def spread(ap, axis, shape):
    return ap.unsqueeze(axis).to_broadcast(shape)


class LayerNorm:

    def __init__(self, s, tiles, pieces=1):
        self.tiles, self.pieces = tiles, pieces
        self.stats = s.sb("ln_stats", [P, tiles, 6 * pieces])
        self.mv = s.sb("ln_mean_var", [P, tiles, 2])
        self.ve = s.sb("ln_var_eps", [P, tiles])
        self.rstd = s.sb("ln_rstd", [P, tiles])
        self.xn = s.sb("ln_out", [P, tiles, DIM])
        self.stats_ready = s.sem("ln_stats_ready")
        self.eps_added = s.sem("ln_eps_added")
        self.rstd_ready = s.sem("ln_rstd_ready")
        self.xn_ready = s.sem("ln_out_ready")

    def statistics(self, nc, link, parts):
        for t in range(self.tiles):
            for i, part in enumerate(parts(t)):
                ins = nc.vector.bn_stats(self.stats[:, t, 6 * i:6 * i + 6], part)
        link(ins)
        for t in range(self.tiles):
            ins = nc.vector.bn_aggr(self.mv[:, t, :], self.stats[:, t, :])
        ins.then_inc(self.stats_ready, 1)

    def root(self, nc, pool, minus_half):
        pool.wait_ge(self.stats_ready, 1)
        nc.gpsimd.tensor_scalar(self.ve[:], self.mv[:, :, 1], LN_EPS, None, ALU.add).then_inc(self.eps_added, 1)
        pool.wait_ge(self.eps_added, 1)
        nc.gpsimd.tensor_tensor(self.rstd[:], self.ve[:], minus_half[:, 0:self.tiles],
                                ALU.pow).then_inc(self.rstd_ready, 1)

    def apply(self, nc, dve, parts):
        dve.wait_ge(self.rstd_ready, 1)
        for t in range(self.tiles):
            at = 0
            for part in parts(t):
                n = part.shape[-1]
                ins = nc.vector.tensor_scalar(self.xn[:, t, at:at + n], part, self.mv[:, t, 0:1],
                                              self.rstd[:, t:t + 1], ALU.subtract, ALU.mult)
                at += n
        ins.then_inc(self.xn_ready, 1)


class Attention:

    def __init__(self, s, heads, width, form):
        self.H, self.D, self.form = heads, width, form
        self.dt = BF16 if form == "bf16" else F32
        self.HP = 32 if form == "bf16" else 64
        self.per_chunk = P // self.HP
        self.chunks = heads // self.per_chunk
        self.cols = 2 * BANK if form == "bf16" else BANK
        self.banks = self.chunks * SEQ // self.cols
        self.W = width + 1
        self.rounds = -(-heads * self.W // BANK)
        self.per_round = heads // self.rounds
        self.q_rows = s.sb("q_rows", [P, 2, heads, self.HP], self.dt)
        self.k_rows = s.sb("k_rows", [P, 2, heads, self.HP], self.dt)
        self.v_wide = s.sb("v_rows", [P, 2, heads * self.W + P])
        self.v_rows = self.v_wide[:, :, 0:heads * self.W].rearrange("p t (h w) -> p t h w", w=self.W)
        if form == "bf16":
            self.qT, self.kT = (s.sb(n, [P, self.chunks, SEQ], BF16) for n in ("qT", "kT"))
        else:
            self.qT, self.kT = s.sb("qT", [P, self.chunks, SEQ], F32R), s.sb("kT", [P, self.chunks, 2, SEQ], F32R)
        if form == "halves":
            self.qL, self.kL = s.sb("qT_low", [P, self.chunks, SEQ], F32R), s.sb("kT_low", [P, self.chunks, 2, SEQ], F32R)
            self.high_kept = s.sem("high_kept")
        self.negmax = s.sb("negmax", [P, 2, heads])
        self.prow = s.sb("probs", [P, 2, CAUSAL3])
        self.probsT = s.sb("probsT", [P, 2, CAUSAL3])
        self.rsum = s.sb("rsum", [P, 2, heads])
        self.o_rows = s.sb("o_rows", [P, 2, heads, width])
        self.psS = s.ps("scores", [P, 2, BANK])
        self.psT = s.ps("probs_turned", [P, 2, BANK])
        self.psO = s.ps("pv", [P, 2, BANK])
        self.v_ready = s.sem("v_ready")
        self.rows_turned, self.operands = s.sem("rows_turned"), s.sem("operands")
        self.scores_done, self.max_taken, self.exp_done = s.sem("scores_done"), s.sem("max_taken"), s.sem("exp_done")
        self.probs_turned, self.probs_ready = s.sem("probs_turned"), s.sem("probs_ready")
        self.pv_done, self.o_ready = s.sem("pv_done"), s.sem("o_ready")

    def clear(self, nc):
        nc.vector.memset(self.q_rows[:], 0.0)
        nc.vector.memset(self.k_rows[:], 0.0)
        nc.vector.memset(self.v_wide[:], 1.0)
        if self.form != "bf16":
            nc.vector.memset(self.kT[:].bitcast(F32), 0.0)
        if self.form == "halves":
            nc.vector.memset(self.kL[:].bitcast(F32), 0.0)

    def products(self, h):
        c, r = h // self.per_chunk, h % self.per_chunk
        if self.form == "bf16":
            rows = slice(r * self.HP, r * self.HP + self.W)
            return [(self.qT[rows, c, :], self.kT[rows, c, :])]
        high = (self.qT[:, c, :], self.kT[:, c, r, :])
        if self.form == "packed":
            return [high]
        return [high, (self.qL[:, c, :], self.kT[:, c, r, :]), (self.qT[:, c, :], self.kL[:, c, r, :])]

    def flip_bank(self, n):
        bank = (self.psT if n % 4 < 2 else self.psO)[:, n % 2, :]
        return bank if self.dt == F32 else bank.bitcast(BF16)

    def flip(self, nc, pe, ident):
        per = self.cols // SEQ
        for n in range(2 * self.banks):
            if n >= 4:
                pe.wait_ge(self.operands, n - 3)
            rows, view = (self.k_rows, self.q_rows)[n % 2], self.flip_bank(n)
            for i in range(per):
                c = n // 2 * per + i
                for t in range(2):
                    src = rows[:, t, c * self.per_chunk:(c + 1) * self.per_chunk, :]
                    ins = nc.tensor.transpose(view[:, i * SEQ + t * P:i * SEQ + (t + 1) * P],
                                              src.rearrange("p h d -> p (h d)"), ident[:])
            ins.then_inc(self.rows_turned, 1)

    def keep_high(self, nc, act):
        per = self.cols // SEQ
        done = self.high_kept if self.form == "halves" else self.operands
        for n in range(2 * self.banks):
            act.wait_ge(self.rows_turned, n + 1)
            view = self.flip_bank(n)[:, 0:self.cols].rearrange("p (c t) -> p c t", t=SEQ)
            m = n // 2 * per
            if n % 2 or self.form == "bf16":
                to = self.qT if n % 2 else self.kT
                ins = nc.scalar.copy(to[:, m:m + per, :], view)
            else:
                for r in range(2):
                    rows = slice(r * 64, (r + 1) * 64)
                    ins = nc.scalar.copy(self.kT[rows, m:m + per, r, :], view[rows])
            ins.then_inc(done, 1)

    def keep_low(self, nc, dve):
        per = self.cols // SEQ
        for n in range(2 * self.banks):
            dve.wait_ge(self.high_kept, n + 1)
            view = self.flip_bank(n).rearrange("p (c t) -> p c t", t=SEQ)
            m = n // 2 * per
            if n % 2:
                ins = nc.vector.tensor_tensor(self.qL[:, m:m + per, :], view,
                                              self.qT[:, m:m + per, :].bitcast(F32), ALU.subtract)
            else:
                for r in range(2):
                    rows = slice(r * 64, (r + 1) * 64)
                    ins = nc.vector.tensor_tensor(self.kL[rows, m:m + per, r, :], view[rows],
                                                  self.kT[rows, m:m + per, r, :].bitcast(F32), ALU.subtract)
            ins.then_inc(self.operands, 1)

    def tensor(self, nc, pe, C, mask, beside):
        self.flip(nc, pe, C["ident"] if self.dt == F32 else C["ident_bf"])
        beside(-1)
        pe.wait_ge(self.v_ready, 1)
        for step in range(self.H + 3):
            if step < self.H:
                self.scores(nc, pe, step, C["ident_bf"], mask(step))
            if 2 <= step < self.H + 2:
                self.turn(nc, pe, step - 2, C["ident"])
            if step >= 3:
                self.values(nc, pe, step - 3)
            beside(step)

    def scores(self, nc, pe, h, ident_bf, mask):
        if h * self.banks % self.H == 0:
            pe.wait_ge(self.operands, 2 * (h * self.banks // self.H + 1))
        if h >= 2:
            pe.wait_ge(self.exp_done, h - 1)
        bank = self.psS[:, h % 2, :]
        nc.tensor.matmul(bank[:, 0:CAUSAL3], ident_bf[:], mask, start=True, stop=True)
        for q, k in self.products(h):
            nc.tensor.matmul(bank[:, 0:P], q[:, 0:P], k[:, 0:P], start=False, stop=False, skip_group_check=True)
            ins = nc.tensor.matmul(bank[:, P:CAUSAL3], q[:, P:SEQ], k, start=False, stop=False,
                                   skip_group_check=True)
        ins.then_inc(self.scores_done, 1)

    def turn(self, nc, pe, h, ident):
        pe.wait_ge(self.exp_done, h + 1)
        if h == 0:
            pe.wait_ge(self.operands, 2 * self.banks)
        if h >= 2:
            pe.wait_ge(self.probs_ready, h - 1)
        for i in range(3):
            at = slice(i * P, (i + 1) * P)
            ins = nc.tensor.transpose(self.psT[:, h % 2, at], self.prow[:, h % 2, at], ident[:])
        ins.then_inc(self.probs_turned, 1)

    def values(self, nc, pe, h):
        pe.wait_ge(self.probs_ready, h + 1)
        if h and h % self.per_round == 0:
            pe.wait_ge(self.o_ready, h // self.per_round)
        o, at = (h % self.per_round) * self.W, h * self.W
        pr = self.probsT[:, h % 2, :]
        low, high = self.v_wide[:, 0, at:at + P], self.v_wide[:, 1, at:at + P]
        nc.tensor.matmul(self.psO[:, 0, o:o + P], pr[:, 0:P], low, start=True, stop=True)
        nc.tensor.matmul(self.psO[:, 1, o:o + P], pr[:, P:SEQ], low, start=True, stop=False)
        nc.tensor.matmul(self.psO[:, 1, o:o + P], pr[:, SEQ:CAUSAL3], high, start=False,
                         stop=True).then_inc(self.pv_done, 1)

    def scalar(self, nc, act, beside):
        self.keep_high(nc, act)
        beside(-1)
        for h in range(self.H):
            act.wait_ge(self.max_taken, h + 1)
            if h >= 2:
                act.wait_ge(self.probs_turned, h - 1)
            for t, (a, b) in enumerate(((0, P), (P, CAUSAL3))):
                ins = nc.scalar.activation(self.prow[:, h % 2, a:b], self.psS[:, h % 2, a:b], ACT.Exp,
                                           bias=self.negmax[:, t, h:h + 1])
            ins.then_inc(self.exp_done, 1)
            beside(h)

    def vector(self, nc, dve, link, beside):
        beside(-1)
        if self.form == "halves":
            self.keep_low(nc, dve)
        for step in range(self.H + 2):
            if step < self.H:
                dve.wait_ge(self.scores_done, step + 1)
                for t, (a, b) in enumerate(((0, P), (P, CAUSAL3))):
                    ins = nc.vector.tensor_reduce(self.negmax[:, t, step:step + 1], self.psS[:, step % 2, a:b],
                                                  AX_X, ALU.max, negate=True)
                ins.then_inc(self.max_taken, 1)
            h = step - 2
            if h >= 0:
                dve.wait_ge(self.probs_turned, h + 1)
                if h >= 2:
                    dve.wait_ge(self.pv_done, h - 1)
                nc.vector.tensor_copy(self.probsT[:, h % 2, :], self.psT[:, h % 2, 0:CAUSAL3]).then_inc(
                    self.probs_ready, 1)
            if h >= 1 and h % self.per_round == 0:
                self.normalise(nc, dve, link, h // self.per_round - 1)
            beside(step)
        self.normalise(nc, dve, link, self.rounds - 1)

    def normalise(self, nc, dve, link, r):
        dve.wait_ge(self.pv_done, (r + 1) * self.per_round)
        hs = slice(r * self.per_round, (r + 1) * self.per_round)
        views = [self.psO[:, t, 0:self.per_round * self.W].rearrange("p (h w) -> p h w", w=self.W) for t in range(2)]
        for t in range(2):
            ins = nc.vector.reciprocal(self.rsum[:, t, hs], views[t][:, :, self.D])
        link(ins)
        for t in range(2):
            ins = nc.vector.tensor_tensor(self.o_rows[:, t, hs, :], views[t][:, :, 0:self.D],
                                          spread(self.rsum[:, t, hs], 2, [P, self.per_round, self.D]), ALU.mult)
        ins.then_inc(self.o_ready, 1)


def load_block(nc, s, pairs):
    landed = s.sem("loaded")
    with nc.Block() as block:
        @block.sync
        def _(sp):
            for to, src in pairs:
                sp.dma_start(to, src).then_inc(landed, 16)
            sp.wait_ge(landed, 16 * len(pairs))


def cross_attention(nc, x, C, D, layer, rounded):
    H, HD = 16, 16
    with ExitStack() as ctx:
        s = Stage(nc, ctx, f"x{layer}")
        wdt = BF16 if rounded else F32
        wq, wkv = s.sb("wq", [P, KD, DIM], wdt), s.sb("wkv", [P, KD, 2 * DIM], wdt)
        wo = s.sb("wo", [P, KD, DIM], wdt)
        bq, bkv, bo = s.sb("bq", [P, DIM], wdt), s.sb("bkv", [P, 2 * DIM], wdt), s.sb("bo", [P, DIM], wdt)
        pairs = []
        staged = []
        for to, name in ((wq, "wqT"), (wkv, "wkvT"), (wo, "woT"), (bq, "bq"), (bkv, "bkv"), (bo, "bo")):
            src = D[f"L{layer}_{name}"]
            if name[0] == "b":
                src = src.partition_broadcast(P)
            if rounded:
                raw = s.sb(f"raw_{name}", list(to.shape))
                staged.append((to, raw))
                pairs.append((raw[:], src))
            else:
                pairs.append((to[:], src))
        if rounded:
            keep = s.sb("key_mask", [P, TILES], I32)
            blocked = s.sb("blocked", [P, TILES])
            pairs.append((keep[:], D["mask_if1"]))
        load_block(nc, s, pairs)

        psA = [s.ps(f"work{i}", [P, BANK]) for i in range(2)]
        att = Attention(s, H, HD, "bf16" if rounded else "packed")
        ln = LayerNorm(s, 2)
        xnb = s.sb("xn_bf", [P, 2, DIM], BF16) if rounded else None
        ctxT = s.sb("ctxT", [P, KD, SEQ])
        ctxTb = s.sb("ctxT_bf", [P, KD, SEQ], BF16) if rounded else ctxT
        xnT = s.sb("xnT", [P, KD, SEQ], wdt)
        oT = s.sb("oT", [P, KD, SEQ], wdt)
        ob = s.sb("o_bf", [P, 2, DIM], BF16) if rounded else None
        raw = s.sb("qk_raw", [P, 2, 2, H, HD], wdt)
        biased = s.sb("biased", [P, 2, 2, DIM], BF16) if rounded else None
        vr = s.sb("v_raw", [P, 2, DIM], wdt)
        rot = s.sb("rotary", [P, 2, 2, H, HD // 2]) if not rounded else None
        turned = s.sb("turned_by_position", [P, 2, H, HD]) if not rounded else None
        prod = s.sb("outproj_bf", [P, 2, DIM], BF16) if rounded else None
        sem = {n: s.sem(n) for n in ("link", "ctx_landed", "ctx_cast", "kv_done", "x_turned", "q_done", "by_act",
                                     "by_dve", "x_bf", "o_bf", "o_turned", "out_done", "bias_added", "x_ready",
                                     "weights_cast")}

        with nc.Block() as block:
            @block.vector
            def _(dve):
                link = chain(dve, sem["link"])
                for to, r in staged:
                    nc.vector.tensor_copy(to[:], r[:])
                att.clear(nc)
                link(nc.vector.memset(raw[:], 0.0))
                if rounded:
                    nc.vector.memset(att.q_rows[:, :, :, HD:HD + 1], 1.0)
                    link(nc.vector.tensor_scalar(blocked[:], keep[:], 0.0, MASKED, ALU.is_le, ALU.mult))
                link(nc.vector.memset(raw[:], 0.0))
        s.again()

        A, V = sem["by_act"], sem["by_dve"]
        ident = C["ident_bf"] if rounded else C["ident"]

        def turn(front, core, tail):
            made = 5 if front is not None else 0
            turned_o = 1 if tail is not None else 0
            readers = [A][:turned_o] + [V, V, A, V, V][:made] + [V, V]
            USE_KV, USE_X, USE_Q, USE_OUT = turned_o, turned_o + 2, turned_o + 3, turned_o + made
            if front is not None:
                first, batch = front

            def parts(t):
                return [x[:, first + t, :]]

            with nc.Block() as block:
                @block.sync
                def _(sp):
                    if front is not None:
                        sp.dma_start(ctxT[:], D["ctxT"][batch]).then_inc(sem["ctx_landed"], 16)

                @block.gpsimd
                def _(pool):
                    if tail is not None and not rounded:
                        for t in range(2):
                            ins = nc.gpsimd.tensor_tensor(x[:, tail + t, :], x[:, tail + t, :], bo[:], ALU.add)
                        ins.then_inc(sem["bias_added"], 1)
                    if front is None:
                        return
                    if rounded:
                        pool.wait_ge(sem["ctx_landed"], 16)
                        nc.gpsimd.tensor_copy(ctxTb[:], ctxT[:]).then_inc(sem["ctx_cast"], 1)
                    ln.root(nc, pool, C["minus_half"])

                @block.tensor
                def _(pe):
                    ring = Ring(psA, readers)

                    def beside(step):
                        if step == -1 and tail is not None:
                            bank = ring.claim(pe)
                            view = bank[:].bitcast(BF16) if rounded else bank[:]
                            orow = ob if rounded else att.o_rows
                            for k in range(KD):
                                for t in range(2):
                                    src = (orow[:, t, k * P:(k + 1) * P] if rounded else
                                           orow[:, t, k * 8:(k + 1) * 8, :].rearrange("p h d -> p (h d)"))
                                    ins = nc.tensor.transpose(view[:, k * SEQ + t * P:k * SEQ + (t + 1) * P], src,
                                                              ident[:])
                            ins.then_inc(sem["o_turned"], 1)
                        if step in (0, 1) and front is not None:
                            if step == 0:
                                if rounded:
                                    pe.wait_ge(sem["ctx_cast"], 1)
                                else:
                                    pe.wait_ge(sem["ctx_landed"], 16)
                            bank = ring.claim(pe)
                            for k in range(KD):
                                ins = nc.tensor.matmul(bank[:], ctxTb[:, k, step * P:(step + 1) * P], wkv[:, k, :],
                                                       start=(k == 0), stop=(k == KD - 1))
                            ins.then_inc(sem["kv_done"], 1)
                        if step == 3 and front is not None:
                            bank = ring.claim(pe)
                            view = bank[:].bitcast(BF16) if rounded else bank[:]
                            src = xnb if rounded else ln.xn
                            pe.wait_ge(sem["x_bf"] if rounded else ln.xn_ready, 1)
                            for k in range(KD):
                                for t in range(2):
                                    ins = nc.tensor.transpose(view[:, k * SEQ + t * P:k * SEQ + (t + 1) * P],
                                                              src[:, t, k * P:(k + 1) * P], ident[:])
                            ins.then_inc(sem["x_turned"], 1)
                        if step in (5, 6) and front is not None:
                            t = step - 5
                            if t == 0:
                                pe.wait_ge(A, turned_o + 1)
                            bank = ring.claim(pe)
                            for k in range(KD):
                                ins = nc.tensor.matmul(bank[:, 0:DIM], xnT[:, k, t * P:(t + 1) * P], wq[:, k, :],
                                                       start=(k == 0), stop=(k == KD - 1))
                            ins.then_inc(sem["q_done"], 1)
                        if step in (7, 8) and tail is not None:
                            t = step - 7
                            if t == 0:
                                pe.wait_ge(A, 1)
                            bank = ring.claim(pe)
                            for k in range(KD):
                                ins = nc.tensor.matmul(bank[:, 0:DIM], oT[:, k, t * P:(t + 1) * P], wo[:, k, :],
                                                       start=(k == 0), stop=(k == KD - 1))
                            ins.then_inc(sem["out_done"], 1)

                    if core is None:
                        for step in range(-1, H):
                            beside(step)
                    else:
                        att.tensor(nc, pe, C, lambda h: C["causal" if rounded or h < 4 else "window"][:], beside)

                @block.scalar
                def _(act):
                    ring = Ring(psA, readers)

                    def beside(step):
                        if step == -1 and tail is not None:
                            act.wait_ge(sem["o_turned"], 1)
                            view = ring.bank(0)[:].bitcast(BF16) if rounded else ring.bank(0)[:]
                            nc.scalar.copy(oT[:], view[:, 0:KD * SEQ].rearrange("p (k t) -> p k t", k=KD)).then_inc(A, 1)
                        if step == 4 and front is not None:
                            act.wait_ge(sem["x_turned"], 1)
                            view = ring.bank(USE_X)[:].bitcast(BF16) if rounded else ring.bank(USE_X)[:]
                            nc.scalar.copy(xnT[:], view[:, 0:KD * SEQ].rearrange("p (k t) -> p k t", k=KD)).then_inc(A, 1)

                    if core is None:
                        for step in range(-1, H):
                            beside(step)
                    else:
                        nc.scalar.copy(att.v_rows[:, :, :, 0:HD],
                                       vr[:].rearrange("p t (h d) -> p t h d", h=H)).then_inc(att.v_ready, 1)
                        att.scalar(nc, act, beside)

                @block.vector
                def _(dve):
                    ring = Ring(psA, readers)
                    link = chain(dve, sem["link"])

                    def by_position(which, t):
                        q_or_k = "q" if which == 0 else "k"
                        cos, sin = C[f"rope_cos_{q_or_k}"], C[f"rope_sin_{q_or_k}"]
                        even, odd = raw[:, t, which, :, 0:HD:2], raw[:, t, which, :, 1:HD:2]
                        shape = [P, H, HD // 2]
                        ct, st = spread(cos[:, t, :], 1, shape), spread(sin[:, t, :], 1, shape)
                        out_e, out_o = turned[:, t, :, 0:HD:2], turned[:, t, :, 1:HD:2]
                        nc.vector.tensor_tensor(rot[:, t, 0], even, st, ALU.mult)
                        nc.vector.tensor_tensor(rot[:, t, 1], odd, st, ALU.mult)
                        nc.vector.tensor_tensor(out_e, even, ct, ALU.mult)
                        link(nc.vector.tensor_tensor(out_o, odd, ct, ALU.mult))
                        nc.vector.tensor_tensor(out_e, out_e, rot[:, t, 1], ALU.subtract)
                        link(nc.vector.tensor_tensor(out_o, out_o, rot[:, t, 0], ALU.add))

                    def split(which, to):
                        low, again = (2, 1) if which == 0 else (1, 2)
                        parts_of = [to[:, :, :, i * HD:(i + 1) * HD] for i in range(3)]
                        nc.vector.tensor_copy(parts_of[again].bitcast(F32R), turned[:])
                        link(nc.vector.tensor_copy(parts_of[0].bitcast(F32R), turned[:]))
                        link(nc.vector.tensor_tensor(parts_of[low], turned[:], parts_of[0], ALU.subtract))

                    def add_output(t):
                        dve.wait_ge(sem["out_done"], t + 1)
                        bank = ring.bank(USE_OUT + t)
                        if rounded:
                            link(nc.vector.tensor_copy(prod[:, t, :], bank[:, 0:DIM]))
                            link(nc.vector.tensor_tensor(prod[:, t, :], prod[:, t, :], bo[:], ALU.add))
                            nc.vector.tensor_tensor(x[:, tail + t, :], x[:, tail + t, :], prod[:, t, :],
                                                    ALU.add).then_inc(V, 1)
                        else:
                            dve.wait_ge(sem["bias_added"], 1)
                            nc.vector.tensor_tensor(x[:, tail + t, :], x[:, tail + t, :], bank[:, 0:DIM],
                                                    ALU.add).then_inc(V, 1)

                    def beside(step):
                        if step == 0 and tail is not None:
                            dve.wait_ge(sem["o_turned"], 1)
                        if step in (12, 13) and tail is not None:
                            add_output(step - 12)
                        if front is None:
                            return
                        if step == -1:
                            ln.statistics(nc, link, parts)
                        if step == 2:
                            ln.apply(nc, dve, parts)
                            if rounded:
                                dve.wait_ge(ln.xn_ready, 1)
                                nc.vector.tensor_copy(xnb[:], ln.xn[:]).then_inc(sem["x_bf"], 1)
                        if step in (1, 3):
                            t = step // 3
                            dve.wait_ge(sem["kv_done"], t + 1)
                            if core is not None and t == 0:
                                dve.wait_ge(att.v_ready, 1)
                            bank = ring.bank(USE_KV + t)
                            if rounded:
                                nc.vector.tensor_copy(biased[:, t, 1, :], bank[:, 0:DIM])
                                nc.vector.tensor_copy(vr[:, t, :], bank[:, DIM:2 * DIM]).then_inc(V, 1)
                            else:
                                nc.vector.tensor_tensor(raw[:, t, 1].rearrange("p h d -> p (h d)"), bank[:, 0:DIM],
                                                        bkv[:, 0:DIM], ALU.add)
                                nc.vector.tensor_tensor(vr[:, t, :], bank[:, DIM:2 * DIM], bkv[:, DIM:2 * DIM],
                                                        ALU.add).then_inc(V, 1)
                        if step in (4, 5):
                            t = step - 4
                            if t == 0:
                                dve.wait_ge(V, 2)
                                if core is not None:
                                    dve.wait_ge(att.rows_turned, 2 * att.banks)
                            if rounded:
                                nc.vector.tensor_tensor(att.k_rows[:, t, :, 0:HD],
                                                        biased[:, t, 1, :].rearrange("p (h d) -> p h d", h=H),
                                                        bkv[:, 0:DIM].rearrange("p (h d) -> p h d", h=H), ALU.add)
                                nc.vector.tensor_copy(att.k_rows[:, t, :, HD:HD + 1],
                                                      blocked[:, bass.ds(first + t, 1)].unsqueeze(1).to_broadcast([P, H, 1]))
                                link(nc.vector.tensor_tensor(vr[:, t, :], vr[:, t, :], bkv[:, DIM:2 * DIM], ALU.add))
                            else:
                                by_position(1, t)
                        if step == 6 and not rounded:
                            split(1, att.k_rows)
                        if step in (7, 8):
                            t = step - 7
                            dve.wait_ge(sem["q_done"], t + 1)
                            bank = ring.bank(USE_Q + t)
                            if rounded:
                                nc.vector.tensor_copy(biased[:, t, 0, :], bank[:, 0:DIM]).then_inc(V, 1)
                            else:
                                nc.vector.tensor_tensor(raw[:, t, 0].rearrange("p h d -> p (h d)"), bank[:, 0:DIM],
                                                        bq[:], ALU.add).then_inc(V, 1)
                        if step in (9, 10):
                            t = step - 9
                            if t == 0:
                                dve.wait_ge(V, 4)
                            if rounded:
                                link(nc.vector.tensor_tensor(att.q_rows[:, t, :, 0:HD],
                                                             biased[:, t, 0, :].rearrange("p (h d) -> p h d", h=H),
                                                             bq[:].rearrange("p (h d) -> p h d", h=H), ALU.add))
                            else:
                                by_position(0, t)
                        if step == 11:
                            if rounded:
                                rows = att.q_rows[:, :, :, 0:HD]
                                link(nc.vector.tensor_scalar(rows, rows, 1.0 / HD ** 0.5, None, ALU.mult))
                            else:
                                split(0, att.q_rows)

                    if core is None:
                        for step in range(-1, H):
                            beside(step)
                    else:
                        att.vector(nc, dve, link, beside)
                        if rounded:
                            dve.wait_ge(att.o_ready, att.rounds)
                            nc.vector.tensor_copy(ob[:], att.o_rows[:].rearrange("p t h d -> p t (h d)")).then_inc(
                                sem["o_bf"], 1)
            s.again()

        turn((0, 0), None, None)
        turn((2, 1), 0, None)
        with nc.Fori(0, BATCH - 2) as b:
            turn((b * 2 + 4, b + 2), b * 2 + 2, b * 2)
        turn(None, 2 * (BATCH - 1), 2 * (BATCH - 2))
        turn(None, None, 2 * (BATCH - 1))


def turn_rows(nc, bank, rows, ident, tiles, width):
    for k in range(width // P):
        for t in range(tiles):
            at = (k * tiles + t) * P
            ins = nc.tensor.transpose(bank[:, at:at + P], rows[:, t, k * P:(k + 1) * P], ident[:])
    return ins


def linear_attention(nc, x, C, D):
    H, HD = 16, 16
    with ExitStack() as ctx:
        s = Stage(nc, ctx, "x1")
        wq, wkv, wo = s.sb("wq", [P, KD, DIM]), s.sb("wkv", [P, KD, 2 * DIM]), s.sb("wo", [P, KD, DIM])
        bq, bkv, bo = s.sb("bq", [P, KD]), s.sb("bkv", [P, 2 * DIM]), s.sb("bo", [P, DIM])
        dropped = s.sb("dropped", [P, TILES], U8)
        keep = s.sb("keep", [P, TILES])
        load_block(nc, s, [(wq[:], D["L1_wqT"]), (wkv[:], D["L1_wkvT"]), (wo[:], D["L1_woT"]),
                           (bq[:], D["L1_bq_col"]), (bkv[:], D["L1_bkv"].partition_broadcast(P)),
                           (bo[:], D["L1_bo"].partition_broadcast(P)), (dropped[:], D["mask_bk1"])])
        ps_kv = [s.ps(f"kv{t}", [P, BANK]) for t in range(2)]
        ps_x = s.ps("turned", [P, BANK])
        ps_q = [s.ps(f"q{c}", [P, BANK]) for c in range(KD)]
        ps_m = s.ps("key_value", [P, BANK])
        ps_y = [s.ps(f"out{t}", [P, BANK]) for t in range(2)]
        ln = LayerNorm(s, 2)
        ctxT, xnT = s.sb("ctxT", [P, KD, SEQ]), s.sb("xnT", [P, KD, SEQ])
        k_raw, k_neg, k_exp, k_sq = (s.sb(n, [P, 2, DIM]) for n in ("k_raw", "k_neg", "k_exp", "k_sq"))
        k_ss, k_rn = s.sb("k_ss", [P, 2 * H]), s.sb("k_rn", [P, 2 * H])
        q_raw, q_neg, q_exp, q_sq = (s.sb(n, [P, KD, SEQ]) for n in ("q_raw", "q_neg", "q_exp", "q_sq"))
        q_ss, q_rn = s.sb("q_ss", [P, KD]), s.sb("q_rn", [P, KD])
        v = s.sb("v", [P, 2, DIM])
        m = s.sb("m", [P, KD, P])
        oT = s.sb("oT", [P, KD, SEQ])
        sem = {n: s.sem(n) for n in ("link", "ctx_landed", "kv_done", "x_turned", "xnT_ready", "q_done", "k_neg",
                                     "k_exp", "k_ss", "k_bounded", "k_rn", "k_ready", "q_neg", "q_exp", "q_ready", "q_ss",
                                     "q_bounded", "q_rn", "m_done", "m_ready", "o_done", "o_ready", "y_done",
                                     "bias_added", "x_ready")}
        with nc.Block() as block:
            @block.vector
            def _(dve):
                link = chain(dve, sem["link"])
                link(nc.vector.tensor_scalar(keep[:], dropped[:], -1.0, 1.0, ALU.mult, ALU.add))
        s.again()
        with nc.Fori(0, BATCH) as b:
            with nc.Block() as block:
                def parts(t):
                    return [x[:, b * 2 + t, :]]

                @block.sync
                def _(sp):
                    sp.dma_start(ctxT[:], D["ctxT"][b]).then_inc(sem["ctx_landed"], 16)

                @block.gpsimd
                def _(pool):
                    ln.root(nc, pool, C["minus_half"])
                    pool.wait_ge(ln.xn_ready, 1)
                    for t in range(2):
                        ins = nc.gpsimd.tensor_tensor(x[:, b * 2 + t, :], x[:, b * 2 + t, :], bo[:], ALU.add)
                    ins.then_inc(sem["bias_added"], 1)
                    pool.wait_ge(sem["k_ss"], 1)
                    nc.gpsimd.tensor_scalar(k_ss[:], k_ss[:], TINY_SQ, None, ALU.max).then_inc(sem["k_bounded"], 1)
                    pool.wait_ge(sem["k_bounded"], 1)
                    nc.gpsimd.tensor_tensor(k_rn[:], k_ss[:], C["minus_half"][:, 0:2 * H], ALU.pow).then_inc(sem["k_rn"], 1)
                    pool.wait_ge(sem["q_ss"], KD)
                    nc.gpsimd.tensor_scalar(q_ss[:], q_ss[:], TINY_SQ, None, ALU.max).then_inc(sem["q_bounded"], 1)
                    pool.wait_ge(sem["q_bounded"], 1)
                    nc.gpsimd.tensor_tensor(q_rn[:], q_ss[:], C["minus_half"][:, 0:KD], ALU.pow).then_inc(sem["q_rn"], 1)

                @block.tensor
                def _(pe):
                    pe.wait_ge(sem["ctx_landed"], 16)
                    for t in range(2):
                        for k in range(KD):
                            ins = nc.tensor.matmul(ps_kv[t][:], ctxT[:, k, t * P:(t + 1) * P], wkv[:, k, :],
                                                   start=(k == 0), stop=(k == KD - 1))
                        ins.then_inc(sem["kv_done"], 1)
                    pe.wait_ge(ln.xn_ready, 1)
                    turn_rows(nc, ps_x, ln.xn, C["ident"], 2, DIM).then_inc(sem["x_turned"], 1)
                    pe.wait_ge(sem["xnT_ready"], 1)
                    for c in range(KD):
                        for k in range(KD):
                            ins = nc.tensor.matmul(ps_q[c][:, 0:SEQ], wq[:, k, c * P:(c + 1) * P], xnT[:, k, :],
                                                   start=(k == 0), stop=(k == KD - 1))
                        ins.then_inc(sem["q_done"], 1)
                    pe.wait_ge(sem["k_ready"], 1)
                    for c in range(KD):
                        for t in range(2):
                            ins = nc.tensor.matmul(ps_m[:, c * P:(c + 1) * P], k_exp[:, t, c * P:(c + 1) * P],
                                                   v[:, t, c * P:(c + 1) * P], start=(t == 0), stop=(t == 1))
                    ins.then_inc(sem["m_done"], 1)
                    pe.wait_ge(sem["m_ready"], 1)
                    for c in range(KD):
                        ins = nc.tensor.matmul(ps_q[c][:, 0:SEQ], m[:, c, :], q_exp[:, c, :], start=True, stop=True)
                        ins.then_inc(sem["o_done"], 1)
                    pe.wait_ge(sem["o_ready"], KD)
                    for t in range(2):
                        for k in range(KD):
                            ins = nc.tensor.matmul(ps_y[t][:, 0:DIM], oT[:, k, t * P:(t + 1) * P], wo[:, k, :],
                                                   start=(k == 0), stop=(k == KD - 1))
                        ins.then_inc(sem["y_done"], 1)

                @block.scalar
                def _(act):
                    act.wait_ge(sem["k_neg"], 1)
                    nc.scalar.activation(k_exp[:], k_neg[:], ACT.Exp).then_inc(sem["k_exp"], 1)
                    act.wait_ge(sem["x_turned"], 1)
                    nc.scalar.copy(xnT[:], ps_x[:].rearrange("p (k t) -> p k t", k=KD)).then_inc(sem["xnT_ready"], 1)
                    act.wait_ge(sem["q_neg"], 1)
                    nc.scalar.activation(q_exp[:], q_neg[:], ACT.Exp).then_inc(sem["q_exp"], 1)
                    act.wait_ge(sem["q_ready"], 1)
                    for c in range(KD):
                        nc.scalar.activation(q_sq[:, c, :], q_exp[:, c, :], ACT.Square,
                                             accum_out=q_ss[:, c:c + 1]).then_inc(sem["q_ss"], 1)
                    for c in range(KD):
                        act.wait_ge(sem["o_done"], c + 1)
                        nc.scalar.copy(oT[:, c, :], ps_q[c][:, 0:SEQ]).then_inc(sem["o_ready"], 1)

                @block.vector
                def _(dve):
                    link = chain(dve, sem["link"])
                    ln.statistics(nc, link, parts)
                    ln.apply(nc, dve, parts)
                    for t in range(2):
                        dve.wait_ge(sem["kv_done"], t + 1)
                        nc.vector.tensor_tensor(k_raw[:, t, :], ps_kv[t][:, 0:DIM], bkv[:, 0:DIM], ALU.add)
                        ins = nc.vector.tensor_tensor(v[:, t, :], ps_kv[t][:, DIM:2 * DIM], bkv[:, DIM:2 * DIM], ALU.add)
                    link(ins)
                    nc.vector.tensor_scalar(k_neg[:], k_raw[:], 0.0, None, ALU.min).then_inc(sem["k_neg"], 1)
                    dve.wait_ge(sem["k_exp"], 1)
                    link(nc.vector.scalar_tensor_tensor(k_exp[:], k_raw[:], 0.0, k_exp[:], ALU.max, ALU.add))
                    for t in range(2):
                        ins = nc.vector.tensor_scalar(k_exp[:, t, :], k_exp[:, t, :], keep[:, bass.ds(b * 2 + t, 1)], None, ALU.mult)
                    link(ins)
                    link(nc.vector.tensor_tensor(k_sq[:], k_exp[:], k_exp[:], ALU.mult))
                    nc.vector.tensor_reduce(k_ss[:], k_sq[:].rearrange("p t (h d) -> p (t h) d", h=H), AX_X,
                                            ALU.add).then_inc(sem["k_ss"], 1)
                    for c in range(KD):
                        dve.wait_ge(sem["q_done"], c + 1)
                        ins = nc.vector.tensor_scalar(q_raw[:, c, :], ps_q[c][:, 0:SEQ], bq[:, c:c + 1], None, ALU.add)
                    link(ins)
                    nc.vector.tensor_scalar(q_neg[:], q_raw[:], 0.0, None, ALU.min).then_inc(sem["q_neg"], 1)
                    dve.wait_ge(sem["k_rn"], 1)
                    heads = k_exp[:].rearrange("p t (h d) -> p (t h) d", h=H)
                    nc.vector.tensor_tensor(heads, heads, spread(k_rn[:], 2, [P, 2 * H, HD]),
                                            ALU.mult).then_inc(sem["k_ready"], 1)
                    dve.wait_ge(sem["q_exp"], 1)
                    nc.vector.scalar_tensor_tensor(q_exp[:], q_raw[:], 0.0, q_exp[:], ALU.max,
                                                   ALU.add).then_inc(sem["q_ready"], 1)
                    dve.wait_ge(sem["m_done"], 1)
                    dve.wait_ge(sem["q_rn"], 1)
                    for c in range(KD):
                        ins = nc.vector.scalar_tensor_tensor(m[:, c, :], ps_m[:, c * P:(c + 1) * P], q_rn[:, c:c + 1],
                                                             C["head_blocks"][:], ALU.mult, ALU.mult)
                    ins.then_inc(sem["m_ready"], 1)
                    dve.wait_ge(sem["bias_added"], 1)
                    for t in range(2):
                        dve.wait_ge(sem["y_done"], t + 1)
                        nc.vector.tensor_tensor(x[:, b * 2 + t, :], x[:, b * 2 + t, :], ps_y[t][:, 0:DIM],
                                                ALU.add).then_inc(sem["x_ready"], 1)
            s.again()


def memory_attention(nc, x, C, D):
    with ExitStack() as ctx:
        s = Stage(nc, ctx, "x3")
        wq, wk, wo = (s.sb(n, [P, KD, DIM]) for n in ("wq", "wk", "wo"))
        bq, bk, bo = s.sb("bq", [P, KD]), s.sb("bk", [P, KD]), s.sb("bo", [P, DIM])
        load_block(nc, s, [(wq[:], D["L3_wqT"]), (wk[:], D["L3_wkT"]), (wo[:], D["L3_woT"]),
                           (bq[:], D["L3_bq_col"]), (bk[:], D["L3_bk_col"]),
                           (bo[:], D["L3_bo"].partition_broadcast(P))])
        ps_k = s.ps("k", [P, KD * SEQ])
        ps_x = s.ps("turned", [P, BANK])
        ps_q = s.ps("q", [P, KD * SEQ])
        ps_s = [s.ps(f"scores{t}", [P, BANK]) for t in range(2)]
        ps_p = s.ps("probs_turned", [P, BANK])
        ps_o = s.ps("o", [P, KD * SEQ])
        ps_y = s.ps("out", [P, BANK])
        ln = LayerNorm(s, 2)
        ctxT, xnT = s.sb("ctxT", [P, KD, SEQ]), s.sb("xnT", [P, KD, SEQ])
        ctx_rows = s.sb("ctx_rows", [P, 2, DIM])
        masked, mrow, ones = s.sb("masked", [1, SEQ], U8), s.sb("mask_row", [1, SEQ]), s.sb("ones", [1, P])
        kT, qT = s.sb("kT", [P, KD, SEQ]), s.sb("qT", [P, KD, SEQ])
        negmax, rsum, rinv = s.sb("negmax", [P, 2]), s.sb("rsum", [P, 2]), s.sb("rinv", [P, 2])
        probs, pT, oT = s.sb("probs", [P, 2, SEQ]), s.sb("pT", [P, 2, SEQ]), s.sb("oT", [P, KD, SEQ])
        sem = {n: s.sem(n) for n in ("link", "ctx_landed", "rows_landed", "mask_landed", "mask_ready", "k_done",
                                     "kT_ready", "x_turned", "xnT_ready", "q_done", "qT_ready", "s_done",
                                     "max_ready", "exp_done", "p_ready", "p_turned", "pT_ready", "o_done",
                                     "oT_ready", "y_done", "bias_added", "x_ready")}
        with nc.Fori(0, BATCH) as b:
            with nc.Block() as block:
                def parts(t):
                    return [x[:, b * 2 + t, :]]

                @block.sync
                def _(sp):
                    sp.dma_start(ctxT[:], D["ctxT"][b]).then_inc(sem["ctx_landed"], 16)
                    sp.dma_start(masked[:], D["mask_bk0"][bass.ds(b, 1), :]).then_inc(sem["mask_landed"], 16)
                    sp.dma_start(ctx_rows[:], D["ctx"][b]).then_inc(sem["rows_landed"], 16)

                @block.gpsimd
                def _(pool):
                    ln.root(nc, pool, C["minus_half"])
                    pool.wait_ge(ln.xn_ready, 1)
                    for t in range(2):
                        ins = nc.gpsimd.tensor_tensor(x[:, b * 2 + t, :], x[:, b * 2 + t, :], bo[:], ALU.add)
                    ins.then_inc(sem["bias_added"], 1)

                @block.tensor
                def _(pe):
                    pe.wait_ge(sem["ctx_landed"], 16)
                    for c in range(KD):
                        for k in range(KD):
                            ins = nc.tensor.matmul(ps_k[:, c * SEQ:(c + 1) * SEQ], wk[:, k, c * P:(c + 1) * P],
                                                   ctxT[:, k, :], start=(k == 0), stop=(k == KD - 1))
                    ins.then_inc(sem["k_done"], 1)
                    pe.wait_ge(ln.xn_ready, 1)
                    turn_rows(nc, ps_x, ln.xn, C["ident"], 2, DIM).then_inc(sem["x_turned"], 1)
                    pe.wait_ge(sem["xnT_ready"], 1)
                    for c in range(KD):
                        for k in range(KD):
                            ins = nc.tensor.matmul(ps_q[:, c * SEQ:(c + 1) * SEQ], wq[:, k, c * P:(c + 1) * P],
                                                   xnT[:, k, :], start=(k == 0), stop=(k == KD - 1))
                    ins.then_inc(sem["q_done"], 1)
                    pe.wait_ge(sem["mask_ready"], 1)
                    pe.wait_ge(sem["kT_ready"], KD)
                    pe.wait_ge(sem["qT_ready"], KD)
                    for t in range(2):
                        nc.tensor.matmul(ps_s[t][:, 0:SEQ], ones[:], mrow[:], start=True, stop=False)
                        for c in range(KD):
                            ins = nc.tensor.matmul(ps_s[t][:, 0:SEQ], qT[:, c, t * P:(t + 1) * P], kT[:, c, :],
                                                   start=False, stop=(c == KD - 1))
                        ins.then_inc(sem["s_done"], 1)
                    pe.wait_ge(sem["p_ready"], 2)
                    turn_rows(nc, ps_p, probs, C["ident"], 2, SEQ).then_inc(sem["p_turned"], 1)
                    pe.wait_ge(sem["pT_ready"], 1)
                    pe.wait_ge(sem["rows_landed"], 16)
                    for c in range(KD):
                        for k in range(2):
                            ins = nc.tensor.matmul(ps_o[:, c * SEQ:(c + 1) * SEQ], ctx_rows[:, k, c * P:(c + 1) * P],
                                                   pT[:, k, :], start=(k == 0), stop=(k == 1))
                    ins.then_inc(sem["o_done"], 1)
                    pe.wait_ge(sem["oT_ready"], 1)
                    for t in range(2):
                        for k in range(KD):
                            ins = nc.tensor.matmul(ps_y[:, t * DIM:(t + 1) * DIM], oT[:, k, t * P:(t + 1) * P],
                                                   wo[:, k, :], start=(k == 0), stop=(k == KD - 1))
                    ins.then_inc(sem["y_done"], 1)

                @block.scalar
                def _(act):
                    act.wait_ge(sem["k_done"], 1)
                    for c in range(KD):
                        nc.scalar.activation(kT[:, c, :], ps_k[:, c * SEQ:(c + 1) * SEQ], ACT.Identity,
                                             bias=bk[:, c:c + 1]).then_inc(sem["kT_ready"], 1)
                    act.wait_ge(sem["x_turned"], 1)
                    nc.scalar.copy(xnT[:], ps_x[:].rearrange("p (k t) -> p k t", k=KD)).then_inc(sem["xnT_ready"], 1)
                    act.wait_ge(sem["q_done"], 1)
                    for c in range(KD):
                        nc.scalar.activation(qT[:, c, :], ps_q[:, c * SEQ:(c + 1) * SEQ], ACT.Identity,
                                             bias=bq[:, c:c + 1]).then_inc(sem["qT_ready"], 1)
                    for t in range(2):
                        act.wait_ge(sem["max_ready"], t + 1)
                        nc.scalar.activation(probs[:, t, :], ps_s[t][:, 0:SEQ], ACT.Exp, bias=negmax[:, t:t + 1],
                                             accum_out=rsum[:, t:t + 1]).then_inc(sem["exp_done"], 1)
                    act.wait_ge(sem["p_turned"], 1)
                    nc.scalar.copy(pT[:], ps_p[:].rearrange("p (k t) -> p k t", k=2)).then_inc(sem["pT_ready"], 1)
                    act.wait_ge(sem["o_done"], 1)
                    nc.scalar.copy(oT[:], ps_o[:].rearrange("p (k t) -> p k t", k=KD)).then_inc(sem["oT_ready"], 1)

                @block.vector
                def _(dve):
                    link = chain(dve, sem["link"])
                    ln.statistics(nc, link, parts)
                    ln.apply(nc, dve, parts)
                    dve.wait_ge(sem["mask_landed"], 16)
                    nc.vector.memset(ones[:], 1.0)
                    nc.vector.tensor_scalar(mrow[:], masked[:], MASKED, None, ALU.mult).then_inc(sem["mask_ready"], 1)
                    for t in range(2):
                        dve.wait_ge(sem["s_done"], t + 1)
                        nc.vector.tensor_reduce(negmax[:, t:t + 1], ps_s[t][:, 0:SEQ], AX_X, ALU.max,
                                                negate=True).then_inc(sem["max_ready"], 1)
                    for t in range(2):
                        dve.wait_ge(sem["exp_done"], t + 1)
                        link(nc.vector.reciprocal(rinv[:, t:t + 1], rsum[:, t:t + 1]))
                        nc.vector.tensor_scalar(probs[:, t, :], probs[:, t, :], rinv[:, t:t + 1], None,
                                                ALU.mult).then_inc(sem["p_ready"], 1)
                    dve.wait_ge(sem["bias_added"], 1)
                    dve.wait_ge(sem["y_done"], 1)
                    for t in range(2):
                        nc.vector.tensor_tensor(x[:, b * 2 + t, :], x[:, b * 2 + t, :], ps_y[:, t * DIM:(t + 1) * DIM],
                                                ALU.add).then_inc(sem["x_ready"], 1)
            s.again()


def mixture(nc, x, C, D, layer):
    gated = layer == 3
    FT = -(-(704 if gated else 512) // P)
    HID = FT * P
    CHUNK = 4
    CHUNKS = TILES // CHUNK
    TOK = CHUNK * P
    ups = 2 if gated else 1
    up_at = [0, KD * HID]
    b1_at = KD * HID
    down_at = ups * KD * HID + (0 if gated else FT)
    size = down_at + FT * DIM
    with ExitStack() as ctx:
        s = Stage(nc, ctx, f"f{layer}")
        gate = s.sb("gate", [P, KD, EXPERTS])
        iota = C["iota8"]
        w_all = s.sb("w_all", [P, TILES, EXPERTS])
        xH, xL = (s.sb(n, [P, KD, TILES * P], F32R) for n in ("x_high", "x_low"))
        pairs = [(gate[:], D[f"L{layer}_gate"])]
        if not gated:
            b2 = s.sb("b2", [EXPERTS, DIM])
            pairs.append((b2[:], D["L0_b2"]))
        load_block(nc, s, pairs)

        with ExitStack() as front:
            g = Stage(nc, front, f"g{layer}")
            ln = LayerNorm(g, CHUNK)
            part = g.sb("xnT_part", [P, KD, TOK])
            ps_x = [g.ps(f"turned{k}", [P, BANK]) for k in range(KD)]
            ps_g = g.ps("logits", [P, CHUNK * EXPERTS])
            ps_w = g.ps("w_turned", [EXPERTS, TOK])
            ps_y = [g.ps(f"bias{t}", [P, DIM]) for t in range(CHUNK)]
            logit, prob, chosen, hot = (g.sb(n, [P, CHUNK, EXPERTS]) for n in ("logit", "prob", "chosen", "hot"))
            top, index, index_f = g.sb("top", [P, CHUNK, 8]), g.sb("index", [P, CHUNK, 8], U32), g.sb("index_f", [P, CHUNK, 8])
            peak, total, inv = g.sb("peak", [P, CHUNK]), g.sb("total", [P, CHUNK]), g.sb("inv", [P, CHUNK])
            gates = g.sb("gates", [P, CHUNK, EXPERTS])
            wT = g.sb("wT", [EXPERTS, TOK])
            sem = {n: g.sem(n) for n in ("link", "x_turned", "part_ready", "high_kept", "low_kept", "logits_done", "shifted", "exp_done",
                                         "gates_ready", "w_turned", "wT_ready", "bias_done", "x_ready")}
            with nc.Fori(0, CHUNKS) as c:
                with nc.Block() as block:
                    def parts(t):
                        return [x[:, c * CHUNK + t, :]]

                    @block.gpsimd
                    def _(pool):
                        ln.root(nc, pool, C["minus_half"])
                        pool.wait_ge(sem["part_ready"], KD)
                        high, low = (a[:, :, bass.ds(c * TOK, TOK)] for a in (xH, xL))
                        nc.gpsimd.tensor_copy(high, part[:]).then_inc(sem["high_kept"], 1)
                        pool.wait_ge(sem["high_kept"], 1)
                        nc.gpsimd.tensor_tensor(low, part[:], high.bitcast(F32), ALU.subtract).then_inc(sem["low_kept"], 1)

                    @block.tensor
                    def _(pe):
                        pe.wait_ge(ln.xn_ready, 1)
                        for k in range(KD):
                            for t in range(CHUNK):
                                ins = nc.tensor.transpose(ps_x[k][:, t * P:(t + 1) * P], ln.xn[:, t, k * P:(k + 1) * P],
                                                          C["ident"][:])
                            ins.then_inc(sem["x_turned"], 1)
                        pe.wait_ge(sem["part_ready"], KD)
                        for t in range(CHUNK):
                            for k in range(KD):
                                ins = nc.tensor.matmul(ps_g[:, t * EXPERTS:(t + 1) * EXPERTS],
                                                       part[:, k, t * P:(t + 1) * P], gate[:, k, :],
                                                       start=(k == 0), stop=(k == KD - 1))
                        ins.then_inc(sem["logits_done"], 1)
                        if not gated:
                            pe.wait_ge(sem["gates_ready"], 1)
                            for t in range(CHUNK):
                                ins = nc.tensor.transpose(ps_w[:, t * P:(t + 1) * P], gates[:, t, :], C["ident"][:])
                            ins.then_inc(sem["w_turned"], 1)
                            pe.wait_ge(sem["wT_ready"], 1)
                            for t in range(CHUNK):
                                nc.tensor.matmul(ps_y[t][:], wT[:, t * P:(t + 1) * P], b2[:], start=True,
                                                 stop=True).then_inc(sem["bias_done"], 1)

                    @block.scalar
                    def _(act):
                        for k in range(KD):
                            act.wait_ge(sem["x_turned"], k + 1)
                            nc.scalar.copy(part[:, k, :], ps_x[k][:]).then_inc(sem["part_ready"], 1)
                        act.wait_ge(sem["shifted"], 1)
                        nc.scalar.activation(prob[:], logit[:], ACT.Exp).then_inc(sem["exp_done"], 1)
                        if not gated:
                            act.wait_ge(sem["w_turned"], 1)
                            nc.scalar.copy(wT[:], ps_w[:]).then_inc(sem["wT_ready"], 1)

                    @block.vector
                    def _(dve):
                        link = chain(dve, sem["link"])
                        ln.statistics(nc, link, parts)
                        ln.apply(nc, dve, parts)
                        shape = [P, CHUNK, EXPERTS]
                        dve.wait_ge(sem["logits_done"], 1)
                        lg = ps_g[:].rearrange("p (t e) -> p t e", e=EXPERTS)
                        link(nc.vector.tensor_reduce(peak[:], lg, AX_X, ALU.max))
                        nc.vector.tensor_tensor(logit[:], lg, spread(peak[:], 2, shape), ALU.subtract).then_inc(sem["shifted"], 1)
                        dve.wait_ge(sem["exp_done"], 1)
                        link(nc.vector.tensor_reduce(total[:], prob[:], AX_X, ALU.add))
                        link(nc.vector.reciprocal(inv[:], total[:]))
                        link(nc.vector.tensor_tensor(prob[:], prob[:], spread(inv[:], 2, shape), ALU.mult))
                        for t in range(CHUNK):
                            ins = nc.vector.max(top[:, t, :], prob[:, t, :])
                        link(ins)
                        for t in range(CHUNK):
                            ins = nc.vector.max_index(index[:, t, :], top[:, t, :], prob[:, t, :])
                        link(ins)
                        link(nc.vector.tensor_copy(index_f[:], index[:]))
                        every = iota[:].unsqueeze(1).to_broadcast(shape)
                        nc.vector.tensor_tensor(chosen[:], every, index_f[:, :, 0:1].to_broadcast(shape), ALU.is_equal)
                        link(nc.vector.tensor_tensor(hot[:], every, index_f[:, :, 1:2].to_broadcast(shape), ALU.is_equal))
                        link(nc.vector.tensor_tensor(chosen[:], chosen[:], hot[:], ALU.add))
                        link(nc.vector.tensor_tensor(chosen[:], chosen[:], prob[:], ALU.mult))
                        link(nc.vector.tensor_reduce(total[:], chosen[:], AX_X, ALU.add))
                        if not gated:
                            link(nc.vector.tensor_scalar(total[:], total[:], 1e-12, None, ALU.max))
                        link(nc.vector.reciprocal(inv[:], total[:]))
                        nc.vector.tensor_tensor(gates[:], chosen[:], spread(inv[:], 2, shape), ALU.mult).then_inc(sem["gates_ready"], 1)
                        dve.wait_ge(sem["gates_ready"], 1)
                        link(nc.vector.tensor_copy(w_all[:, bass.ds(c * CHUNK, CHUNK), :], gates[:]))
                        if not gated:
                            for t in range(CHUNK):
                                dve.wait_ge(sem["bias_done"], t + 1)
                                nc.vector.tensor_tensor(x[:, c * CHUNK + t, :], x[:, c * CHUNK + t, :], ps_y[t][:],
                                                        ALU.add).then_inc(sem["x_ready"], 1)
                g.again()

        PAIR = 2
        STEPS = PAIR * CHUNKS
        raw = s.sb("weights_raw", [P, size])
        wH = [s.sb(f"weights_high{i}", [P, size], F32R) for i in range(PAIR)]
        wL = [s.sb(f"weights_low{i}", [P, size], F32R) for i in range(PAIR)]
        b1 = [s.sb(f"bias1_{i}", [P, FT]) for i in range(PAIR)] if not gated else None
        wcur = s.sb("gates_now", [P, TILES, PAIR])
        full = s.sb("hidden_full", [P, 2, TOK])
        hH, hL = (s.sb(n, [P, 2, FT, TOK], F32R) for n in ("hidden_high", "hidden_low"))
        silu = s.sb("silu", [P, 2, TOK]) if gated else None
        slots = 2 if gated else 4
        psU = [[s.ps(f"up{i}_{u}", [P, BANK]) for u in range(ups)] for i in range(slots)]
        psD = [s.ps(f"down{i}", [P, DIM]) for i in range(4)]
        landed, high_done, split_done = s.sem("landed"), s.sem("high_done"), s.sem("split_done")
        gates_now, up_done, silu_done = s.sem("gates_now"), s.sem("up_done"), s.sem("silu_done")
        full_ready, high_ready, hidden_ready = s.sem("full_ready"), s.sem("high_ready"), s.sem("hidden_ready")
        down_done, added = s.sem("down_done"), s.sem("added")
        b1_of = slice(b1_at, b1_at + FT)

        def split_weights(pool, to, times):
            nc.gpsimd.tensor_copy(wH[to][:], raw[:]).then_inc(high_done, 1)
            if not gated:
                nc.gpsimd.tensor_copy(b1[to][:], raw[:, b1_of])
            pool.wait_ge(high_done, times)
            nc.gpsimd.tensor_tensor(wL[to][:], raw[:], wH[to][:].bitcast(F32), ALU.subtract).then_inc(split_done, 1)

        with nc.Block() as block:
            @block.sync
            def _(sp):
                sp.dma_start(raw[:], D[f"L{layer}_experts"][0]).then_inc(landed, 16)

            @block.gpsimd
            def _(pool):
                pool.wait_ge(landed, 16)
                split_weights(pool, 0, 1)
        s.again()
        with nc.Fori(0, EXPERTS // PAIR) as pair:
            with nc.Block() as block:
                @block.sync
                def _(sp):
                    sp.dma_start(raw[:], D[f"L{layer}_experts"][pair * PAIR + 1]).then_inc(landed, 16)
                    sp.wait_ge(split_done, 1)
                    sp.dma_start(raw[:], D[f"L{layer}_experts"][pair * PAIR + 2]).then_inc(landed, 16)

                @block.gpsimd
                def _(pool):
                    pool.wait_ge(landed, 16)
                    split_weights(pool, 1, 1)
                    pool.wait_ge(landed, 32)
                    pool.wait_ge(down_done, CHUNKS * CHUNK)
                    split_weights(pool, 0, 2)

                @block.tensor
                def _(pe):
                    def up(step):
                        e, c = divmod(step, CHUNKS)
                        if step == CHUNKS:
                            pe.wait_ge(split_done, 1)
                        for f in range(FT):
                            n = step * FT + f
                            if n >= slots:
                                pe.wait_ge(full_ready, n - slots + 1)
                            for u in range(ups):
                                for k in range(KD):
                                    at = up_at[u] + k * HID + f * P
                                    tok = slice(c * TOK, (c + 1) * TOK)
                                    for i, (a, m) in enumerate(((wH, xH), (wH, xL), (wL, xH))):
                                        ins = nc.tensor.matmul(psU[n % slots][u][:], a[e][:, at:at + P], m[:, k, tok],
                                                               start=(k == 0 and i == 0), stop=(k == KD - 1 and i == 2))
                            ins.then_inc(up_done, 1)

                    def down(step):
                        e, c = divmod(step, CHUNKS)
                        pe.wait_ge(hidden_ready, (step + 1) * FT)
                        for t in range(CHUNK):
                            n = step * CHUNK + t
                            if n >= len(psD):
                                pe.wait_ge(added, n - len(psD) + 1)
                            for f in range(FT):
                                at = down_at + f * DIM
                                for i, (h, m) in enumerate(((hH, wH), (hH, wL), (hL, wH))):
                                    ins = nc.tensor.matmul(psD[n % len(psD)][:], h[:, step % 2, f, t * P:(t + 1) * P],
                                                           m[e][:, at:at + DIM], start=(f == 0 and i == 0),
                                                           stop=(f == FT - 1 and i == 2))
                            ins.then_inc(down_done, 1)

                    for step in range(STEPS + 1):
                        if step < STEPS:
                            up(step)
                        if step:
                            down(step - 1)

                @block.scalar
                def _(act):
                    def high(n):
                        step, f = divmod(n, FT)
                        if step >= 2:
                            act.wait_ge(down_done, (step - 1) * CHUNK)
                        act.wait_ge(full_ready, n + 1)
                        nc.scalar.copy(hH[:, step % 2, f, :], full[:, n % 2, :]).then_inc(high_ready, 1)

                    for n in range(STEPS * FT + 1):
                        if n < STEPS * FT:
                            act.wait_ge(up_done, n + 1)
                            if gated:
                                if n >= 2:
                                    act.wait_ge(full_ready, n - 1)
                                nc.scalar.activation(silu[:, n % 2, :], psU[n % slots][0][:],
                                                     ACT.Silu).then_inc(silu_done, 1)
                            else:
                                if n >= 2:
                                    act.wait_ge(hidden_ready, n - 1)
                                nc.scalar.activation(full[:, n % 2, :], psU[n % slots][0][:], ACT.Relu,
                                                     bias=b1[n // FT // CHUNKS][:, n % FT:n % FT + 1]).then_inc(full_ready, 1)
                        if n:
                            high(n - 1)

                @block.vector
                def _(dve):
                    nc.vector.tensor_copy(wcur[:], w_all[:, :, bass.ds(pair * PAIR, PAIR)]).then_inc(gates_now, 1)
                    dve.wait_ge(gates_now, 1)

                    def product(n):
                        dve.wait_ge(silu_done, n + 1)
                        if n >= 2:
                            dve.wait_ge(hidden_ready, n - 1)
                        nc.vector.tensor_tensor(full[:, n % 2, :], psU[n % slots][1][:], silu[:, n % 2, :],
                                                ALU.mult).then_inc(full_ready, 1)

                    def low(n):
                        step, f = divmod(n, FT)
                        dve.wait_ge(high_ready, n + 1)
                        nc.vector.tensor_tensor(hL[:, step % 2, f, :], full[:, n % 2, :],
                                                hH[:, step % 2, f, :].bitcast(F32), ALU.subtract).then_inc(hidden_ready, 1)

                    def add(n):
                        step, t = divmod(n, CHUNK)
                        e, c = divmod(step, CHUNKS)
                        dve.wait_ge(down_done, n + 1)
                        if n >= CHUNKS * CHUNK:
                            dve.wait_ge(added, n - CHUNKS * CHUNK + 1)
                        tile = c * CHUNK + t
                        nc.vector.scalar_tensor_tensor(x[:, tile, :], psD[n % len(psD)][:], wcur[:, tile, e:e + 1],
                                                       x[:, tile, :], ALU.mult, ALU.add).then_inc(added, 1)

                    for step in range(STEPS + 1):
                        if step < STEPS:
                            for f in range(FT):
                                n = step * FT + f
                                if gated:
                                    product(n)
                                    if n:
                                        low(n - 1)
                                else:
                                    low(n)
                        if gated and step == STEPS:
                            low(STEPS * FT - 1)
                        if step:
                            for t in range(CHUNK):
                                add((step - 1) * CHUNK + t)
            s.again()


def quantised_ffn(nc, x, C, D):
    INNER = 1024
    KI = INNER // P
    T = 4
    HALF = INNER // BANK
    with ExitStack() as ctx:
        s = Stage(nc, ctx, "f1")
        wg, wu, wd = s.sb("wg", [P, KD * INNER], BF16), s.sb("wu", [P, KD * INNER], BF16), s.sb("wd", [P, KI * DIM], BF16)
        mean, inv_mean = s.sb("mean", [P, 3]), s.sb("inv_mean", [P, 3])
        with ExitStack() as setup:
            g = Stage(nc, setup, "q1")
            raws = [g.sb(f"raw{i}", [P, KD * INNER]) for i in range(3)]
            sums, ones = g.sb("sums", [P, 3]), g.sb("ones", [P, P])
            ps_sum = g.ps("sum", [P, 3])
            link_sem, sums_ready, sum_done = g.sem("link"), g.sem("sums_ready"), g.sem("sum_done")
            load_block(nc, g, [(raws[i][:], D[f"L1_w_{n}"]) for i, n in enumerate(("gate", "up", "down"))])
            with nc.Block() as block:
                @block.tensor
                def _(pe):
                    pe.wait_ge(sums_ready, 1)
                    nc.tensor.matmul(ps_sum[:], ones[:], sums[:], start=True, stop=True).then_inc(sum_done, 1)

                @block.vector
                def _(dve):
                    link = chain(dve, link_sem)
                    nc.vector.memset(ones[:], 1.0)
                    for i in range(3):
                        ins = nc.vector.tensor_reduce(sums[:, i:i + 1], raws[i][:], AX_X, ALU.add,
                                                      apply_absolute_value=True)
                    ins.then_inc(sums_ready, 1)
                    dve.wait_ge(sum_done, 1)
                    link(nc.vector.tensor_scalar(mean[:], ps_sum[:], 1.0 / (INNER * DIM), QUANT_MIN, ALU.mult, ALU.max))
                    link(nc.vector.reciprocal(inv_mean[:], mean[:]))
                    for i, w in enumerate((wg, wu, wd)):
                        r = raws[i]
                        link(nc.vector.tensor_scalar(r[:], r[:], inv_mean[:, i:i + 1], 1.0, ALU.mult, ALU.min))
                        link(nc.vector.tensor_scalar(r[:], r[:], -1.0, ROUND, ALU.max, ALU.add))
                        link(nc.vector.tensor_scalar(w[:], r[:], -ROUND, None, ALU.add))
            g.again()
        ln = LayerNorm(s, T)
        psT = [s.ps(f"turned{i}", [P, 2 * BANK], BF16) for i in range(2)]
        psG = [s.ps(f"gate{i}", [P, BANK]) for i in range(2)]
        psU = [s.ps(f"up{i}", [P, BANK]) for i in range(2)]
        psD = [s.ps(f"down{i}", [P, DIM]) for i in range(2)]
        peak, speed = s.sb("peak", [P, T]), s.sb("quant_scale", [P, T])
        gs, us = s.sb("gate_scale", [P, T]), s.sb("up_scale", [P, T])
        v = s.sb("rounding", [P, T, DIM])
        xq, xqT = s.sb("xq", [P, T, DIM], BF16), s.sb("xqT", [P, KD, T * P], BF16)
        sg = s.sb("silu", [P, 2, BANK])
        h = s.sb("h", [P, 2, INNER])
        hpeak, hspeed, hs = s.sb("h_peak", [P, T]), s.sb("h_quant_scale", [P, T]), s.sb("down_scale", [P, T])
        hq, hqT = s.sb("hq", [P, 2, INNER], BF16), s.sb("hqT", [P, 2, KI, P], BF16)
        sem = {n: s.sem(n) for n in ("link", "xq_ready", "x_turned", "xqT_ready", "up_done", "silu_done", "h_ready",
                                     "h_rounded", "hq_ready", "h_turned", "hqT_ready", "down_done", "x_ready")}
        with nc.Fori(0, TILES // T) as c:
            with nc.Block() as block:
                def parts(t):
                    return [x[:, c * T + t, :]]

                @block.gpsimd
                def _(pool):
                    ln.root(nc, pool, C["minus_half"])

                @block.tensor
                def _(pe):
                    pe.wait_ge(sem["xq_ready"], 1)
                    for k in range(KD):
                        for t in range(T):
                            at = (k * T + t) * P
                            ins = nc.tensor.transpose(psT[0][:, at:at + P], xq[:, t, k * P:(k + 1) * P], C["ident_bf"][:])
                    ins.then_inc(sem["x_turned"], 1)
                    pe.wait_ge(sem["xqT_ready"], 1)

                    def gate_up(t):
                        for n in range(HALF):
                            u = t * HALF + n
                            if u >= 2:
                                pe.wait_ge(sem["h_ready"], u - 1)
                            for w, ps in ((wg, psG), (wu, psU)):
                                for k in range(KD):
                                    at = k * INNER + n * BANK
                                    ins = nc.tensor.matmul(ps[u % 2][:], xqT[:, k, t * P:(t + 1) * P],
                                                           w[:, at:at + BANK], start=(k == 0), stop=(k == KD - 1))
                            ins.then_inc(sem["up_done"], 1)

                    def down(t):
                        pe.wait_ge(sem["hq_ready"], t + 1)
                        if t >= 1:
                            pe.wait_ge(sem["hqT_ready"], t)
                        for k in range(KI):
                            ins = nc.tensor.transpose(psT[1][:, k * P:(k + 1) * P], hq[:, t % 2, k * P:(k + 1) * P],
                                                      C["ident_bf"][:])
                        ins.then_inc(sem["h_turned"], 1)
                        pe.wait_ge(sem["hqT_ready"], t + 1)
                        if t >= 2:
                            pe.wait_ge(sem["x_ready"], t - 1)
                        for k in range(KI):
                            ins = nc.tensor.matmul(psD[t % 2][:], hqT[:, t % 2, k, :], wd[:, k * DIM:(k + 1) * DIM],
                                                   start=(k == 0), stop=(k == KI - 1))
                        ins.then_inc(sem["down_done"], 1)

                    for t in range(T + 1):
                        if t < T:
                            gate_up(t)
                        if t:
                            down(t - 1)

                @block.scalar
                def _(act):
                    act.wait_ge(sem["x_turned"], 1)
                    nc.scalar.copy(xqT[:], psT[0][:].rearrange("p (k t) -> p k t", k=KD)).then_inc(sem["xqT_ready"], 1)
                    for t in range(T + 1):
                        if t < T:
                            for n in range(HALF):
                                u = t * HALF + n
                                act.wait_ge(sem["up_done"], u + 1)
                                if u >= 2:
                                    act.wait_ge(sem["h_ready"], u - 1)
                                nc.scalar.activation(sg[:, u % 2, :], psG[u % 2][:], ACT.Silu,
                                                     scale=gs[:, t:t + 1]).then_inc(sem["silu_done"], 1)
                        if t:
                            act.wait_ge(sem["h_turned"], t)
                            if t >= 3:
                                act.wait_ge(sem["down_done"], t - 2)
                            nc.scalar.copy(hqT[:, (t - 1) % 2, :, :],
                                           psT[1][:].rearrange("p (k t) -> p k t", k=KI)).then_inc(sem["hqT_ready"], 1)

                @block.vector
                def _(dve):
                    link = chain(dve, sem["link"])
                    ln.statistics(nc, link, parts)
                    ln.apply(nc, dve, parts)
                    dve.wait_ge(ln.xn_ready, 1)
                    link(nc.vector.tensor_reduce(peak[:], ln.xn[:], AX_X, ALU.max, apply_absolute_value=True))
                    link(nc.vector.tensor_scalar(peak[:], peak[:], QUANT_MIN, None, ALU.max))
                    link(nc.vector.reciprocal(speed[:], peak[:]))
                    nc.vector.tensor_scalar(gs[:], peak[:], mean[:, 0:1], 1.0 / 127.0, ALU.mult, ALU.mult)
                    nc.vector.tensor_scalar(us[:], peak[:], mean[:, 1:2], 1.0 / 127.0, ALU.mult, ALU.mult)
                    link(nc.vector.tensor_scalar(speed[:], speed[:], 127.0, None, ALU.mult))
                    for t in range(T):
                        ins = nc.vector.tensor_scalar(v[:, t, :], ln.xn[:, t, :], speed[:, t:t + 1], 127.0, ALU.mult, ALU.min)
                    link(ins)
                    link(nc.vector.tensor_scalar(v[:], v[:], -128.0, ROUND, ALU.max, ALU.add))
                    nc.vector.tensor_scalar(xq[:], v[:], -ROUND, None, ALU.add).then_inc(sem["xq_ready"], 1)

                    def product(t):
                        for n in range(HALF):
                            u = t * HALF + n
                            dve.wait_ge(sem["silu_done"], u + 1)
                            nc.vector.scalar_tensor_tensor(h[:, t % 2, n * BANK:(n + 1) * BANK], psU[u % 2][:],
                                                           us[:, t:t + 1], sg[:, u % 2, :], ALU.mult,
                                                           ALU.mult).then_inc(sem["h_ready"], 1)

                    def quantise(t):
                        hh, at = h[:, t % 2, :], slice(t, t + 1)
                        dve.wait_ge(sem["h_ready"], (t + 1) * HALF)
                        link(nc.vector.tensor_reduce(hpeak[:, at], hh, AX_X, ALU.max, apply_absolute_value=True))
                        link(nc.vector.tensor_scalar(hpeak[:, at], hpeak[:, at], QUANT_MIN, None, ALU.max))
                        link(nc.vector.reciprocal(hspeed[:, at], hpeak[:, at]))
                        nc.vector.tensor_scalar(hs[:, at], hpeak[:, at], mean[:, 2:3], 1.0 / 127.0, ALU.mult, ALU.mult)
                        link(nc.vector.tensor_scalar(hspeed[:, at], hspeed[:, at], 127.0, None, ALU.mult))
                        link(nc.vector.tensor_scalar(hh, hh, hspeed[:, at], 127.0, ALU.mult, ALU.min))
                        link(nc.vector.tensor_scalar(hh, hh, -128.0, ROUND, ALU.max, ALU.add))
                        if t >= 2:
                            dve.wait_ge(sem["h_turned"], t - 1)
                        nc.vector.tensor_scalar(hq[:, t % 2, :], hh, -ROUND, None, ALU.add).then_inc(sem["hq_ready"], 1)

                    def add(t):
                        dve.wait_ge(sem["down_done"], t + 1)
                        nc.vector.scalar_tensor_tensor(x[:, c * T + t, :], psD[t % 2][:], hs[:, t:t + 1],
                                                       x[:, c * T + t, :], ALU.mult, ALU.add).then_inc(sem["x_ready"], 1)

                    for t in range(T + 1):
                        if t < T:
                            product(t)
                            if t >= 2:
                                dve.wait_ge(sem["hq_ready"], t - 1)
                            quantise(t)
                        if t:
                            add(t - 1)
            s.again()


def shift_rows(nc, s, y, shifted, sem):
    with nc.Block() as block:
        @block.sync
        def _(sp):
            sp.dma_start(shifted[1:P, :, :], y[0:P - 1, :, P:DIM]).then_inc(sem, 16)
            sp.dma_start(shifted[0:1, 1:TILES:2, :], y[P - 1:P, 0:TILES:2, P:DIM]).then_inc(sem, 16)
            sp.wait_ge(sem, 32)
    s.again()


def local_attention_block(nc, x, C, D):
    DEPTH, H, HD, HID = 2, 8, 64, 682
    INNER = H * HD
    with ExitStack() as ctx:
        s = Stage(nc, ctx, "f2")
        y, shifted = s.sb("y", [P, TILES, DIM]), s.sb("shifted", [P, TILES, P])
        set_done, shift_landed = s.sem("set_done"), s.sem("shift_landed")
        T = 4
        with nc.Block() as block:
            @block.vector
            def _(dve):
                nc.vector.memset(shifted[:], 0.0).then_inc(set_done, 1)
                dve.wait_ge(set_done, 1)
        s.again()
        with ExitStack() as front:
            g = Stage(nc, front, "n2")
            ln = LayerNorm(g, T)
            link_sem, copied = g.sem("link"), g.sem("copied")
            with nc.Fori(0, TILES // T) as c:
                with nc.Block() as block:
                    def parts(t):
                        return [x[:, c * T + t, :]]

                    @block.gpsimd
                    def _(pool):
                        ln.root(nc, pool, C["minus_half"])

                    @block.scalar
                    def _(act):
                        act.wait_ge(ln.xn_ready, 1)
                        nc.scalar.copy(y[:, bass.ds(c * T, T), :], ln.xn[:]).then_inc(copied, 1)

                    @block.vector
                    def _(dve):
                        link = chain(dve, link_sem)
                        ln.statistics(nc, link, parts)
                        ln.apply(nc, dve, parts)
                g.again()
        with nc.Fori(0, DEPTH) as layer:
            shift_rows(nc, s, y, shifted, shift_landed)
            local_attention(nc, C, D, y, shifted, layer, H, HD)
            shift_rows(nc, s, y, shifted, shift_landed)
            gelu_ffn(nc, C, D, y, shifted, layer, HID)
        with nc.Block() as block:
            @block.vector
            def _(dve):
                nc.vector.tensor_tensor(x[:], x[:], y[:], ALU.add).then_inc(set_done, 1)
                dve.wait_ge(set_done, 1)
        s.again()


def local_attention(nc, C, D, y, shifted, layer, H, HD):
    INNER = H * HD
    KI = INNER // P
    with ExitStack() as ctx:
        s = Stage(nc, ctx, "a2")
        wqkv, wo = s.sb("wqkv", [P, KD, 3 * INNER]), s.sb("wo", [P, KI, DIM])
        scale = s.sb("scale", [P, 4, HD])
        tables = s.sb("tables", [P, 2, 2, 2, HD])
        psA = [s.ps(f"work{i}", [P, BANK]) for i in range(2)]
        att = Attention(s, H, HD, "halves")
        link0 = s.sem("tables_link")
        load_block(nc, s, [(wqkv[:], D["L2_wqkv"][layer]), (wo[:], D["L2_wo"][layer]),
                           (scale[:], D["L2_qk_scale"][layer].partition_broadcast(P))])
        with nc.Block() as block:
            @block.vector
            def _(dve):
                link = chain(dve, link0)
                for w, which in enumerate(("q", "k")):
                    for f, fn in enumerate(("cos", "sin")):
                        ins = nc.vector.tensor_tensor(tables[:, w, f], C[f"xpos_{fn}_{which}"][:],
                                                      spread(scale[:, 2 * w + f, :], 1, [P, 2, HD]), ALU.mult)
                link(ins)
                att.clear(nc)
                link(nc.vector.memset(att.rsum[:], 0.0))
        s.again()
        h = s.sb("h", [P, 2, DIM])
        hT = s.sb("hT", [P, KD, SEQ])
        raw = s.sb("raw", [P, 2, 2, INNER])
        vr = s.sb("v_raw", [P, 2, INNER])
        sq = s.sb("squares", [P, 2, INNER])
        ss, rn = s.sb("sum_squares", [P, 2, 2 * H]), s.sb("inv_norm", [P, 2, 2 * H])
        rot = s.sb("rotated", [P, 2, H, HD])
        oT = s.sb("oT", [P, KI, SEQ])
        sem = {n: s.sem(n) for n in ("link", "h_ready", "h_turned", "qkv_done", "by_act", "by_dve", "squared",
                                     "ss_ready", "bounded", "rn_ready", "o_turned", "out_done")}
        A, V = sem["by_act"], sem["by_dve"]
        QKV = 6
        turn_o = KI * SEQ // BANK
        STEPS = H + 3

        def turn(front, core, tail):
            turned_h = 1 if front is not None else 0
            turned_o = turn_o if tail is not None else 0
            made = QKV if front is not None else 0
            readers = [A] * (turned_h + turned_o + made) + [V, V]
            USE_O, USE_QKV, USE_OUT = turned_h, turned_h + turned_o, turned_h + turned_o + made
            with nc.Block() as block:
                @block.gpsimd
                def _(pool):
                    if front is None:
                        return
                    nc.gpsimd.tensor_copy(h[:, :, 0:P], y[:, bass.ds(front, 2), 0:P])
                    nc.gpsimd.tensor_copy(h[:, :, P:DIM], shifted[:, bass.ds(front, 2), :]).then_inc(sem["h_ready"], 1)
                    for w in range(2):
                        pool.wait_ge(sem["ss_ready"], w + 1)
                        nc.gpsimd.tensor_scalar(ss[:, w, :], ss[:, w, :], TINY_SQ, None, ALU.max).then_inc(sem["bounded"], 1)
                        pool.wait_ge(sem["bounded"], w + 1)
                        nc.gpsimd.tensor_tensor(rn[:, w, :], ss[:, w, :], C["minus_half"][:, 0:2 * H],
                                                ALU.pow).then_inc(sem["rn_ready"], 1)

                @block.tensor
                def _(pe):
                    ring = Ring(psA, readers)

                    def beside(step):
                        if step == -1 and front is not None:
                            pe.wait_ge(sem["h_ready"], 1)
                            turn_rows(nc, ring.claim(pe), h, C["ident"], 2, DIM).then_inc(sem["h_turned"], 1)
                        if step == -1 and tail is not None:
                            for n in range(turn_o):
                                bank = ring.claim(pe)
                                for i in range(2):
                                    k = n * 2 + i
                                    for t in range(2):
                                        at = (i * 2 + t) * P
                                        src = att.o_rows[:, t, 2 * k:2 * k + 2, :].rearrange("p h d -> p (h d)")
                                        ins = nc.tensor.transpose(bank[:, at:at + P], src, C["ident"][:])
                                ins.then_inc(sem["o_turned"], 1)
                        if step < QKV and step >= 0 and front is not None:
                            if step == 0:
                                pe.wait_ge(A, 1)
                            part, t = (1, 0, 2)[step // 2], step % 2
                            bank = ring.claim(pe)
                            for k in range(KD):
                                ins = nc.tensor.matmul(bank[:], hT[:, k, t * P:(t + 1) * P],
                                                       wqkv[:, k, part * INNER:(part + 1) * INNER],
                                                       start=(k == 0), stop=(k == KD - 1))
                            ins.then_inc(sem["qkv_done"], 1)
                        if step in (QKV, QKV + 1) and tail is not None:
                            t = step - QKV
                            if t == 0:
                                pe.wait_ge(A, turned_h + turned_o)
                            bank = ring.claim(pe)
                            for k in range(KI):
                                ins = nc.tensor.matmul(bank[:, 0:DIM], oT[:, k, t * P:(t + 1) * P], wo[:, k, :],
                                                       start=(k == 0), stop=(k == KI - 1))
                            ins.then_inc(sem["out_done"], 1)

                    if core is None:
                        for step in range(-1, STEPS):
                            beside(step)
                    else:
                        att.tensor(nc, pe, C, lambda h: C["local"][:], beside)

                @block.scalar
                def _(act):
                    ring = Ring(psA, readers)

                    def beside(step):
                        if step == -1 and front is not None:
                            act.wait_ge(sem["h_turned"], 1)
                            nc.scalar.copy(hT[:], ring.bank(0)[:].rearrange("p (k t) -> p k t", k=KD)).then_inc(A, 1)
                        if step == -1 and tail is not None:
                            for n in range(turn_o):
                                act.wait_ge(sem["o_turned"], n + 1)
                                nc.scalar.copy(oT[:, 2 * n:2 * n + 2, :],
                                               ring.bank(USE_O + n)[:].rearrange("p (k t) -> p k t", k=2)).then_inc(A, 1)
                        if 0 <= step < 4 and front is not None:
                            w, t = step // 2, step % 2
                            act.wait_ge(sem["qkv_done"], step + 1)
                            nc.scalar.copy(raw[:, w, t, :], ring.bank(USE_QKV + step)[:]).then_inc(A, 1)
                            act.wait_ge(A, USE_QKV + step + 1)
                            if step == 2:
                                act.wait_ge(sem["ss_ready"], 1)
                            nc.scalar.activation(sq[:, t, :], raw[:, w, t, :], ACT.Square).then_inc(sem["squared"], 1)
                        if 4 <= step < QKV and front is not None:
                            act.wait_ge(sem["qkv_done"], step + 1)
                            if core is not None and step == 4:
                                act.wait_ge(att.v_ready, 1)
                            nc.scalar.copy(vr[:, step - 4, :], ring.bank(USE_QKV + step)[:]).then_inc(A, 1)

                    if core is None:
                        for step in range(-1, STEPS):
                            beside(step)
                    else:
                        nc.scalar.copy(att.v_rows[:, :, :, 0:HD],
                                       vr[:].rearrange("p t (h d) -> p t h d", h=H)).then_inc(att.v_ready, 1)
                        att.scalar(nc, act, beside)

                @block.vector
                def _(dve):
                    ring = Ring(psA, readers)
                    link = chain(dve, sem["link"])

                    def sum_squares(w):
                        dve.wait_ge(sem["squared"], 2 * w + 2)
                        nc.vector.tensor_reduce(ss[:, w, :], sq[:].rearrange("p t (h d) -> p (t h) d", h=H), AX_X,
                                                ALU.add).then_inc(sem["ss_ready"], 1)

                    def normalise(w):
                        dve.wait_ge(sem["rn_ready"], w + 1)
                        rows = raw[:, w].rearrange("p t (h d) -> p (t h) d", h=H)
                        link(nc.vector.tensor_tensor(rows, rows, spread(rn[:, w, :], 2, [P, 2 * H, HD]), ALU.mult))

                    def by_position(w, to, t):
                        r = raw[:, w, t, :].rearrange("p (h d) -> p h d", h=H)
                        cos, sin = tables[:, 1 - w, 0, t, :], tables[:, 1 - w, 1, t, :]
                        half = HD // 2
                        nc.vector.tensor_tensor(rot[:, t, :, 0:half], r[:, :, half:HD],
                                                spread(sin[:, 0:half], 1, [P, H, half]), ALU.mult)
                        nc.vector.tensor_tensor(rot[:, t, :, half:HD], r[:, :, 0:half],
                                                spread(sin[:, half:HD], 1, [P, H, half]), ALU.mult)
                        link(nc.vector.tensor_tensor(to[:, t, :, 0:HD], r, spread(cos, 1, [P, H, HD]), ALU.mult))
                        link(nc.vector.tensor_tensor(to[:, t, :, 0:HD], to[:, t, :, 0:HD], rot[:, t], ALU.add))

                    def beside(step):
                        if step == 0 and tail is not None:
                            dve.wait_ge(sem["o_turned"], turn_o)
                        if step in (8, 9) and tail is not None:
                            t = step - 8
                            dve.wait_ge(sem["out_done"], t + 1)
                            nc.vector.tensor_tensor(y[:, tail + t, :], y[:, tail + t, :],
                                                    ring.bank(USE_OUT + t)[:, 0:DIM], ALU.add).then_inc(V, 1)
                        if front is None:
                            return
                        if step == 2:
                            sum_squares(0)
                        if step == 4:
                            sum_squares(1)
                            normalise(0)
                        if step in (4, 5):
                            if core is not None:
                                dve.wait_ge(att.rows_turned, 2 * att.banks)
                            by_position(0, att.k_rows, step - 4)
                        if step == 6:
                            normalise(1)
                        if step in (6, 7):
                            by_position(1, att.q_rows, step - 6)

                    if core is None:
                        for step in range(-1, STEPS):
                            beside(step)
                    else:
                        att.vector(nc, dve, link, beside)
            s.again()

        turn(0, None, None)
        turn(2, 0, None)
        with nc.Fori(0, BATCH - 2) as b:
            turn(b * 2 + 4, b * 2 + 2, b * 2)
        turn(None, 2 * (BATCH - 1), 2 * (BATCH - 2))
        turn(None, None, 2 * (BATCH - 1))


def gelu_ffn(nc, C, D, y, shifted, layer, HID):
    FT = -(-HID // P)
    rows = [min(P, HID - f * P) for f in range(FT)]
    T = 4
    TOK = T * P
    with ExitStack() as ctx:
        s = Stage(nc, ctx, "g2")
        w1, w2 = s.sb("w1", [P, KD, 2 * HID]), s.sb("w2", [P, FT, DIM])
        b1, b2 = s.sb("b1", [P, 2, FT]), s.sb("b2", [P, DIM])
        gain, bias = s.sb("ln_gain", [P, KD]), s.sb("ln_bias", [P, KD])
        load_block(nc, s, [(w1[:], D["L2_w1"][layer]), (w2[:], D["L2_w2"][layer]), (b1[:], D["L2_b1"][layer]),
                           (b2[:], D["L2_b2"][layer].partition_broadcast(P)), (gain[:], D["L2_ln_g"][layer]),
                           (bias[:], D["L2_ln_b"][layer])])
        s.again()
        ln = LayerNorm(s, T, 2)
        ps_x = [s.ps(f"turned{k}", [P, BANK]) for k in range(KD)]
        psU = [[s.ps(f"up{i}_{u}", [P, BANK]) for u in range(2)] for i in range(2)]
        psD = [s.ps(f"down{i}", [P, DIM]) for i in range(2)]
        hT = s.sb("hT", [P, KD, TOK])
        gelu = s.sb("gelu", [P, 2, TOK])
        hidden = s.sb("hidden", [P, FT, TOK])
        sem = {n: s.sem(n) for n in ("link", "x_turned", "hT_ready", "up_done", "gelu_done", "hidden_ready",
                                     "down_done", "bias_added", "y_ready")}
        with nc.Fori(0, TILES // T) as c:
            with nc.Block() as block:
                def parts(t):
                    return [y[:, c * T + t, 0:P], shifted[:, c * T + t, :]]

                @block.gpsimd
                def _(pool):
                    ln.root(nc, pool, C["minus_half"])
                    pool.wait_ge(ln.xn_ready, 1)
                    for t in range(T):
                        ins = nc.gpsimd.tensor_tensor(y[:, c * T + t, :], y[:, c * T + t, :], b2[:], ALU.add)
                    ins.then_inc(sem["bias_added"], 1)

                @block.tensor
                def _(pe):
                    pe.wait_ge(ln.xn_ready, 1)
                    for k in range(KD):
                        for t in range(T):
                            ins = nc.tensor.transpose(ps_x[k][:, t * P:(t + 1) * P], ln.xn[:, t, k * P:(k + 1) * P],
                                                      C["ident"][:])
                        ins.then_inc(sem["x_turned"], 1)
                    pe.wait_ge(sem["hT_ready"], KD)
                    for f in range(FT):
                        if f >= 2:
                            pe.wait_ge(sem["hidden_ready"], f - 1)
                        for u in (1, 0):
                            for k in range(KD):
                                at = u * HID + f * P
                                ins = nc.tensor.matmul(psU[f % 2][u][0:rows[f], :], w1[:, k, at:at + rows[f]], hT[:, k, :],
                                                       start=(k == 0), stop=(k == KD - 1))
                        ins.then_inc(sem["up_done"], 1)
                    pe.wait_ge(sem["hidden_ready"], FT)
                    for t in range(T):
                        if t >= 2:
                            pe.wait_ge(sem["y_ready"], t - 1)
                        for f in range(FT):
                            ins = nc.tensor.matmul(psD[t % 2][:], hidden[0:rows[f], f, t * P:(t + 1) * P],
                                                   w2[0:rows[f], f, :], start=(f == 0), stop=(f == FT - 1))
                        ins.then_inc(sem["down_done"], 1)

                @block.scalar
                def _(act):
                    for k in range(KD):
                        act.wait_ge(sem["x_turned"], k + 1)
                        nc.scalar.activation(hT[:, k, :], ps_x[k][:], ACT.Identity, bias=bias[:, k:k + 1],
                                             scale=gain[:, k:k + 1]).then_inc(sem["hT_ready"], 1)
                    for f in range(FT):
                        act.wait_ge(sem["up_done"], f + 1)
                        if f >= 2:
                            act.wait_ge(sem["hidden_ready"], f - 1)
                        nc.scalar.activation(gelu[0:rows[f], f % 2, :], psU[f % 2][1][0:rows[f], :], ACT.Gelu,
                                             bias=b1[0:rows[f], 1, f:f + 1]).then_inc(sem["gelu_done"], 1)

                @block.vector
                def _(dve):
                    link = chain(dve, sem["link"])
                    ln.statistics(nc, link, parts)
                    ln.apply(nc, dve, parts)
                    for f in range(FT):
                        dve.wait_ge(sem["gelu_done"], f + 1)
                        nc.vector.scalar_tensor_tensor(hidden[0:rows[f], f, :], psU[f % 2][0][0:rows[f], :],
                                                       b1[0:rows[f], 0, f:f + 1], gelu[0:rows[f], f % 2, :], ALU.add,
                                                       ALU.mult).then_inc(sem["hidden_ready"], 1)
                    dve.wait_ge(sem["bias_added"], 1)
                    for t in range(T):
                        dve.wait_ge(sem["down_done"], t + 1)
                        nc.vector.tensor_tensor(y[:, c * T + t, :], y[:, c * T + t, :], psD[t % 2][:],
                                                ALU.add).then_inc(sem["y_ready"], 1)
            s.again()


def constants():
    bf = mybir.dt.np(BF16)
    p = np.arange(P)
    c = {}
    c["ident"] = np.eye(P, dtype=np.float32)
    c["ident_bf"] = np.eye(P).astype(bf)

    def masks(allowed):
        q, k = p[:, None], p[None, :]
        m = np.concatenate([allowed(q, k), allowed(q + P, k), allowed(q + P, k + P)], 1)
        return np.where(m, 0.0, MASKED).astype(bf)

    c["causal"] = masks(lambda q, k: k <= q)
    c["window"] = masks(lambda q, k: (k <= q) & (k >= q - 62))
    c["local"] = masks(lambda q, k: (k <= q) & (q <= k + P))
    c["head_blocks"] = (p[:, None] // 16 == p[None, :] // 16).astype(np.float32)
    c["iota8"] = np.tile(np.arange(EXPERTS, dtype=np.float32), (P, 1))
    t = np.arange(SEQ, dtype=np.float32)

    def by_token(a):
        return np.ascontiguousarray(a.reshape(2, P, -1).transpose(1, 0, 2)).astype(np.float32)

    inv = (1.0 / np.float32(10000.0) ** (np.arange(0, 16, 2, dtype=np.float32) / 16)).astype(np.float32)
    f = t[:, None] * inv[None, :]
    c["rope_cos_k"], c["rope_sin_k"] = by_token(np.cos(f)), by_token(np.sin(f))
    c["rope_cos_q"], c["rope_sin_q"] = c["rope_cos_k"] * np.float32(0.25), c["rope_sin_k"] * np.float32(0.25)
    half = np.arange(0, 64, 2, dtype=np.float32)
    inv = (1.0 / np.float32(10000.0) ** (half / 64)).astype(np.float32)
    f = t[:, None] * inv[None, :]
    f = np.concatenate([f, f], -1)
    base = (half + np.float32(0.4 * 64)) / np.float32(1.4 * 64)
    scale = base[None, :] ** ((t - SEQ // 2) / np.float32(64.0))[:, None]
    scale = np.concatenate([scale, scale], -1)
    sign = np.where(np.arange(64) < 32, -1.0, 1.0).astype(np.float32)
    c["xpos_cos_q"], c["xpos_sin_q"] = by_token(np.cos(f) * scale * 8), by_token(np.sin(f) * scale * sign * 8)
    c["xpos_cos_k"], c["xpos_sin_k"] = by_token(np.cos(f) / scale), by_token(np.sin(f) / scale * sign)
    return c


def chunks(w):
    return w.reshape(-1, P, w.shape[1]).transpose(1, 0, 2)


def layouts(i):
    d = {"x": i["x"].reshape(TILES, P, DIM).transpose(1, 0, 2)}
    d["ctxT"] = i["ctx_1024"].reshape(BATCH, SEQ, KD, P).transpose(0, 3, 2, 1)
    d["ctx"] = i["ctx_1024"].reshape(BATCH, 2, P, DIM).transpose(0, 2, 1, 3)
    d["mask_if1"] = i["mask_BxS2_if1"].reshape(TILES, P).T
    d["mask_bk1"] = i["mask_BxS2_bk1"].reshape(TILES, P).T
    d["mask_bk0"] = i["mask_BxS2_bk0"]
    for l in (0, 1, 2):
        n = f"L{l}_xattn_"
        d[f"L{l}_wqT"] = chunks(i[n + "Wq"].T if l < 2 else i[n + "Wq"])
        d[f"L{l}_wkvT"] = chunks(np.concatenate([i[n + "Wk"].T, i[n + "Wv"].T] if l < 2 else
                                                [i[n + "Wk"], i[n + "Wv"]], 1))
        d[f"L{l}_woT"] = chunks(i[n + "Wo"].T if l < 2 else i[n + "Wo"])
        d[f"L{l}_bq"], d[f"L{l}_bo"] = i[n + "bq"], i[n + "bo"]
        d[f"L{l}_bkv"] = np.concatenate([i[n + "bk"], i[n + "bv"]])
    d["L1_bq_col"] = i["L1_xattn_bq"].reshape(KD, P).T
    for w in ("q", "k", "o"):
        d[f"L3_w{w}T"] = chunks(i[f"L3_xattn_W{w}"].T)
    d["L3_bq_col"], d["L3_bk_col"] = i["L3_xattn_bq"].reshape(KD, P).T, i["L3_xattn_bk"].reshape(KD, P).T
    d["L3_bo"] = i["L3_xattn_bo"]
    d["L0_gate"], d["L3_gate"] = chunks(i["L0_ffn_gate"]), chunks(i["L3_ffn_gate_w"].T)
    d["L0_b2"] = i["L0_ffn_b2"]

    def rows_of(w):
        e, k, n = w.shape
        w = np.concatenate([w, np.zeros((e, -k % P, n), w.dtype)], 1)
        return w.reshape(e, -1, P, n).transpose(0, 2, 1, 3).reshape(e, P, -1)

    def wrapped(parts):
        a = np.concatenate(parts, 2)
        return np.concatenate([a, a[:1]], 0)

    d["L0_experts"] = wrapped([rows_of(i["L0_ffn_W1"]), i["L0_ffn_b1"].reshape(EXPERTS, -1, P).transpose(0, 2, 1),
                               rows_of(i["L0_ffn_W2"])])

    def padded(w):
        e, h, k = w.shape
        return np.concatenate([w, np.zeros((e, -h % P, k), w.dtype)], 1).transpose(0, 2, 1)

    d["L3_experts"] = wrapped([rows_of(padded(i["L3_ffn_w1"])), rows_of(padded(i["L3_ffn_w3"])),
                               rows_of(i["L3_ffn_w2"].transpose(0, 2, 1))])
    for n in ("gate", "up", "down"):
        d[f"L1_w_{n}"] = rows_of(i[f"L1_ffn_w_{n}"].T[None])[0]
    n = "L2_ffn_"
    depth = i[n + "wqkv"].shape[0]
    hid = i[n + "w2"].shape[1]

    def by_layer(f):
        return np.stack([f(l) for l in range(depth)])

    d["L2_wqkv"] = by_layer(lambda l: chunks(i[n + "wqkv"][l]))
    d["L2_wo"] = by_layer(lambda l: chunks(i[n + "wo"][l]))
    d["L2_w1"] = by_layer(lambda l: chunks(i[n + "w1"][l]))
    d["L2_w2"] = rows_of(i[n + "w2"]).reshape(depth, P, -1, DIM)
    b1 = i[n + "b1"].reshape(depth, 2, hid)
    b1 = np.concatenate([b1, np.zeros((depth, 2, -hid % P), b1.dtype)], 2)
    d["L2_b1"] = b1.reshape(depth, 2, -1, P).transpose(0, 3, 1, 2)
    d["L2_b2"] = i[n + "b2"]
    d["L2_ln_g"], d["L2_ln_b"] = (i[n + v].reshape(depth, KD, P).transpose(0, 2, 1) for v in ("ln_g", "ln_b"))
    qs, ks = i[n + "q_scale"], i[n + "k_scale"]
    d["L2_qk_scale"] = np.stack([qs, np.concatenate([qs[:, 32:], qs[:, :32]], 1),
                                 ks, np.concatenate([ks[:, 32:], ks[:, :32]], 1)], 1)
    return d


STAGES = [
    ("L0x", lambda nc, x, C, D: cross_attention(nc, x, C, D, 0, False)),
    ("L0f", lambda nc, x, C, D: mixture(nc, x, C, D, 0)),
    ("L1x", linear_attention),
    ("L1f", quantised_ffn),
    ("L2x", lambda nc, x, C, D: cross_attention(nc, x, C, D, 2, True)),
    ("L2f", local_attention_block),
    ("L3x", memory_attention),
    ("L3f", lambda nc, x, C, D: mixture(nc, x, C, D, 3)),
]


def program(nc, D, out, const_inputs, stages):
    with ExitStack() as ctx:
        s = Stage(nc, ctx, "all")
        x = s.sb("x", [P, TILES, DIM])
        C = {}
        pairs = [(x[:], D["x"])]
        for name, src in const_inputs.items():
            C[name] = s.sb(name, list(src.shape), src.dtype)
            pairs.append((C[name][:], src))
        C["minus_half"] = s.sb("minus_half", [P, 2 * TILES])
        set_done = s.sem("set_done")
        stored = s.sem("stored")
        load_block(nc, s, pairs)
        with nc.Block() as block:
            @block.vector
            def _(dve):
                nc.vector.memset(C["minus_half"][:], -0.5).then_inc(set_done, 1)
                dve.wait_ge(set_done, 1)
        for _, stage in stages:
            stage(nc, x, C, D)
        with nc.Block() as block:
            @block.sync
            def _(sp):
                sp.dma_start(out, x[:]).then_inc(stored, 16)
                sp.wait_ge(stored, 16)


def kernel(**inputs):
    import concourse.bacc as bacc
    from concourse.bass_utils import run_bass_kernel_spmd

    nc = bacc.Bacc("TRN2", target_bir_lowering=False, num_devices=1)
    arrays, aps = {}, []
    for group in (layouts(inputs), constants()):
        made = {}
        for name, a in group.items():
            a = np.ascontiguousarray(a)
            arrays[f"in_{name}"] = a
            kind = U8 if a.dtype == bool else mybir.dt.from_np(a.dtype)
            made[name] = nc.dram_tensor(f"in_{name}", a.shape, kind, kind="ExternalInput").ap()
        aps.append(made)
    out = nc.dram_tensor("out_x", (P, TILES, DIM), F32, kind="ExternalOutput").ap()
    program(nc, aps[0], out, aps[1], STAGES)
    r = run_bass_kernel_spmd(nc, [arrays], core_ids=[0])
    y = r.results[0]["out_x"]
    return y.transpose(1, 0, 2).reshape(BATCH, SEQ, DIM)
```

```python
from contextlib import ExitStack

import numpy as np

import concourse.bass as bass
from concourse import mybir

ALU = mybir.AluOpType
ACT = mybir.ActivationFunctionType
F32 = mybir.dt.float32
F32R = mybir.dt.float32r
BF16 = mybir.dt.bfloat16
U8 = mybir.dt.uint8
U32 = mybir.dt.uint32
I32 = mybir.dt.int32
AX_X = mybir.AxisListType.X

P = 128
BATCH, SEQ, DIM = 8, 256, 256
TILES = BATCH * SEQ // P
KD = DIM // P
BANK = 512
CAUSAL3 = 3 * P
MASKED = -1e30
LN_EPS = 1e-5
TINY_SQ = 1e-24
EXPERTS = 8
ROUND = 12582912.0
QUANT_MIN = 1e-5


class Stage:

    def __init__(self, nc, ctx, name):
        self.nc, self.ctx, self.name = nc, ctx, name
        self.sems = []

    def sem(self, name):
        s = self.ctx.enter_context(self.nc.semaphore(f"{self.name}_{name}"))
        self.sems.append(s)
        return s

    def sb(self, name, shape, dt=F32):
        return self.ctx.enter_context(self.nc.sbuf_tensor(f"{self.name}_{name}", shape, dt))

    def ps(self, name, shape, dt=F32):
        return self.ctx.enter_context(self.nc.psum_tensor(f"{self.name}_{name}", shape, dt))

    def again(self):
        numbers = sorted(s.num for s in self.sems)
        first = numbers[0]
        for number, following in zip(numbers, numbers[1:] + [None]):
            if following != number + 1:
                self.nc.gpsimd.sem_clear(range(first, number + 1))
                first = following
        self.nc.all_engine_barrier()


def chain(eng, sem):
    count = [0]

    def link(ins):
        count[0] += 1
        ins.then_inc(sem, 1)
        eng.wait_ge(sem, count[0])

    return link


class Ring:

    def __init__(self, banks, readers):
        self.banks, self.readers, self.n = banks, readers, 0

    def claim(self, eng):
        old = self.n - len(self.banks)
        if old >= 0:
            reader = self.readers[old]
            eng.wait_ge(reader, sum(r is reader for r in self.readers[:old + 1]))
        bank = self.banks[self.n % len(self.banks)]
        self.n += 1
        return bank

    def bank(self, n):
        return self.banks[n % len(self.banks)]


def spread(ap, axis, shape):
    return ap.unsqueeze(axis).to_broadcast(shape)


class LayerNorm:

    def __init__(self, s, tiles, pieces=1, out=None):
        self.tiles, self.pieces = tiles, pieces
        self.stats = s.sb("ln_stats", [P, tiles, 6 * pieces])
        self.mv = s.sb("ln_mean_var", [P, tiles, 2])
        self.ve = s.sb("ln_var_eps", [P, tiles])
        self.rstd = s.sb("ln_rstd", [P, tiles])
        self.xn = s.sb("ln_out", [P, tiles, DIM]) if out is None else out
        self.stats_ready = s.sem("ln_stats_ready")
        self.eps_added = s.sem("ln_eps_added")
        self.rstd_ready = s.sem("ln_rstd_ready")
        self.xn_ready = s.sem("ln_out_ready")

    def statistics(self, nc, link, parts):
        for t in range(self.tiles):
            for i, part in enumerate(parts(t)):
                ins = nc.vector.bn_stats(self.stats[:, t, 6 * i:6 * i + 6], part)
        link(ins)
        for t in range(self.tiles):
            ins = nc.vector.bn_aggr(self.mv[:, t, :], self.stats[:, t, :])
        ins.then_inc(self.stats_ready, 1)

    def root(self, nc, pool, minus_half):
        pool.wait_ge(self.stats_ready, 1)
        nc.gpsimd.tensor_scalar(self.ve[:], self.mv[:, :, 1], LN_EPS, None, ALU.add).then_inc(self.eps_added, 1)
        pool.wait_ge(self.eps_added, 1)
        nc.gpsimd.tensor_tensor(self.rstd[:], self.ve[:], minus_half[:, 0:self.tiles],
                                ALU.pow).then_inc(self.rstd_ready, 1)

    def apply(self, nc, dve, parts):
        dve.wait_ge(self.rstd_ready, 1)
        for t in range(self.tiles):
            at = 0
            for part in parts(t):
                n = part.shape[-1]
                ins = nc.vector.tensor_scalar(self.xn[:, t, at:at + n], part, self.mv[:, t, 0:1],
                                              self.rstd[:, t:t + 1], ALU.subtract, ALU.mult)
                at += n
        ins.then_inc(self.xn_ready, 1)


class Attention:

    def __init__(self, s, heads, width, form):
        self.H, self.D, self.form = heads, width, form
        self.owed = 0
        self.dt = BF16 if form == "bf16" else F32
        self.HP = 32 if form == "bf16" else 64
        self.per_chunk = P // self.HP
        self.chunks = heads // self.per_chunk
        self.cols = 2 * BANK if form == "bf16" else BANK
        self.banks = self.chunks * SEQ // self.cols
        self.early = 1 if form == "halves" else self.banks
        self.W = width + 1
        self.rounds = -(-heads * self.W // BANK)
        self.per_round = heads // self.rounds
        self.q_rows = s.sb("q_rows", [P, 2, heads, self.HP], self.dt)
        self.k_rows = s.sb("k_rows", [P, 2, heads, self.HP], self.dt)
        self.v_wide = s.sb("v_rows", [P, 2, heads * self.W + P])
        self.v_rows = self.v_wide[:, :, 0:heads * self.W].rearrange("p t (h w) -> p t h w", w=self.W)
        if form == "bf16":
            self.qT, self.kT = (s.sb(n, [P, self.chunks, SEQ], BF16) for n in ("qT", "kT"))
        else:
            self.qT, self.kT = s.sb("qT", [P, self.chunks, SEQ], F32R), s.sb("kT", [P, self.chunks, 2, SEQ], F32R)
        if form == "halves":
            self.qL, self.kL = s.sb("qT_low", [P, self.chunks, SEQ], F32R), s.sb("kT_low", [P, self.chunks, 2, SEQ], F32R)
            self.high_kept = s.sem("high_kept")
        if form == "packed":
            self.keys_placed = s.sem("keys_placed")
        self.negmax = s.sb("negmax", [P, 2, heads])
        self.prow = s.sb("probs", [P, 2, CAUSAL3])
        self.probsT = s.sb("probsT", [P, 2, CAUSAL3])
        self.rsum = s.sb("rsum", [P, 2, heads])
        self.o_rows = s.sb("o_rows", [P, 2, heads, width])
        self.psS = s.ps("scores", [P, 2, BANK])
        self.psT = s.ps("probs_turned", [P, 2, BANK])
        self.psO = s.ps("pv", [P, 2, BANK])
        self.v_ready = s.sem("v_ready")
        self.rows_turned, self.operands = s.sem("rows_turned"), s.sem("operands")
        self.scores_done, self.max_taken, self.exp_done = s.sem("scores_done"), s.sem("max_taken"), s.sem("exp_done")
        self.probs_turned, self.probs_ready = s.sem("probs_turned"), s.sem("probs_ready")
        self.pv_done, self.o_ready = s.sem("pv_done"), s.sem("o_ready")

    def clear(self, nc, pool, done):
        nc.gpsimd.memset(self.q_rows[:], 0.0)
        nc.gpsimd.memset(self.k_rows[:], 0.0)
        if self.form != "bf16":
            nc.gpsimd.memset(self.kT[:].bitcast(F32), 0.0)
        if self.form == "halves":
            nc.gpsimd.memset(self.kL[:].bitcast(F32), 0.0)
        nc.gpsimd.memset(self.v_wide[:], 1.0).then_inc(done, 1)
        pool.wait_ge(done, 1)

    def products(self, h):
        c, r = h // self.per_chunk, h % self.per_chunk
        if self.form == "bf16":
            rows = slice(r * self.HP, r * self.HP + self.W)
            return [(self.qT[rows, c, :], self.kT[rows, c, :])]
        high = (self.qT[:, c, :], self.kT[:, c, r, :])
        if self.form == "packed":
            return [high]
        return [high, (self.qL[:, c, :], self.kT[:, c, r, :]), (self.qT[:, c, :], self.kL[:, c, r, :])]

    def flip_bank(self, n):
        bank = (self.psT if n % 4 < 2 else self.psO)[:, n % 2, :]
        return bank if self.dt == F32 else bank.bitcast(BF16)

    def flip(self, nc, pe, ident):
        per = self.cols // SEQ
        for n in range(2 * self.banks):
            if n >= 4:
                pe.wait_ge(self.operands, n - 3)
                if self.form == "packed" and n % 2 == 0:
                    pe.wait_ge(self.keys_placed, n // 2 - 1)
            if n == 2 and self.owed:
                pe.wait_ge(self.o_ready, 1)
            rows, view = (self.k_rows, self.q_rows)[n % 2], self.flip_bank(n)
            for i in range(per):
                c = n // 2 * per + i
                for t in range(2):
                    src = rows[:, t, c * self.per_chunk:(c + 1) * self.per_chunk, :]
                    ins = nc.tensor.transpose(view[:, i * SEQ + t * P:i * SEQ + (t + 1) * P],
                                              src.rearrange("p h d -> p (h d)"), ident[:])
            ins.then_inc(self.rows_turned, 1)

    def keep_high(self, nc, act, pairs):
        per = self.cols // SEQ
        done = self.high_kept if self.form == "halves" else self.operands
        for n in range(2 * pairs.start, 2 * pairs.stop):
            act.wait_ge(self.rows_turned, n + 1)
            view = self.flip_bank(n)[:, 0:self.cols].rearrange("p (c t) -> p c t", t=SEQ)
            m = n // 2 * per
            if n % 2 or self.form == "bf16":
                to = self.qT if n % 2 else self.kT
                ins = nc.scalar.copy(to[:, m:m + per, :], view)
            else:
                for r in range(2 if self.form == "halves" else 1):
                    rows = slice(r * 64, (r + 1) * 64)
                    ins = nc.scalar.copy(self.kT[rows, m:m + per, r, :], view[rows])
            ins.then_inc(done, 1)

    def place_keys(self, nc, dve, pairs):
        per = self.cols // SEQ
        for n in range(2 * pairs.start, 2 * pairs.stop, 2):
            dve.wait_ge(self.rows_turned, n + 1)
            view = self.flip_bank(n)[:, 0:self.cols].rearrange("p (c t) -> p c t", t=SEQ)
            m = n // 2 * per
            nc.vector.tensor_copy(self.kT[64:P, m:m + per, 1, :], view[64:P]).then_inc(self.keys_placed, 1)

    def keep_low(self, nc, dve, pairs):
        per = self.cols // SEQ
        for n in range(2 * pairs.start, 2 * pairs.stop):
            dve.wait_ge(self.high_kept, n + 1)
            view = self.flip_bank(n).rearrange("p (c t) -> p c t", t=SEQ)
            m = n // 2 * per
            if n % 2:
                ins = nc.vector.tensor_tensor(self.qL[:, m:m + per, :], view,
                                              self.qT[:, m:m + per, :].bitcast(F32), ALU.subtract)
            else:
                for r in range(2):
                    rows = slice(r * 64, (r + 1) * 64)
                    ins = nc.vector.tensor_tensor(self.kL[rows, m:m + per, r, :], view[rows],
                                                  self.kT[rows, m:m + per, r, :].bitcast(F32), ALU.subtract)
            ins.then_inc(self.operands, 1)

    def keep_rest(self, nc, dve, pairs):
        if self.form == "halves":
            self.keep_low(nc, dve, pairs)
        if self.form == "packed":
            self.place_keys(nc, dve, pairs)

    def tensor(self, nc, pe, C, mask, beside):
        self.flip(nc, pe, C["ident"] if self.dt == F32 else C["ident_bf"])
        beside(-1)
        for step in range(self.H + 3):
            if step < self.H:
                self.scores(nc, pe, step, C["ident_bf"], mask(step))
            if 2 <= step < self.H + 2:
                self.turn(nc, pe, step - 2, C["ident"])
            if step >= 3:
                self.values(nc, pe, step - 3)
            beside(step)

    def scores(self, nc, pe, h, ident_bf, mask):
        if h * self.banks % self.H == 0:
            pe.wait_ge(self.operands, 2 * (h * self.banks // self.H + 1))
            if self.form == "packed":
                pe.wait_ge(self.keys_placed, h * self.banks // self.H + 1)
        if h >= 2:
            pe.wait_ge(self.exp_done, h - 1)
        bank = self.psS[:, h % 2, :]
        nc.tensor.matmul(bank[:, 0:CAUSAL3], ident_bf[:], mask, start=True, stop=True)
        for q, k in self.products(h):
            nc.tensor.matmul(bank[:, 0:P], q[:, 0:P], k[:, 0:P], start=False, stop=False, skip_group_check=True)
            ins = nc.tensor.matmul(bank[:, P:CAUSAL3], q[:, P:SEQ], k, start=False, stop=False,
                                   skip_group_check=True)
        ins.then_inc(self.scores_done, 1)

    def turn(self, nc, pe, h, ident):
        pe.wait_ge(self.exp_done, h + 1)
        if h == 0:
            pe.wait_ge(self.operands, 2 * self.early)
            if self.form == "packed":
                pe.wait_ge(self.keys_placed, self.banks)
        if h >= 2:
            pe.wait_ge(self.probs_ready, h - 1)
        for i in range(3):
            at = slice(i * P, (i + 1) * P)
            ins = nc.tensor.transpose(self.psT[:, h % 2, at], self.prow[:, h % 2, at], ident[:])
        ins.then_inc(self.probs_turned, 1)

    def values(self, nc, pe, h):
        pe.wait_ge(self.probs_ready, h + 1)
        if h == 0:
            pe.wait_ge(self.v_ready, 1)
            pe.wait_ge(self.operands, 2 * self.banks)
        if h % self.per_round == 0 and self.owed + h:
            pe.wait_ge(self.o_ready, h // self.per_round + self.owed)
        o, at = (h % self.per_round) * self.W, h * self.W
        pr = self.probsT[:, h % 2, :]
        low, high = self.v_wide[:, 0, at:at + P], self.v_wide[:, 1, at:at + P]
        nc.tensor.matmul(self.psO[:, 0, o:o + P], pr[:, 0:P], low, start=True, stop=True)
        nc.tensor.matmul(self.psO[:, 1, o:o + P], pr[:, P:SEQ], low, start=True, stop=False)
        nc.tensor.matmul(self.psO[:, 1, o:o + P], pr[:, SEQ:CAUSAL3], high, start=False,
                         stop=True).then_inc(self.pv_done, 1)

    def scalar(self, nc, act, beside):
        self.keep_high(nc, act, range(0, self.early))
        beside(-1)
        for step in range(self.H + 2):
            h = step - 2
            if h >= 0:
                act.wait_ge(self.probs_turned, h + 1)
                if h >= 2:
                    act.wait_ge(self.pv_done, h - 1)
                nc.scalar.copy(self.probsT[:, h % 2, :], self.psT[:, h % 2, 0:CAUSAL3]).then_inc(self.probs_ready, 1)
            if step < self.H:
                act.wait_ge(self.max_taken, step + 1)
                if step >= 2:
                    act.wait_ge(self.probs_turned, step - 1)
                for t, (a, b) in enumerate(((0, P), (P, CAUSAL3))):
                    ins = nc.scalar.activation(self.prow[:, step % 2, a:b], self.psS[:, step % 2, a:b], ACT.Exp,
                                               bias=self.negmax[:, t, step:step + 1])
                ins.then_inc(self.exp_done, 1)
            if step and self.early + step - 1 < self.banks:
                self.keep_high(nc, act, range(self.early + step - 1, self.early + step))
            beside(step)

    def vector(self, nc, dve, link, beside):
        self.settle(nc, dve, link)
        self.keep_rest(nc, dve, range(0, self.early))
        beside(-1)
        for step in range(self.H + 2):
            if step < self.H:
                dve.wait_ge(self.scores_done, step + 1)
                for t, (a, b) in enumerate(((0, P), (P, CAUSAL3))):
                    ins = nc.vector.tensor_reduce(self.negmax[:, t, step:step + 1], self.psS[:, step % 2, a:b],
                                                  AX_X, ALU.max, negate=True)
                ins.then_inc(self.max_taken, 1)
            if step and self.early + step - 1 < self.banks:
                self.keep_rest(nc, dve, range(self.early + step - 1, self.early + step))
            h = step - 2
            if h >= 1 and h % self.per_round == 0:
                self.normalise(nc, dve, link, h // self.per_round - 1)
            beside(step)

    def settle(self, nc, dve, link):
        if self.owed:
            self.normalise(nc, dve, link, self.rounds - 1, owed=True)

    def normalise(self, nc, dve, link, r, owed=False):
        if not owed:
            dve.wait_ge(self.pv_done, (r + 1) * self.per_round)
        hs = slice(r * self.per_round, (r + 1) * self.per_round)
        views = [self.psO[:, t, 0:self.per_round * self.W].rearrange("p (h w) -> p h w", w=self.W) for t in range(2)]
        for t in range(2):
            ins = nc.vector.reciprocal(self.rsum[:, t, hs], views[t][:, :, self.D])
        link(ins)
        for t in range(2):
            ins = nc.vector.tensor_tensor(self.o_rows[:, t, hs, :], views[t][:, :, 0:self.D],
                                          spread(self.rsum[:, t, hs], 2, [P, self.per_round, self.D]), ALU.mult)
        ins.then_inc(self.o_ready, 1)


def load_block(nc, s, pairs):
    landed = s.sem("loaded")
    with nc.Block() as block:
        @block.sync
        def _(sp):
            for to, src in pairs:
                sp.dma_start(to, src).then_inc(landed, 16)
            sp.wait_ge(landed, 16 * len(pairs))


def cross_attention(nc, x, C, D, layer, rounded):
    H, HD = 16, 16
    with ExitStack() as ctx:
        s = Stage(nc, ctx, f"x{layer}")
        wdt = BF16 if rounded else F32
        wq, wkv = s.sb("wq", [P, KD, DIM], wdt), s.sb("wkv", [P, KD, 2 * DIM], wdt)
        wo = s.sb("wo", [P, KD, DIM], wdt)
        bq, bkv, bo = s.sb("bq", [P, DIM], wdt), s.sb("bkv", [P, 2 * DIM], wdt), s.sb("bo", [P, DIM], wdt)
        pairs = []
        staged = []
        for to, name in ((wq, "wqT"), (wkv, "wkvT"), (wo, "woT"), (bq, "bq"), (bkv, "bkv"), (bo, "bo")):
            src = D[f"L{layer}_{name}"]
            if name[0] == "b":
                src = src.partition_broadcast(P)
            if rounded:
                raw = s.sb(f"raw_{name}", list(to.shape))
                staged.append((to, raw))
                pairs.append((raw[:], src))
            else:
                pairs.append((to[:], src))
        if rounded:
            keep = s.sb("key_mask", [P, TILES], I32)
            blocked = s.sb("blocked", [P, TILES])
            pairs.append((keep[:], D["mask_if1"]))
        load_block(nc, s, pairs)

        psA = [s.ps(f"work{i}", [P, BANK]) for i in range(2)]
        att = Attention(s, H, HD, "bf16" if rounded else "packed")
        ln = LayerNorm(s, 2)
        xnb = s.sb("xn_bf", [P, 2, DIM], BF16) if rounded else None
        ctxT = s.sb("ctxT", [P, KD, SEQ])
        ctxTb = s.sb("ctxT_bf", [P, KD, SEQ], BF16) if rounded else ctxT
        xnT = s.sb("xnT", [P, KD, SEQ], wdt)
        oT = s.sb("oT", [P, KD, SEQ], wdt)
        ob = s.sb("o_bf", [P, 2, DIM], BF16) if rounded else None
        raw = s.sb("qk_raw", [P, 2, 2, H, HD], wdt)
        biased = s.sb("biased", [P, 2, 2, DIM], BF16) if rounded else None
        vr = s.sb("v_raw", [P, 2, DIM], wdt)
        rot = s.sb("rotary", [P, 2, 2, H, HD // 2]) if not rounded else None
        turned = s.sb("turned_by_position", [P, 2, H, HD]) if not rounded else None
        prod = s.sb("outproj_bf", [P, 2, DIM], BF16) if rounded else None
        sem = {n: s.sem(n) for n in ("link", "ctx_landed", "ctx_cast", "kv_done", "x_turned", "q_done", "by_act",
                                     "by_dve", "x_bf", "o_bf", "o_turned", "out_done", "bias_added", "x_ready",
                                     "weights_cast", "cleared")}

        with nc.Block() as block:
            @block.gpsimd
            def _(pool):
                att.clear(nc, pool, sem["cleared"])
                if rounded:
                    nc.gpsimd.memset(att.q_rows[:, :, :, HD:HD + 1], 1.0).then_inc(sem["cleared"], 1)
                    pool.wait_ge(sem["cleared"], 2)

            @block.vector
            def _(dve):
                link = chain(dve, sem["link"])
                for to, r in staged:
                    nc.vector.tensor_copy(to[:], r[:])
                if rounded:
                    link(nc.vector.tensor_scalar(blocked[:], keep[:], 0.0, MASKED, ALU.is_le, ALU.mult))
                link(nc.vector.memset(raw[:], 0.0))
        s.again()

        KV_STEPS, KV_READS = ((1, 2), (2, 3)) if rounded else ((0, 1), (1, 3))
        A, V = sem["by_act"], sem["by_dve"]
        ident = C["ident_bf"] if rounded else C["ident"]

        def turn(front, core, tail):
            made = 5 if front is not None else 0
            turned_o = att.owed = 1 if tail is not None else 0
            readers = [A][:turned_o] + [V, V, A, V, V][:made] + [V, V]
            USE_KV, USE_X, USE_Q, USE_OUT = turned_o, turned_o + 2, turned_o + 3, turned_o + made
            if front is not None:
                first, batch = front

            def parts(t):
                return [x[:, first + t, :]]

            with nc.Block() as block:
                @block.sync
                def _(sp):
                    if front is not None:
                        sp.dma_start(ctxT[:], D["ctxT"][batch]).then_inc(sem["ctx_landed"], 16)

                @block.gpsimd
                def _(pool):
                    if tail is not None and not rounded:
                        for t in range(2):
                            ins = nc.gpsimd.tensor_tensor(x[:, tail + t, :], x[:, tail + t, :], bo[:], ALU.add)
                        ins.then_inc(sem["bias_added"], 1)
                    if front is None:
                        return
                    if rounded:
                        pool.wait_ge(sem["ctx_landed"], 16)
                        nc.gpsimd.tensor_copy(ctxTb[:], ctxT[:]).then_inc(sem["ctx_cast"], 1)
                    ln.root(nc, pool, C["minus_half"])

                @block.tensor
                def _(pe):
                    ring = Ring(psA, readers)

                    def beside(step):
                        if step == -1 and tail is not None:
                            bank = ring.claim(pe)
                            view = bank[:].bitcast(BF16) if rounded else bank[:]
                            orow = ob if rounded else att.o_rows
                            pe.wait_ge(sem["o_bf"] if rounded else att.o_ready, 1)
                            for k in range(KD):
                                for t in range(2):
                                    src = (orow[:, t, k * P:(k + 1) * P] if rounded else
                                           orow[:, t, k * 8:(k + 1) * 8, :].rearrange("p h d -> p (h d)"))
                                    ins = nc.tensor.transpose(view[:, k * SEQ + t * P:k * SEQ + (t + 1) * P], src,
                                                              ident[:])
                            ins.then_inc(sem["o_turned"], 1)
                        if step in KV_STEPS and front is not None:
                            t = step - KV_STEPS[0]
                            if t == 0:
                                if rounded:
                                    pe.wait_ge(sem["ctx_cast"], 1)
                                else:
                                    pe.wait_ge(sem["ctx_landed"], 16)
                            bank = ring.claim(pe)
                            for k in range(KD):
                                ins = nc.tensor.matmul(bank[:], ctxTb[:, k, t * P:(t + 1) * P], wkv[:, k, :],
                                                       start=(k == 0), stop=(k == KD - 1))
                            ins.then_inc(sem["kv_done"], 1)
                        if step == 3 and front is not None:
                            bank = ring.claim(pe)
                            view = bank[:].bitcast(BF16) if rounded else bank[:]
                            src = xnb if rounded else ln.xn
                            pe.wait_ge(sem["x_bf"] if rounded else ln.xn_ready, 1)
                            for k in range(KD):
                                for t in range(2):
                                    ins = nc.tensor.transpose(view[:, k * SEQ + t * P:k * SEQ + (t + 1) * P],
                                                              src[:, t, k * P:(k + 1) * P], ident[:])
                            ins.then_inc(sem["x_turned"], 1)
                        if step in (5, 6) and front is not None:
                            t = step - 5
                            if t == 0:
                                pe.wait_ge(A, turned_o + 1)
                            bank = ring.claim(pe)
                            for k in range(KD):
                                ins = nc.tensor.matmul(bank[:, 0:DIM], xnT[:, k, t * P:(t + 1) * P], wq[:, k, :],
                                                       start=(k == 0), stop=(k == KD - 1))
                            ins.then_inc(sem["q_done"], 1)
                        if step in (7, 8) and tail is not None:
                            t = step - 7
                            if t == 0:
                                pe.wait_ge(A, 1)
                            bank = ring.claim(pe)
                            for k in range(KD):
                                ins = nc.tensor.matmul(bank[:, 0:DIM], oT[:, k, t * P:(t + 1) * P], wo[:, k, :],
                                                       start=(k == 0), stop=(k == KD - 1))
                            ins.then_inc(sem["out_done"], 1)

                    if core is None:
                        for step in range(-1, H):
                            beside(step)
                    else:
                        att.tensor(nc, pe, C, lambda h: C["causal" if rounded or h < 4 else "window"][:], beside)

                @block.scalar
                def _(act):
                    ring = Ring(psA, readers)

                    def beside(step):
                        if step == -1 and core is not None:
                            nc.scalar.copy(att.v_rows[:, :, :, 0:HD],
                                           vr[:].rearrange("p t (h d) -> p t h d", h=H)).then_inc(att.v_ready, 1)
                        if step == -1 and tail is not None:
                            act.wait_ge(sem["o_turned"], 1)
                            view = ring.bank(0)[:].bitcast(BF16) if rounded else ring.bank(0)[:]
                            nc.scalar.copy(oT[:], view[:, 0:KD * SEQ].rearrange("p (k t) -> p k t", k=KD)).then_inc(A, 1)
                        if step == 4 and front is not None:
                            act.wait_ge(sem["x_turned"], 1)
                            view = ring.bank(USE_X)[:].bitcast(BF16) if rounded else ring.bank(USE_X)[:]
                            nc.scalar.copy(xnT[:], view[:, 0:KD * SEQ].rearrange("p (k t) -> p k t", k=KD)).then_inc(A, 1)

                    if core is None:
                        for step in range(-1, H):
                            beside(step)
                    else:
                        att.scalar(nc, act, beside)

                @block.vector
                def _(dve):
                    ring = Ring(psA, readers)
                    link = chain(dve, sem["link"])

                    def by_position(which, t):
                        q_or_k = "q" if which == 0 else "k"
                        cos, sin = C[f"rope_cos_{q_or_k}"], C[f"rope_sin_{q_or_k}"]
                        even, odd = raw[:, t, which, :, 0:HD:2], raw[:, t, which, :, 1:HD:2]
                        shape = [P, H, HD // 2]
                        ct, st = spread(cos[:, t, :], 1, shape), spread(sin[:, t, :], 1, shape)
                        out_e, out_o = turned[:, t, :, 0:HD:2], turned[:, t, :, 1:HD:2]
                        nc.vector.tensor_tensor(rot[:, t, 0], even, st, ALU.mult)
                        nc.vector.tensor_tensor(rot[:, t, 1], odd, st, ALU.mult)
                        nc.vector.tensor_tensor(out_e, even, ct, ALU.mult)
                        link(nc.vector.tensor_tensor(out_o, odd, ct, ALU.mult))
                        nc.vector.tensor_tensor(out_e, out_e, rot[:, t, 1], ALU.subtract)
                        link(nc.vector.tensor_tensor(out_o, out_o, rot[:, t, 0], ALU.add))

                    def split(which, to):
                        low, again = (2, 1) if which == 0 else (1, 2)
                        parts_of = [to[:, :, :, i * HD:(i + 1) * HD] for i in range(3)]
                        nc.vector.tensor_copy(parts_of[again].bitcast(F32R), turned[:])
                        link(nc.vector.tensor_copy(parts_of[0].bitcast(F32R), turned[:]))
                        link(nc.vector.tensor_tensor(parts_of[low], turned[:], parts_of[0], ALU.subtract))

                    def add_output(t):
                        dve.wait_ge(sem["out_done"], t + 1)
                        bank = ring.bank(USE_OUT + t)
                        if rounded:
                            link(nc.vector.tensor_copy(prod[:, t, :], bank[:, 0:DIM]))
                            link(nc.vector.tensor_tensor(prod[:, t, :], prod[:, t, :], bo[:], ALU.add))
                            nc.vector.tensor_tensor(x[:, tail + t, :], x[:, tail + t, :], prod[:, t, :],
                                                    ALU.add).then_inc(V, 1)
                        else:
                            dve.wait_ge(sem["bias_added"], 1)
                            nc.vector.tensor_tensor(x[:, tail + t, :], x[:, tail + t, :], bank[:, 0:DIM],
                                                    ALU.add).then_inc(V, 1)

                    def beside(step):
                        if step == -1 and tail is not None and rounded:
                            dve.wait_ge(att.o_ready, 1)
                            nc.vector.tensor_copy(ob[:], att.o_rows[:].rearrange("p t h d -> p t (h d)")).then_inc(
                                sem["o_bf"], 1)
                        if step == 0 and tail is not None:
                            dve.wait_ge(sem["o_turned"], 1)
                        if step in (12, 13) and tail is not None:
                            add_output(step - 12)
                        if front is None:
                            return
                        if step == -1:
                            ln.statistics(nc, link, parts)
                        if step == 2:
                            ln.apply(nc, dve, parts)
                            if rounded:
                                dve.wait_ge(ln.xn_ready, 1)
                                nc.vector.tensor_copy(xnb[:], ln.xn[:]).then_inc(sem["x_bf"], 1)
                        if step in KV_READS:
                            t = KV_READS.index(step)
                            dve.wait_ge(sem["kv_done"], t + 1)
                            if core is not None and t == 0:
                                dve.wait_ge(att.v_ready, 1)
                            bank = ring.bank(USE_KV + t)
                            if rounded:
                                nc.vector.tensor_copy(biased[:, t, 1, :], bank[:, 0:DIM])
                                nc.vector.tensor_copy(vr[:, t, :], bank[:, DIM:2 * DIM]).then_inc(V, 1)
                            else:
                                nc.vector.tensor_tensor(raw[:, t, 1].rearrange("p h d -> p (h d)"), bank[:, 0:DIM],
                                                        bkv[:, 0:DIM], ALU.add)
                                nc.vector.tensor_tensor(vr[:, t, :], bank[:, DIM:2 * DIM], bkv[:, DIM:2 * DIM],
                                                        ALU.add).then_inc(V, 1)
                        if step in (4, 5):
                            t = step - 4
                            if t == 0:
                                dve.wait_ge(V, 2)
                                if core is not None:
                                    dve.wait_ge(att.rows_turned, 2 * att.banks)
                            if rounded:
                                nc.vector.tensor_tensor(att.k_rows[:, t, :, 0:HD],
                                                        biased[:, t, 1, :].rearrange("p (h d) -> p h d", h=H),
                                                        bkv[:, 0:DIM].rearrange("p (h d) -> p h d", h=H), ALU.add)
                                nc.vector.tensor_copy(att.k_rows[:, t, :, HD:HD + 1],
                                                      blocked[:, bass.ds(first + t, 1)].unsqueeze(1).to_broadcast([P, H, 1]))
                                link(nc.vector.tensor_tensor(vr[:, t, :], vr[:, t, :], bkv[:, DIM:2 * DIM], ALU.add))
                            else:
                                by_position(1, t)
                        if step == 6 and not rounded:
                            split(1, att.k_rows)
                        if step in (7, 8):
                            t = step - 7
                            dve.wait_ge(sem["q_done"], t + 1)
                            bank = ring.bank(USE_Q + t)
                            if rounded:
                                nc.vector.tensor_copy(biased[:, t, 0, :], bank[:, 0:DIM]).then_inc(V, 1)
                            else:
                                nc.vector.tensor_tensor(raw[:, t, 0].rearrange("p h d -> p (h d)"), bank[:, 0:DIM],
                                                        bq[:], ALU.add).then_inc(V, 1)
                        if step in (9, 10):
                            t = step - 9
                            if t == 0:
                                dve.wait_ge(V, 4)
                            if rounded:
                                link(nc.vector.tensor_tensor(att.q_rows[:, t, :, 0:HD],
                                                             biased[:, t, 0, :].rearrange("p (h d) -> p h d", h=H),
                                                             bq[:].rearrange("p (h d) -> p h d", h=H), ALU.add))
                            else:
                                by_position(0, t)
                        if step == 11:
                            if rounded:
                                rows = att.q_rows[:, :, :, 0:HD]
                                link(nc.vector.tensor_scalar(rows, rows, 1.0 / HD ** 0.5, None, ALU.mult))
                            else:
                                split(0, att.q_rows)

                    if core is None:
                        att.settle(nc, dve, link)
                        for step in range(-1, H):
                            beside(step)
                    else:
                        att.vector(nc, dve, link, beside)
            s.again()

        turn((0, 0), None, None)
        turn((2, 1), 0, None)
        with nc.Fori(0, BATCH - 2) as b:
            turn((b * 2 + 4, b + 2), b * 2 + 2, b * 2)
        turn(None, 2 * (BATCH - 1), 2 * (BATCH - 2))
        turn(None, None, 2 * (BATCH - 1))


def turn_rows(nc, bank, rows, ident, tiles, width):
    for k in range(width // P):
        for t in range(tiles):
            at = (k * tiles + t) * P
            ins = nc.tensor.transpose(bank[:, at:at + P], rows[:, t, k * P:(k + 1) * P], ident[:])
    return ins


def layer_one(nc, x, C, D):
    with ExitStack() as ctx:
        s = Stage(nc, ctx, "w1")
        raw = s.sb("ffn_weights", [P, D["L1_ffn"].shape[0] * D["L1_ffn"].shape[2]])
        linear_attention(nc, x, C, D, raw)
        quantised_ffn(nc, x, C, raw)


def linear_attention(nc, x, C, D, ffn_weights):
    H, HD = 16, 16
    PAIR = 2
    with ExitStack() as ctx:
        s = Stage(nc, ctx, "x1")
        wq, wkv, wo = s.sb("wq", [P, KD, DIM]), s.sb("wkv", [P, KD, 2 * DIM]), s.sb("wo", [P, KD, DIM])
        bq, bkv, bo = s.sb("bq", [P, KD]), s.sb("bkv", [P, 2 * DIM]), s.sb("bo", [P, DIM])
        dropped = s.sb("dropped", [P, TILES], U8)
        keep = s.sb("keep", [P, TILES])
        load_block(nc, s, [(wq[:], D["L1_wqT"]), (wkv[:], D["L1_wkvT"]), (wo[:], D["L1_woT"]),
                           (bq[:], D["L1_bq_col"]), (bkv[:], D["L1_bkv"].partition_broadcast(P)),
                           (bo[:], D["L1_bo"].partition_broadcast(P)), (dropped[:], D["mask_bk1"])])
        banks = [s.ps(f"bank{i}", [P, BANK]) for i in range(8)]
        ln = LayerNorm(s, 2 * PAIR)
        ctxT = s.sb("ctxT", [P, PAIR, KD, SEQ])
        xnT = s.sb("xnT", [P, PAIR, KD, SEQ])
        k_raw, k_neg, k_exp, k_sq = (s.sb(n, [P, PAIR, 2, DIM]) for n in ("k_raw", "k_neg", "k_exp", "k_sq"))
        k_ss, k_rn = s.sb("k_ss", [P, PAIR, 2 * H]), s.sb("k_rn", [P, PAIR, 2 * H])
        q_raw, q_neg, q_exp, q_sq = (s.sb(n, [P, PAIR, KD, SEQ]) for n in ("q_raw", "q_neg", "q_exp", "q_sq"))
        q_ss, q_rn = s.sb("q_ss", [P, PAIR, KD]), s.sb("q_rn", [P, PAIR, KD])
        v = s.sb("v", [P, PAIR, 2, DIM])
        m = s.sb("m", [P, PAIR, KD, P])
        oT = s.sb("oT", [P, PAIR, KD, SEQ])
        sem = {n: s.sem(n) for n in ("link", "ctx_landed", "kv_done", "kv_read", "x_turned", "xnT_ready", "q_done",
                                     "q_read", "k_neg", "k_exp", "k_ss", "k_bounded", "k_rn", "k_ready", "q_neg", "q_exp",
                                     "q_ready", "q_ss", "q_bounded", "q_rn", "m_done", "m_ready", "o_done", "o_ready",
                                     "y_done", "bias_added", "x_ready", "piece_landed")}
        with nc.Block() as block:
            @block.sync
            def _(sp):
                for j in range(PAIR):
                    sp.dma_start(ctxT[:, j], D["ctxT"][j]).then_inc(sem["ctx_landed"], 16)
                sp.wait_ge(sem["ctx_landed"], 16 * PAIR)

            @block.vector
            def _(dve):
                link = chain(dve, sem["link"])
                link(nc.vector.tensor_scalar(keep[:], dropped[:], -1.0, 1.0, ALU.mult, ALU.add))
        s.again()
        readers = ([sem["kv_read"]] * 4 + [sem["xnT_ready"]] * 2 + [sem["q_read"]] * 2 + [sem["m_ready"]] * 2 +
                   [sem["o_ready"]] * 2 + [sem["x_ready"]] * 2)
        KV, X, Q, M, O, Y = 0, 4, 6, 8, 10, 12
        with nc.Fori(0, BATCH // PAIR) as p:
            with nc.Block() as block:
                first = p * 2 * PAIR
                pair = range(PAIR)

                @block.sync
                def _(sp):
                    piece = D["L1_ffn"].shape[2]
                    sp.dma_start(ffn_weights[:, bass.ds(p * piece, piece)], D["L1_ffn"][p]).then_inc(sem["piece_landed"], 16)
                    sp.wait_ge(sem["kv_done"], 2 * PAIR)
                    for j in pair:
                        sp.dma_start(ctxT[:, j], D["ctxT"][p * PAIR + PAIR + j]).then_inc(sem["ctx_landed"], 16)
                    sp.wait_ge(sem["piece_landed"], 16)
                    sp.wait_ge(sem["ctx_landed"], 16 * PAIR)

                @block.gpsimd
                def _(pool):
                    ln.root(nc, pool, C["minus_half"])
                    for j in pair:
                        pool.wait_ge(sem["k_ss"], j + 1)
                        nc.gpsimd.tensor_scalar(k_ss[:, j], k_ss[:, j], TINY_SQ, None, ALU.max).then_inc(sem["k_bounded"], 1)
                        pool.wait_ge(sem["k_bounded"], j + 1)
                        nc.gpsimd.tensor_tensor(k_rn[:, j], k_ss[:, j], C["minus_half"][:, 0:2 * H],
                                                ALU.pow).then_inc(sem["k_rn"], 1)
                    for j in pair:
                        pool.wait_ge(sem["q_ss"], (j + 1) * KD)
                        nc.gpsimd.tensor_scalar(q_ss[:, j], q_ss[:, j], TINY_SQ, None, ALU.max).then_inc(sem["q_bounded"], 1)
                        pool.wait_ge(sem["q_bounded"], j + 1)
                        nc.gpsimd.tensor_tensor(q_rn[:, j], q_ss[:, j], C["minus_half"][:, 0:KD],
                                                ALU.pow).then_inc(sem["q_rn"], 1)
                    pool.wait_ge(ln.xn_ready, PAIR)
                    for t in range(2 * PAIR):
                        ins = nc.gpsimd.tensor_tensor(x[:, first + t, :], x[:, first + t, :], bo[:], ALU.add)
                    ins.then_inc(sem["bias_added"], 1)

                @block.tensor
                def _(pe):
                    ring = Ring(banks, readers)
                    for j in pair:
                        for t in range(2):
                            bank = ring.claim(pe)
                            for k in range(KD):
                                ins = nc.tensor.matmul(bank[:], ctxT[:, j, k, t * P:(t + 1) * P], wkv[:, k, :],
                                                       start=(k == 0), stop=(k == KD - 1))
                            ins.then_inc(sem["kv_done"], 1)
                    for j in pair:
                        pe.wait_ge(ln.xn_ready, j + 1)
                        turn_rows(nc, ring.claim(pe), ln.xn[:, 2 * j:2 * j + 2, :], C["ident"], 2,
                                  DIM).then_inc(sem["x_turned"], 1)
                    for j in pair:
                        pe.wait_ge(sem["xnT_ready"], j + 1)
                        bank = ring.claim(pe)
                        for c in range(KD):
                            for k in range(KD):
                                ins = nc.tensor.matmul(bank[:, c * SEQ:(c + 1) * SEQ], wq[:, k, c * P:(c + 1) * P],
                                                       xnT[:, j, k, :], start=(k == 0), stop=(k == KD - 1))
                        ins.then_inc(sem["q_done"], 1)
                    for j in pair:
                        pe.wait_ge(sem["k_ready"], j + 1)
                        bank = ring.claim(pe)
                        for c in range(KD):
                            for t in range(2):
                                ins = nc.tensor.matmul(bank[:, c * P:(c + 1) * P], k_exp[:, j, t, c * P:(c + 1) * P],
                                                       v[:, j, t, c * P:(c + 1) * P], start=(t == 0), stop=(t == 1))
                        ins.then_inc(sem["m_done"], 1)
                    for j in pair:
                        pe.wait_ge(sem["m_ready"], j + 1)
                        bank = ring.claim(pe)
                        for c in range(KD):
                            ins = nc.tensor.matmul(bank[:, c * SEQ:(c + 1) * SEQ], m[:, j, c, :], q_exp[:, j, c, :],
                                                   start=True, stop=True)
                        ins.then_inc(sem["o_done"], 1)
                    for j in pair:
                        pe.wait_ge(sem["o_ready"], j + 1)
                        bank = ring.claim(pe)
                        for t in range(2):
                            for k in range(KD):
                                ins = nc.tensor.matmul(bank[:, t * DIM:(t + 1) * DIM], oT[:, j, k, t * P:(t + 1) * P],
                                                       wo[:, k, :], start=(k == 0), stop=(k == KD - 1))
                        ins.then_inc(sem["y_done"], 1)

                @block.scalar
                def _(act):
                    ring = Ring(banks, readers)

                    def turned(n):
                        return ring.bank(n)[:].rearrange("p (k t) -> p k t", k=KD)

                    for j in pair:
                        act.wait_ge(sem["k_neg"], j + 1)
                        nc.scalar.activation(k_exp[:, j], k_neg[:, j], ACT.Exp).then_inc(sem["k_exp"], 1)
                    for j in pair:
                        act.wait_ge(sem["x_turned"], j + 1)
                        nc.scalar.copy(xnT[:, j], turned(X + j)).then_inc(sem["xnT_ready"], 1)
                    for j in pair:
                        act.wait_ge(sem["q_neg"], j + 1)
                        nc.scalar.activation(q_exp[:, j], q_neg[:, j], ACT.Exp).then_inc(sem["q_exp"], 1)
                    for j in pair:
                        act.wait_ge(sem["q_ready"], j + 1)
                        for c in range(KD):
                            nc.scalar.activation(q_sq[:, j, c, :], q_exp[:, j, c, :], ACT.Square,
                                                 accum_out=q_ss[:, j, c:c + 1]).then_inc(sem["q_ss"], 1)
                    for j in pair:
                        act.wait_ge(sem["o_done"], j + 1)
                        nc.scalar.copy(oT[:, j], turned(O + j)).then_inc(sem["o_ready"], 1)

                @block.vector
                def _(dve):
                    ring = Ring(banks, readers)
                    link = chain(dve, sem["link"])
                    ln.statistics(nc, link, lambda t: [x[:, first + t, :]])
                    dve.wait_ge(ln.rstd_ready, 1)
                    for t in range(2 * PAIR):
                        ins = nc.vector.tensor_scalar(ln.xn[:, t, :], x[:, first + t, :], ln.mv[:, t, 0:1],
                                                      ln.rstd[:, t:t + 1], ALU.subtract, ALU.mult)
                        if t % 2:
                            ins.then_inc(ln.xn_ready, 1)
                    for j in pair:
                        for t in range(2):
                            dve.wait_ge(sem["kv_done"], 2 * j + t + 1)
                            bank = ring.bank(KV + 2 * j + t)
                            nc.vector.tensor_tensor(k_raw[:, j, t, :], bank[:, 0:DIM], bkv[:, 0:DIM], ALU.add)
                            nc.vector.tensor_tensor(v[:, j, t, :], bank[:, DIM:2 * DIM], bkv[:, DIM:2 * DIM],
                                                    ALU.add).then_inc(sem["kv_read"], 1)
                        dve.wait_ge(sem["kv_read"], 2 * j + 2)
                        nc.vector.tensor_scalar(k_neg[:, j], k_raw[:, j], 0.0, None, ALU.min).then_inc(sem["k_neg"], 1)
                        dve.wait_ge(sem["k_exp"], j + 1)
                        link(nc.vector.scalar_tensor_tensor(k_exp[:, j], k_raw[:, j], 0.0, k_exp[:, j], ALU.max, ALU.add))
                        for t in range(2):
                            ins = nc.vector.tensor_scalar(k_exp[:, j, t, :], k_exp[:, j, t, :],
                                                          keep[:, bass.ds(first + 2 * j + t, 1)], None, ALU.mult)
                        link(ins)
                        link(nc.vector.tensor_tensor(k_sq[:, j], k_exp[:, j], k_exp[:, j], ALU.mult))
                        nc.vector.tensor_reduce(k_ss[:, j], k_sq[:, j].rearrange("p t (h d) -> p (t h) d", h=H), AX_X,
                                                ALU.add).then_inc(sem["k_ss"], 1)
                    for j in pair:
                        dve.wait_ge(sem["q_done"], j + 1)
                        for c in range(KD):
                            ins = nc.vector.tensor_scalar(q_raw[:, j, c, :], ring.bank(Q + j)[:, c * SEQ:(c + 1) * SEQ],
                                                          bq[:, c:c + 1], None, ALU.add)
                        ins.then_inc(sem["q_read"], 1)
                        dve.wait_ge(sem["q_read"], j + 1)
                        nc.vector.tensor_scalar(q_neg[:, j], q_raw[:, j], 0.0, None, ALU.min).then_inc(sem["q_neg"], 1)
                    for j in pair:
                        dve.wait_ge(sem["k_rn"], j + 1)
                        heads = k_exp[:, j].rearrange("p t (h d) -> p (t h) d", h=H)
                        nc.vector.tensor_tensor(heads, heads, spread(k_rn[:, j], 2, [P, 2 * H, HD]),
                                                ALU.mult).then_inc(sem["k_ready"], 1)
                        dve.wait_ge(sem["q_exp"], j + 1)
                        nc.vector.scalar_tensor_tensor(q_exp[:, j], q_raw[:, j], 0.0, q_exp[:, j], ALU.max,
                                                       ALU.add).then_inc(sem["q_ready"], 1)
                    for j in pair:
                        dve.wait_ge(sem["m_done"], j + 1)
                        dve.wait_ge(sem["q_rn"], j + 1)
                        for c in range(KD):
                            ins = nc.vector.scalar_tensor_tensor(m[:, j, c, :], ring.bank(M + j)[:, c * P:(c + 1) * P],
                                                                 q_rn[:, j, c:c + 1], C["head_blocks"][:], ALU.mult, ALU.mult)
                        ins.then_inc(sem["m_ready"], 1)
                    dve.wait_ge(sem["bias_added"], 1)
                    for j in pair:
                        dve.wait_ge(sem["y_done"], j + 1)
                        for t in range(2):
                            at = first + 2 * j + t
                            ins = nc.vector.tensor_tensor(x[:, at, :], x[:, at, :],
                                                          ring.bank(Y + j)[:, t * DIM:(t + 1) * DIM], ALU.add)
                        ins.then_inc(sem["x_ready"], 1)
            s.again()


def memory_attention(nc, x, C, D):
    PAIR = 2
    with ExitStack() as ctx:
        s = Stage(nc, ctx, "x3")
        wq, wk, wo = (s.sb(n, [P, KD, DIM]) for n in ("wq", "wk", "wo"))
        bq, bk, bo = s.sb("bq", [P, KD]), s.sb("bk", [P, KD]), s.sb("bo", [P, DIM])
        ctxT, xnT = s.sb("ctxT", [P, PAIR, KD, SEQ]), s.sb("xnT", [P, PAIR, KD, SEQ])
        load_block(nc, s, [(wq[:], D["L3_wqT"]), (wk[:], D["L3_wkT"]), (wo[:], D["L3_woT"]),
                           (bq[:], D["L3_bq_col"]), (bk[:], D["L3_bk_col"]),
                           (bo[:], D["L3_bo"].partition_broadcast(P))] +
                   [(ctxT[:, j], D["ctxT"][j]) for j in range(PAIR)])
        banks = [s.ps(f"bank{i}", [P, BANK]) for i in range(8)]
        ln = LayerNorm(s, 2 * PAIR)
        ctx_rows = s.sb("ctx_rows", [P, PAIR, 2, DIM])
        masked, mrow, ones = s.sb("masked", [1, PAIR, SEQ], U8), s.sb("mask_row", [1, PAIR, SEQ]), s.sb("ones", [1, P])
        kT, qT = s.sb("kT", [P, PAIR, KD, SEQ]), s.sb("qT", [P, PAIR, KD, SEQ])
        negmax, rsum, rinv = (s.sb(n, [P, 2 * PAIR]) for n in ("negmax", "rsum", "rinv"))
        probs, pT, oT = (s.sb(n, [P, PAIR, 2, SEQ]) for n in ("probs", "pT", "oT"))
        sem = {n: s.sem(n) for n in ("link", "ctx_landed", "rows_landed", "mask_landed", "mask_ready", "k_done",
                                     "kT_ready", "x_turned", "xnT_ready", "q_done", "qT_ready", "s_done",
                                     "max_ready", "exp_done", "p_ready", "p_turned", "pT_ready", "o_done",
                                     "oT_ready", "y_done", "bias_added", "x_ready")}
        readers = [sem[n] for n in ("kT_ready", "xnT_ready", "qT_ready", "exp_done", "pT_ready", "oT_ready", "x_ready")
                   for _ in range(PAIR)]
        K, X, Q, S, PT, O, Y = range(0, 7 * PAIR, PAIR)
        s.again()
        with nc.Fori(0, BATCH // PAIR) as p:
            with nc.Block() as block:
                first = p * 2 * PAIR
                pair = range(PAIR)

                @block.sync
                def _(sp):
                    for j in pair:
                        sp.dma_start(masked[:, j, :], D["mask_bk0"][bass.ds(p * PAIR + j, 1), :]).then_inc(sem["mask_landed"], 16)
                    for j in pair:
                        sp.dma_start(ctx_rows[:, j], D["ctx"][p * PAIR + j]).then_inc(sem["rows_landed"], 16)
                    sp.wait_ge(sem["k_done"], PAIR)
                    for j in pair:
                        sp.dma_start(ctxT[:, j], D["ctxT"][p * PAIR + PAIR + j]).then_inc(sem["ctx_landed"], 16)
                    sp.wait_ge(sem["ctx_landed"], 16 * PAIR)

                @block.gpsimd
                def _(pool):
                    ln.root(nc, pool, C["minus_half"])
                    pool.wait_ge(ln.xn_ready, PAIR)
                    for t in range(2 * PAIR):
                        ins = nc.gpsimd.tensor_tensor(x[:, first + t, :], x[:, first + t, :], bo[:], ALU.add)
                    ins.then_inc(sem["bias_added"], 1)

                @block.tensor
                def _(pe):
                    ring = Ring(banks, readers)
                    for j in pair:
                        bank = ring.claim(pe)
                        for c in range(KD):
                            for k in range(KD):
                                ins = nc.tensor.matmul(bank[:, c * SEQ:(c + 1) * SEQ], wk[:, k, c * P:(c + 1) * P],
                                                       ctxT[:, j, k, :], start=(k == 0), stop=(k == KD - 1))
                        ins.then_inc(sem["k_done"], 1)
                    for j in pair:
                        pe.wait_ge(ln.xn_ready, j + 1)
                        turn_rows(nc, ring.claim(pe), ln.xn[:, 2 * j:2 * j + 2, :], C["ident"], 2,
                                  DIM).then_inc(sem["x_turned"], 1)
                    for j in pair:
                        pe.wait_ge(sem["xnT_ready"], j + 1)
                        bank = ring.claim(pe)
                        for c in range(KD):
                            for k in range(KD):
                                ins = nc.tensor.matmul(bank[:, c * SEQ:(c + 1) * SEQ], wq[:, k, c * P:(c + 1) * P],
                                                       xnT[:, j, k, :], start=(k == 0), stop=(k == KD - 1))
                        ins.then_inc(sem["q_done"], 1)
                    pe.wait_ge(sem["mask_ready"], 1)
                    for j in pair:
                        pe.wait_ge(sem["kT_ready"], j + 1)
                        pe.wait_ge(sem["qT_ready"], j + 1)
                        bank = ring.claim(pe)
                        for t in range(2):
                            at = slice(t * SEQ, (t + 1) * SEQ)
                            nc.tensor.matmul(bank[:, at], ones[:], mrow[:, j, :], start=True, stop=False)
                            for c in range(KD):
                                ins = nc.tensor.matmul(bank[:, at], qT[:, j, c, t * P:(t + 1) * P], kT[:, j, c, :],
                                                       start=False, stop=(c == KD - 1))
                        ins.then_inc(sem["s_done"], 1)
                    for j in pair:
                        pe.wait_ge(sem["p_ready"], 2 * j + 2)
                        turn_rows(nc, ring.claim(pe), probs[:, j], C["ident"], 2, SEQ).then_inc(sem["p_turned"], 1)
                    pe.wait_ge(sem["rows_landed"], 16 * PAIR)
                    for j in pair:
                        pe.wait_ge(sem["pT_ready"], j + 1)
                        bank = ring.claim(pe)
                        for c in range(KD):
                            for k in range(2):
                                ins = nc.tensor.matmul(bank[:, c * SEQ:(c + 1) * SEQ], ctx_rows[:, j, k, c * P:(c + 1) * P],
                                                       pT[:, j, k, :], start=(k == 0), stop=(k == 1))
                        ins.then_inc(sem["o_done"], 1)
                    for j in pair:
                        pe.wait_ge(sem["oT_ready"], j + 1)
                        bank = ring.claim(pe)
                        for t in range(2):
                            for k in range(KD):
                                ins = nc.tensor.matmul(bank[:, t * DIM:(t + 1) * DIM], oT[:, j, k, t * P:(t + 1) * P],
                                                       wo[:, k, :], start=(k == 0), stop=(k == KD - 1))
                        ins.then_inc(sem["y_done"], 1)

                @block.scalar
                def _(act):
                    ring = Ring(banks, readers)

                    def turned(n):
                        return ring.bank(n)[:].rearrange("p (k t) -> p k t", k=KD)

                    def with_bias(to, n, bias, done):
                        for c in range(KD):
                            ins = nc.scalar.activation(to[:, c, :], turned(n)[:, c, :], ACT.Identity, bias=bias[:, c:c + 1])
                        ins.then_inc(done, 1)

                    for j in pair:
                        act.wait_ge(sem["k_done"], j + 1)
                        with_bias(kT[:, j], K + j, bk, sem["kT_ready"])
                    for j in pair:
                        act.wait_ge(sem["x_turned"], j + 1)
                        nc.scalar.copy(xnT[:, j], turned(X + j)).then_inc(sem["xnT_ready"], 1)
                    for j in pair:
                        act.wait_ge(sem["q_done"], j + 1)
                        with_bias(qT[:, j], Q + j, bq, sem["qT_ready"])
                    for j in pair:
                        act.wait_ge(sem["max_ready"], j + 1)
                        for t in range(2):
                            n = 2 * j + t
                            ins = nc.scalar.activation(probs[:, j, t, :], turned(S + j)[:, t, :], ACT.Exp,
                                                       bias=negmax[:, n:n + 1], accum_out=rsum[:, n:n + 1])
                        ins.then_inc(sem["exp_done"], 1)
                    for j in pair:
                        act.wait_ge(sem["p_turned"], j + 1)
                        nc.scalar.copy(pT[:, j], turned(PT + j)).then_inc(sem["pT_ready"], 1)
                    for j in pair:
                        act.wait_ge(sem["o_done"], j + 1)
                        nc.scalar.copy(oT[:, j], turned(O + j)).then_inc(sem["oT_ready"], 1)

                @block.vector
                def _(dve):
                    ring = Ring(banks, readers)
                    link = chain(dve, sem["link"])
                    ln.statistics(nc, link, lambda t: [x[:, first + t, :]])
                    dve.wait_ge(ln.rstd_ready, 1)
                    for t in range(2 * PAIR):
                        ins = nc.vector.tensor_scalar(ln.xn[:, t, :], x[:, first + t, :], ln.mv[:, t, 0:1],
                                                      ln.rstd[:, t:t + 1], ALU.subtract, ALU.mult)
                        if t % 2:
                            ins.then_inc(ln.xn_ready, 1)
                    dve.wait_ge(sem["mask_landed"], 16 * PAIR)
                    nc.vector.memset(ones[:], 1.0)
                    nc.vector.tensor_scalar(mrow[:], masked[:], MASKED, None, ALU.mult).then_inc(sem["mask_ready"], 1)
                    for j in pair:
                        dve.wait_ge(sem["s_done"], j + 1)
                        nc.vector.tensor_reduce(negmax[:, 2 * j:2 * j + 2], ring.bank(S + j)[:].rearrange(
                            "p (t k) -> p t k", t=2), AX_X, ALU.max, negate=True).then_inc(sem["max_ready"], 1)
                    for j in pair:
                        dve.wait_ge(sem["exp_done"], j + 1)
                        link(nc.vector.reciprocal(rinv[:, 2 * j:2 * j + 2], rsum[:, 2 * j:2 * j + 2]))
                        for t in range(2):
                            n = 2 * j + t
                            nc.vector.tensor_scalar(probs[:, j, t, :], probs[:, j, t, :], rinv[:, n:n + 1], None,
                                                    ALU.mult).then_inc(sem["p_ready"], 1)
                    dve.wait_ge(sem["bias_added"], 1)
                    for j in pair:
                        dve.wait_ge(sem["y_done"], j + 1)
                        for t in range(2):
                            at = first + 2 * j + t
                            ins = nc.vector.tensor_tensor(x[:, at, :], x[:, at, :],
                                                          ring.bank(Y + j)[:, t * DIM:(t + 1) * DIM], ALU.add)
                        ins.then_inc(sem["x_ready"], 1)
            s.again()


def mixture(nc, x, C, D, layer):
    gated = layer == 3
    HID = 704 if gated else 512
    FT = -(-HID // P)
    HALF = P // 2
    WHOLE = HID // P * P
    CHUNK = 4
    CHUNKS = TILES // CHUNK
    TOK = CHUNK * P
    ups = 2 if gated else 1
    up_at = [0, KD * WHOLE]
    shared_at = ups * KD * WHOLE
    b1_at = KD * HID
    down_at = shared_at + (KD * P if gated else FT)
    size = down_at + FT * DIM

    def shared(f):
        return gated and f == FT - 1

    def rows(f):
        return slice(HALF, P) if shared(f) else slice(0, P)

    with ExitStack() as ctx:
        s = Stage(nc, ctx, f"f{layer}")
        gate = s.sb("gate", [P, KD, EXPERTS])
        iota = C["iota8"]
        w_all = s.sb("w_all", [P, TILES, EXPERTS])
        xH, xL = (s.sb(n, [P, KD, TILES * P], F32R) for n in ("x_high", "x_low"))
        pairs = [(gate[:], D[f"L{layer}_gate"])]
        if not gated:
            b2 = s.sb("b2", [EXPERTS, DIM])
            pairs.append((b2[:], D["L0_b2"]))

        PAIR = 2
        STEPS = PAIR * CHUNKS
        raw = s.sb("weights_raw", [P, size])
        wH = [s.sb(f"weights_high{i}", [P, size], F32R) for i in range(PAIR)]
        wL = [s.sb(f"weights_low{i}", [P, size], F32R) for i in range(PAIR)]
        b1 = [s.sb(f"bias1_{i}", [P, FT]) for i in range(PAIR)] if not gated else None
        wcur = s.sb("gates_now", [P, TILES, PAIR])
        full = s.sb("hidden_full", [P, 2, TOK])
        hH, hL = (s.sb(n, [P, 2, FT, TOK], F32R) for n in ("hidden_high", "hidden_low"))
        silu = s.sb("silu", [P, 2, TOK])
        landed, high_done, split_done = s.sem("landed"), s.sem("high_done"), s.sem("split_done")
        gates_now, up_done, silu_done = s.sem("gates_now"), s.sem("up_done"), s.sem("silu_done")
        full_ready, high_ready, hidden_ready = s.sem("full_ready"), s.sem("high_ready"), s.sem("hidden_ready")
        down_done, added = s.sem("down_done"), s.sem("added")
        b1_of = slice(b1_at, b1_at + FT)

        def split_weights(pool, to, times):
            nc.gpsimd.tensor_copy(wH[to][:], raw[:]).then_inc(high_done, 1)
            if not gated:
                nc.gpsimd.tensor_copy(b1[to][:], raw[:, b1_of])
            pool.wait_ge(high_done, times)
            nc.gpsimd.tensor_tensor(wL[to][:], raw[:], wH[to][:].bitcast(F32), ALU.subtract).then_inc(split_done, 1)

        with ExitStack() as front:
            g = Stage(nc, front, f"g{layer}")
            xn = silu[:].rearrange("p a b -> p (a b)").rearrange("p (t d) -> p t d", d=DIM)
            ln = LayerNorm(g, TILES, out=xn)
            part = full
            ps_x = [g.ps(f"turned{k}", [P, BANK]) for k in range(KD)]
            ps_g = g.ps("logits", [P, TILES * EXPERTS])
            ps_w = g.ps("w_turned", [EXPERTS, TOK])
            ps_y = [g.ps(f"bias{t}", [P, DIM]) for t in range(CHUNK)]
            logit, prob, chosen, hot = (g.sb(n, [P, TILES, EXPERTS]) for n in ("logit", "prob", "chosen", "hot"))
            top, index, index_f = g.sb("top", [P, TILES, 8]), g.sb("index", [P, TILES, 8], U32), g.sb("index_f", [P, TILES, 8])
            peak, total, inv = g.sb("peak", [P, TILES]), g.sb("total", [P, TILES]), g.sb("inv", [P, TILES])
            wT = g.sb("wT", [EXPERTS, TOK]) if not gated else None
            sem = {n: g.sem(n) for n in ("link", "x_turned", "part_ready", "high_kept", "low_kept", "logits_done", "shifted",
                                         "exp_done", "gates_ready", "w_turned", "wT_ready", "bias_done", "x_ready",
                                         "gate_landed")}
            with nc.Block() as block:
                def chunk(c):
                    return slice(c * TOK, (c + 1) * TOK)

                @block.sync
                def _(sp):
                    for to, src in pairs:
                        sp.dma_start(to, src).then_inc(sem["gate_landed"], 16)
                    sp.dma_start(raw[:], D[f"L{layer}_experts"][0]).then_inc(landed, 16)

                @block.gpsimd
                def _(pool):
                    ln.root(nc, pool, C["minus_half"])
                    pool.wait_ge(landed, 16)
                    split_weights(pool, 0, 1)

                @block.tensor
                def _(pe):
                    for c in range(CHUNKS + 1):
                        if c < CHUNKS:
                            pe.wait_ge(ln.xn_ready, c + 1)
                            for k in range(KD):
                                if c:
                                    pe.wait_ge(sem["part_ready"], (c - 1) * KD + k + 1)
                                for t in range(CHUNK):
                                    ins = nc.tensor.transpose(ps_x[k][:, t * P:(t + 1) * P],
                                                              xn[:, t, k * P:(k + 1) * P], C["ident"][:])
                                ins.then_inc(sem["x_turned"], 1)
                        if c == 0:
                            pe.wait_ge(sem["gate_landed"], 16 * len(pairs))
                        if c:
                            pe.wait_ge(sem["part_ready"], c * KD)
                            for t in range(CHUNK):
                                at = ((c - 1) * CHUNK + t) * EXPERTS
                                for k in range(KD):
                                    ins = nc.tensor.matmul(ps_g[:, at:at + EXPERTS], part[:, k, t * P:(t + 1) * P],
                                                           gate[:, k, :], start=(k == 0), stop=(k == KD - 1))
                            ins.then_inc(sem["logits_done"], 1)
                    if not gated:
                        pe.wait_ge(sem["gates_ready"], 1)
                        for c in range(CHUNKS):
                            if c:
                                pe.wait_ge(sem["wT_ready"], c)
                            for t in range(CHUNK):
                                ins = nc.tensor.transpose(ps_w[:, t * P:(t + 1) * P], w_all[:, c * CHUNK + t, :],
                                                          C["ident"][:])
                            ins.then_inc(sem["w_turned"], 1)
                            pe.wait_ge(sem["wT_ready"], c + 1)
                            for t in range(CHUNK):
                                if c:
                                    pe.wait_ge(sem["x_ready"], (c - 1) * CHUNK + t + 1)
                                nc.tensor.matmul(ps_y[t][:], wT[:, t * P:(t + 1) * P], b2[:], start=True,
                                                 stop=True).then_inc(sem["bias_done"], 1)

                @block.scalar
                def _(act):
                    for c in range(CHUNKS):
                        for k in range(KD):
                            act.wait_ge(sem["x_turned"], c * KD + k + 1)
                            if c and k == 0:
                                act.wait_ge(sem["logits_done"], c)
                                act.wait_ge(sem["low_kept"], c)
                            nc.scalar.copy(part[:, k, :], ps_x[k][:]).then_inc(sem["part_ready"], 1)
                        act.wait_ge(sem["part_ready"], (c + 1) * KD)
                        nc.scalar.copy(xH[:, :, chunk(c)], part[:]).then_inc(sem["high_kept"], 1)
                    act.wait_ge(sem["shifted"], 1)
                    nc.scalar.activation(prob[:], logit[:], ACT.Exp).then_inc(sem["exp_done"], 1)
                    if not gated:
                        for c in range(CHUNKS):
                            act.wait_ge(sem["w_turned"], c + 1)
                            if c:
                                act.wait_ge(sem["bias_done"], c * CHUNK)
                            nc.scalar.copy(wT[:], ps_w[:]).then_inc(sem["wT_ready"], 1)

                @block.vector
                def _(dve):
                    link = chain(dve, sem["link"])
                    ln.statistics(nc, link, lambda t: [x[:, t, :]])
                    dve.wait_ge(ln.rstd_ready, 1)
                    for c in range(CHUNKS + 1):
                        if c < CHUNKS:
                            if c:
                                dve.wait_ge(sem["x_turned"], c * KD)
                            for t in range(CHUNK):
                                tile = c * CHUNK + t
                                ins = nc.vector.tensor_scalar(xn[:, t, :], x[:, tile, :], ln.mv[:, tile, 0:1],
                                                              ln.rstd[:, tile:tile + 1], ALU.subtract, ALU.mult)
                            ins.then_inc(ln.xn_ready, 1)
                        if c:
                            dve.wait_ge(sem["high_kept"], c)
                            nc.vector.tensor_tensor(xL[:, :, chunk(c - 1)], part[:], xH[:, :, chunk(c - 1)].bitcast(F32),
                                                    ALU.subtract).then_inc(sem["low_kept"], 1)
                    shape = [P, TILES, EXPERTS]
                    dve.wait_ge(sem["logits_done"], CHUNKS)
                    lg = ps_g[:].rearrange("p (t e) -> p t e", e=EXPERTS)
                    link(nc.vector.tensor_reduce(peak[:], lg, AX_X, ALU.max))
                    nc.vector.tensor_tensor(logit[:], lg, spread(peak[:], 2, shape), ALU.subtract).then_inc(sem["shifted"], 1)
                    dve.wait_ge(sem["exp_done"], 1)
                    link(nc.vector.tensor_reduce(total[:], prob[:], AX_X, ALU.add))
                    link(nc.vector.reciprocal(inv[:], total[:]))
                    link(nc.vector.tensor_tensor(prob[:], prob[:], spread(inv[:], 2, shape), ALU.mult))
                    for t in range(TILES):
                        ins = nc.vector.max(top[:, t, :], prob[:, t, :])
                    link(ins)
                    for t in range(TILES):
                        ins = nc.vector.max_index(index[:, t, :], top[:, t, :], prob[:, t, :])
                    link(ins)
                    link(nc.vector.tensor_copy(index_f[:], index[:]))
                    every = iota[:].unsqueeze(1).to_broadcast(shape)
                    nc.vector.tensor_tensor(chosen[:], every, index_f[:, :, 0:1].to_broadcast(shape), ALU.is_equal)
                    link(nc.vector.tensor_tensor(hot[:], every, index_f[:, :, 1:2].to_broadcast(shape), ALU.is_equal))
                    link(nc.vector.tensor_tensor(chosen[:], chosen[:], hot[:], ALU.add))
                    link(nc.vector.tensor_tensor(chosen[:], chosen[:], prob[:], ALU.mult))
                    link(nc.vector.tensor_reduce(total[:], chosen[:], AX_X, ALU.add))
                    if not gated:
                        link(nc.vector.tensor_scalar(total[:], total[:], 1e-12, None, ALU.max))
                    link(nc.vector.reciprocal(inv[:], total[:]))
                    nc.vector.tensor_tensor(w_all[:], chosen[:], spread(inv[:], 2, shape), ALU.mult).then_inc(
                        sem["gates_ready"], 1)
                    if not gated:
                        for tile in range(TILES):
                            dve.wait_ge(sem["bias_done"], tile + 1)
                            nc.vector.tensor_tensor(x[:, tile, :], x[:, tile, :], ps_y[tile % CHUNK][:],
                                                    ALU.add).then_inc(sem["x_ready"], 1)
            g.again()
            s.again()

        slots = 2 if gated else 4
        psU = [[s.ps(f"up{i}_{u}", [P, BANK]) for u in range(ups)] for i in range(slots)]
        psD = [s.ps(f"down{i}", [P, DIM]) for i in range(4)]
        with nc.Fori(0, EXPERTS // PAIR) as pair:
            with nc.Block() as block:
                @block.sync
                def _(sp):
                    sp.dma_start(raw[:], D[f"L{layer}_experts"][pair * PAIR + 1]).then_inc(landed, 16)
                    sp.wait_ge(split_done, 1)
                    sp.dma_start(raw[:], D[f"L{layer}_experts"][pair * PAIR + 2]).then_inc(landed, 16)

                @block.gpsimd
                def _(pool):
                    pool.wait_ge(landed, 16)
                    split_weights(pool, 1, 1)
                    pool.wait_ge(landed, 32)
                    pool.wait_ge(down_done, CHUNKS * CHUNK)
                    split_weights(pool, 0, 2)

                @block.tensor
                def _(pe):
                    def up(step):
                        e, c = divmod(step, CHUNKS)
                        if step == CHUNKS:
                            pe.wait_ge(split_done, 1)
                        for f in range(FT):
                            n = step * FT + f
                            if n >= slots:
                                pe.wait_ge(full_ready, n - slots + 1)
                            for u in range(1 if shared(f) else ups):
                                for k in range(KD):
                                    at = shared_at + k * P if shared(f) else up_at[u] + k * WHOLE + f * P
                                    tok = slice(c * TOK, (c + 1) * TOK)
                                    for i, (a, m) in enumerate(((wH, xH), (wH, xL), (wL, xH))):
                                        ins = nc.tensor.matmul(psU[n % slots][u][:], a[e][:, at:at + P], m[:, k, tok],
                                                               start=(k == 0 and i == 0), stop=(k == KD - 1 and i == 2))
                            ins.then_inc(up_done, 1)

                    def down(step):
                        e, c = divmod(step, CHUNKS)
                        pe.wait_ge(hidden_ready, (step + 1) * FT)
                        for t in range(CHUNK):
                            n = step * CHUNK + t
                            if n >= len(psD):
                                pe.wait_ge(added, n - len(psD) + 1)
                            for f in range(FT):
                                at = down_at + f * DIM
                                products = [(hH, wH), (hH, wL)] + ([] if shared(f) else [(hL, wH)])
                                for i, (h, m) in enumerate(products):
                                    ins = nc.tensor.matmul(psD[n % len(psD)][:], h[:, step % 2, f, t * P:(t + 1) * P],
                                                           m[e][:, at:at + DIM], start=(f == 0 and i == 0),
                                                           stop=(f == FT - 1 and i == len(products) - 1))
                            ins.then_inc(down_done, 1)

                    for step in range(STEPS + 1):
                        if step < STEPS:
                            up(step)
                        if step:
                            down(step - 1)

                @block.scalar
                def _(act):
                    def high(n):
                        step, f = divmod(n, FT)
                        if step >= 2:
                            act.wait_ge(down_done, (step - 1) * CHUNK)
                        act.wait_ge(full_ready, n + 1)
                        nc.scalar.copy(hH[rows(f), step % 2, f, :], full[rows(f), n % 2, :]).then_inc(high_ready, 1)

                    for n in range(STEPS * FT + 1):
                        if n < STEPS * FT:
                            act.wait_ge(up_done, n + 1)
                            if gated:
                                if n >= 2:
                                    act.wait_ge(full_ready, n - 1)
                                gate_rows = slice(0, HALF) if shared(n % FT) else slice(0, P)
                                nc.scalar.activation(silu[rows(n % FT), n % 2, :], psU[n % slots][0][gate_rows, :],
                                                     ACT.Silu).then_inc(silu_done, 1)
                            else:
                                if n >= 2:
                                    act.wait_ge(hidden_ready, n - 1)
                                nc.scalar.activation(full[:, n % 2, :], psU[n % slots][0][:], ACT.Relu,
                                                     bias=b1[n // FT // CHUNKS][:, n % FT:n % FT + 1]).then_inc(full_ready, 1)
                        if n:
                            high(n - 1)

                @block.vector
                def _(dve):
                    nc.vector.tensor_copy(wcur[:], w_all[:, :, bass.ds(pair * PAIR, PAIR)]).then_inc(gates_now, 1)
                    dve.wait_ge(gates_now, 1)

                    def product(n):
                        dve.wait_ge(silu_done, n + 1)
                        if n >= 2:
                            dve.wait_ge(hidden_ready, n - 1)
                        at = rows(n % FT)
                        bank = psU[n % slots][0 if shared(n % FT) else 1]
                        nc.vector.tensor_tensor(full[at, n % 2, :], bank[at, :], silu[at, n % 2, :],
                                                ALU.mult).then_inc(full_ready, 1)

                    def low(n):
                        step, f = divmod(n, FT)
                        dve.wait_ge(high_ready, n + 1)
                        to = hH[0:HALF, step % 2, f, :] if shared(f) else hL[:, step % 2, f, :]
                        nc.vector.tensor_tensor(to, full[rows(f), n % 2, :],
                                                hH[rows(f), step % 2, f, :].bitcast(F32),
                                                ALU.subtract).then_inc(hidden_ready, 1)

                    def add(n):
                        step, t = divmod(n, CHUNK)
                        e, c = divmod(step, CHUNKS)
                        dve.wait_ge(down_done, n + 1)
                        if n >= CHUNKS * CHUNK:
                            dve.wait_ge(added, n - CHUNKS * CHUNK + 1)
                        tile = c * CHUNK + t
                        nc.vector.scalar_tensor_tensor(x[:, tile, :], psD[n % len(psD)][:], wcur[:, tile, e:e + 1],
                                                       x[:, tile, :], ALU.mult, ALU.add).then_inc(added, 1)

                    for step in range(STEPS + 1):
                        if step < STEPS:
                            for f in range(FT):
                                n = step * FT + f
                                if gated:
                                    product(n)
                                    if n:
                                        low(n - 1)
                                else:
                                    low(n)
                        if gated and step == STEPS:
                            low(STEPS * FT - 1)
                        if step:
                            for t in range(CHUNK):
                                add((step - 1) * CHUNK + t)
            s.again()


def quantised_ffn(nc, x, C, raw):
    INNER = 1024
    KI = INNER // P
    T = 8
    GROUP = 4
    LAG = 2
    HALF = INNER // BANK
    with ExitStack() as ctx:
        s = Stage(nc, ctx, "f1")
        wg, wu, wd = s.sb("wg", [P, KD * INNER], BF16), s.sb("wu", [P, KD * INNER], BF16), s.sb("wd", [P, KI * DIM], BF16)
        mean, inv_mean = s.sb("mean", [P, 3]), s.sb("inv_mean", [P, 3])
        with ExitStack() as setup:
            g = Stage(nc, setup, "q1")
            raws = [raw[:, i * KD * INNER:(i + 1) * KD * INNER] for i in range(3)]
            sums, ones = g.sb("sums", [P, 3]), g.sb("ones", [P, P])
            ps_sum = g.ps("sum", [P, 3])
            link_sem, sums_ready, sum_done = g.sem("link"), g.sem("sums_ready"), g.sem("sum_done")
            rounded, cast = g.sem("rounded"), g.sem("cast")
            with nc.Block() as block:
                @block.tensor
                def _(pe):
                    pe.wait_ge(sums_ready, 1)
                    nc.tensor.matmul(ps_sum[:], ones[:], sums[:], start=True, stop=True).then_inc(sum_done, 1)

                @block.scalar
                def _(act):
                    for i, w in enumerate((wg, wu, wd)):
                        act.wait_ge(rounded, i + 1)
                        nc.scalar.activation(w[:], raws[i][:], ACT.Copy, bias=-ROUND).then_inc(cast, 1)

                @block.vector
                def _(dve):
                    link = chain(dve, link_sem)
                    nc.vector.memset(ones[:], 1.0)
                    for i in range(3):
                        ins = nc.vector.tensor_reduce(sums[:, i:i + 1], raws[i][:], AX_X, ALU.add,
                                                      apply_absolute_value=True)
                    ins.then_inc(sums_ready, 1)
                    dve.wait_ge(sum_done, 1)
                    link(nc.vector.tensor_scalar(mean[:], ps_sum[:], 1.0 / (INNER * DIM), QUANT_MIN, ALU.mult, ALU.max))
                    link(nc.vector.reciprocal(inv_mean[:], mean[:]))
                    for i, w in enumerate((wg, wu, wd)):
                        r = raws[i]
                        link(nc.vector.tensor_scalar(r[:], r[:], inv_mean[:, i:i + 1], 1.0, ALU.mult, ALU.min))
                        nc.vector.tensor_scalar(r[:], r[:], -1.0, ROUND, ALU.max, ALU.add).then_inc(rounded, 1)
            g.again()
        ln = LayerNorm(s, T)
        psT = [s.ps(f"turned{i}", [P, 2 * BANK], BF16) for i in range(2)]
        psG = [s.ps(f"gate{i}", [P, BANK]) for i in range(2)]
        psU = [s.ps(f"up{i}", [P, BANK]) for i in range(2)]
        psD = [s.ps(f"down{i}", [P, DIM]) for i in range(2)]
        peak, speed = s.sb("peak", [P, T]), s.sb("quant_scale", [P, T])
        gs, us = s.sb("gate_scale", [P, T]), s.sb("up_scale", [P, T])
        v = s.sb("rounding", [P, T, DIM])
        xq, xqT = s.sb("xq", [P, T, DIM], BF16), s.sb("xqT", [P, KD, T * P], BF16)
        sg = s.sb("silu", [P, 2, BANK])
        h = s.sb("h", [P, 2, INNER])
        hpeak, hspeed, hs = s.sb("h_peak", [P, T]), s.sb("h_quant_scale", [P, T]), s.sb("down_scale", [P, T])
        hq, hqT = s.sb("hq", [P, 2, INNER], BF16), s.sb("hqT", [P, 2, KI, P], BF16)
        sem = {n: s.sem(n) for n in ("link", "xq_ready", "x_turned", "xqT_ready", "up_done", "silu_done", "h_ready",
                                     "h_rounded", "hq_ready", "h_turned", "hqT_ready", "down_done", "x_ready")}
        with nc.Fori(0, TILES // T) as c:
            with nc.Block() as block:
                def parts(t):
                    return [x[:, c * T + t, :]]

                @block.gpsimd
                def _(pool):
                    ln.root(nc, pool, C["minus_half"])

                @block.tensor
                def _(pe):
                    def turn_group(g):
                        pe.wait_ge(sem["xq_ready"], g + 1)
                        if g:
                            pe.wait_ge(sem["xqT_ready"], g)
                        for k in range(KD):
                            for i in range(GROUP):
                                at, t = (k * GROUP + i) * P, g * GROUP + i
                                ins = nc.tensor.transpose(psT[0][:, at:at + P], xq[:, t, k * P:(k + 1) * P],
                                                          C["ident_bf"][:])
                        ins.then_inc(sem["x_turned"], 1)

                    def gate_up(t):
                        for n in range(HALF):
                            u = t * HALF + n
                            if u >= 2:
                                pe.wait_ge(sem["h_ready"], u - 1)
                            for w, ps in ((wg, psG), (wu, psU)):
                                for k in range(KD):
                                    at = k * INNER + n * BANK
                                    ins = nc.tensor.matmul(ps[u % 2][:], xqT[:, k, t * P:(t + 1) * P],
                                                           w[:, at:at + BANK], start=(k == 0), stop=(k == KD - 1))
                            ins.then_inc(sem["up_done"], 1)

                    def down(t):
                        pe.wait_ge(sem["hq_ready"], t + 1)
                        if t >= 1:
                            pe.wait_ge(sem["hqT_ready"], t)
                        for k in range(KI):
                            ins = nc.tensor.transpose(psT[1][:, k * P:(k + 1) * P], hq[:, t % 2, k * P:(k + 1) * P],
                                                      C["ident_bf"][:])
                        ins.then_inc(sem["h_turned"], 1)
                        pe.wait_ge(sem["hqT_ready"], t + 1)
                        if t >= 2:
                            pe.wait_ge(sem["x_ready"], t - 1)
                        for k in range(KI):
                            ins = nc.tensor.matmul(psD[t % 2][:], hqT[:, t % 2, k, :], wd[:, k * DIM:(k + 1) * DIM],
                                                   start=(k == 0), stop=(k == KI - 1))
                        ins.then_inc(sem["down_done"], 1)

                    turn_group(0)
                    for t in range(T + LAG):
                        if t < T:
                            if t % GROUP == 0:
                                pe.wait_ge(sem["xqT_ready"], t // GROUP + 1)
                            gate_up(t)
                            if t % GROUP == 0 and t + GROUP < T:
                                turn_group(t // GROUP + 1)
                        if t >= LAG:
                            down(t - LAG)

                @block.scalar
                def _(act):
                    def keep_group(g):
                        act.wait_ge(sem["x_turned"], g + 1)
                        nc.scalar.copy(xqT[:, :, g * GROUP * P:(g + 1) * GROUP * P],
                                       psT[0][:].rearrange("p (k t) -> p k t", k=KD)).then_inc(sem["xqT_ready"], 1)

                    keep_group(0)
                    for t in range(T + LAG):
                        if t < T:
                            for n in range(HALF):
                                u = t * HALF + n
                                act.wait_ge(sem["up_done"], u + 1)
                                if u >= 2:
                                    act.wait_ge(sem["h_ready"], u - 1)
                                nc.scalar.activation(sg[:, u % 2, :], psG[u % 2][:], ACT.Silu,
                                                     scale=gs[:, t:t + 1]).then_inc(sem["silu_done"], 1)
                            if t % GROUP == 0 and t + GROUP < T:
                                keep_group(t // GROUP + 1)
                        q = t - 1
                        if 0 <= q < T:
                            act.wait_ge(sem["h_rounded"], q + 1)
                            if q >= 2:
                                act.wait_ge(sem["h_turned"], q - 1)
                            nc.scalar.activation(hq[:, q % 2, :], h[:, q % 2, :], ACT.Copy,
                                                 bias=-ROUND).then_inc(sem["hq_ready"], 1)
                        d = t - LAG
                        if d >= 0:
                            act.wait_ge(sem["h_turned"], d + 1)
                            if d >= 2:
                                act.wait_ge(sem["down_done"], d - 1)
                            nc.scalar.copy(hqT[:, d % 2, :, :],
                                           psT[1][:].rearrange("p (k t) -> p k t", k=KI)).then_inc(sem["hqT_ready"], 1)

                @block.vector
                def _(dve):
                    link = chain(dve, sem["link"])
                    ln.statistics(nc, link, parts)
                    ln.apply(nc, dve, parts)
                    dve.wait_ge(ln.xn_ready, 1)
                    for g in range(T // GROUP):
                        at = slice(g * GROUP, (g + 1) * GROUP)
                        link(nc.vector.tensor_reduce(peak[:, at], ln.xn[:, at, :], AX_X, ALU.max, apply_absolute_value=True))
                        link(nc.vector.tensor_scalar(peak[:, at], peak[:, at], QUANT_MIN, None, ALU.max))
                        link(nc.vector.reciprocal(speed[:, at], peak[:, at]))
                        nc.vector.tensor_scalar(gs[:, at], peak[:, at], mean[:, 0:1], 1.0 / 127.0, ALU.mult, ALU.mult)
                        nc.vector.tensor_scalar(us[:, at], peak[:, at], mean[:, 1:2], 1.0 / 127.0, ALU.mult, ALU.mult)
                        link(nc.vector.tensor_scalar(speed[:, at], speed[:, at], 127.0, None, ALU.mult))
                        for t in range(at.start, at.stop):
                            ins = nc.vector.tensor_scalar(v[:, t, :], ln.xn[:, t, :], speed[:, t:t + 1], 127.0, ALU.mult,
                                                          ALU.min)
                        link(ins)
                        link(nc.vector.tensor_scalar(v[:, at, :], v[:, at, :], -128.0, ROUND, ALU.max, ALU.add))
                        nc.vector.tensor_scalar(xq[:, at, :], v[:, at, :], -ROUND, None, ALU.add).then_inc(sem["xq_ready"], 1)

                    def product(t):
                        for n in range(HALF):
                            u = t * HALF + n
                            dve.wait_ge(sem["silu_done"], u + 1)
                            nc.vector.scalar_tensor_tensor(h[:, t % 2, n * BANK:(n + 1) * BANK], psU[u % 2][:],
                                                           us[:, t:t + 1], sg[:, u % 2, :], ALU.mult,
                                                           ALU.mult).then_inc(sem["h_ready"], 1)

                    def quantise(t):
                        hh, at = h[:, t % 2, :], slice(t, t + 1)
                        dve.wait_ge(sem["h_ready"], (t + 1) * HALF)
                        link(nc.vector.tensor_reduce(hpeak[:, at], hh, AX_X, ALU.max, apply_absolute_value=True))
                        link(nc.vector.tensor_scalar(hpeak[:, at], hpeak[:, at], QUANT_MIN, None, ALU.max))
                        link(nc.vector.reciprocal(hspeed[:, at], hpeak[:, at]))
                        nc.vector.tensor_scalar(hs[:, at], hpeak[:, at], mean[:, 2:3], 1.0 / 127.0, ALU.mult, ALU.mult)
                        link(nc.vector.tensor_scalar(hspeed[:, at], hspeed[:, at], 127.0, None, ALU.mult))
                        link(nc.vector.tensor_scalar(hh, hh, hspeed[:, at], 127.0, ALU.mult, ALU.min))
                        nc.vector.tensor_scalar(hh, hh, -128.0, ROUND, ALU.max, ALU.add).then_inc(sem["h_rounded"], 1)

                    def add(t):
                        dve.wait_ge(sem["down_done"], t + 1)
                        nc.vector.scalar_tensor_tensor(x[:, c * T + t, :], psD[t % 2][:], hs[:, t:t + 1],
                                                       x[:, c * T + t, :], ALU.mult, ALU.add).then_inc(sem["x_ready"], 1)

                    for t in range(T + LAG):
                        if t < T:
                            if t >= 2:
                                dve.wait_ge(sem["hq_ready"], t - 1)
                            product(t)
                            quantise(t)
                        if t >= LAG:
                            add(t - LAG)
            s.again()


def shift_rows(sp, y, shifted, landed):
    sp.dma_start(shifted[1:P, :, :], y[0:P - 1, :, P:DIM]).then_inc(landed, 16)
    sp.dma_start(shifted[0:1, 1:TILES:2, :], y[P - 1:P, 0:TILES:2, P:DIM]).then_inc(landed, 16)
    sp.wait_ge(landed, 32)


def local_attention_block(nc, x, C, D):
    DEPTH, H, HD, HID = 2, 8, 64, 682
    FT = -(-HID // P)
    with ExitStack() as ctx:
        s = Stage(nc, ctx, "f2")
        y, shifted = s.sb("y", [P, TILES, DIM]), s.sb("shifted", [P, TILES, P])
        set_done = s.sem("set_done")
        weights, gelu_weights = AttentionWeights(s, H, HD), GeluWeights(s, FT)
        loaded = s.sem("loaded")
        with ExitStack() as front:
            g = Stage(nc, front, "n2")
            ln = LayerNorm(g, TILES, out=y)
            link_sem = g.sem("link")
            with nc.Block() as block:
                def parts(t):
                    return [x[:, t, :]]

                @block.sync
                def _(sp):
                    pairs = weights.pairs(D, 0)
                    for to, src in pairs:
                        sp.dma_start(to, src).then_inc(loaded, 16)
                    sp.wait_ge(loaded, 16 * len(pairs))

                @block.gpsimd
                def _(pool):
                    ln.root(nc, pool, C["minus_half"])

                @block.vector
                def _(dve):
                    link = chain(dve, link_sem)
                    nc.vector.memset(shifted[:], 0.0).then_inc(set_done, 1)
                    ln.statistics(nc, link, parts)
                    ln.apply(nc, dve, parts)
                    dve.wait_ge(set_done, 1)
            g.again()
        s.again()
        with nc.Fori(0, DEPTH) as layer:
            local_attention(nc, C, y, shifted, weights, H, HD, gelu_weights.pairs(D, layer))
            gelu_ffn(nc, C, y, shifted, gelu_weights, FT, weights.pairs(D, layer + 1))
        with nc.Block() as block:
            @block.vector
            def _(dve):
                nc.vector.tensor_tensor(x[:], x[:], y[:], ALU.add).then_inc(set_done, 1)
                dve.wait_ge(set_done, 1)
        s.again()


class AttentionWeights:

    def __init__(self, s, H, HD):
        INNER = H * HD
        self.wqkv, self.wo = s.sb("wqkv", [P, KD, 3 * INNER]), s.sb("wo", [P, INNER // P, DIM])
        self.scale = s.sb("scale", [P, 4, HD])

    def pairs(self, D, layer):
        return [(self.wqkv[:], D["L2_wqkv"][layer]), (self.wo[:], D["L2_wo"][layer]),
                (self.scale[:], D["L2_qk_scale"][layer].partition_broadcast(P))]


def local_attention(nc, C, y, shifted, weights, H, HD, prefetch):
    INNER = H * HD
    KI = INNER // P
    with ExitStack() as ctx:
        s = Stage(nc, ctx, "a2")
        wqkv, wo, scale = weights.wqkv, weights.wo, weights.scale
        wqkvH, wqkvL = (s.sb(n, [P, KD, 3 * INNER], F32R) for n in ("wqkv_high", "wqkv_low"))
        woH, woL = (s.sb(n, [P, KI, DIM], F32R) for n in ("wo_high", "wo_low"))
        w_high, cleared, shift_landed = s.sem("w_high"), s.sem("cleared"), s.sem("shift_landed")
        tables = s.sb("tables", [P, 2, 2, 2, HD])
        psA = [s.ps(f"work{i}", [P, BANK]) for i in range(2)]
        att = Attention(s, H, HD, "halves")
        link0 = s.sem("tables_link")
        with nc.Block() as block:
            @block.sync
            def _(sp):
                shift_rows(sp, y, shifted, shift_landed)

            @block.gpsimd
            def _(pool):
                att.clear(nc, pool, cleared)

            @block.scalar
            def _(act):
                for k in range(KD):
                    nc.scalar.copy(wqkvH[:, k, :], wqkv[:, k, :]).then_inc(w_high, 1)
                nc.scalar.copy(woH[:], wo[:]).then_inc(w_high, 1)

            @block.vector
            def _(dve):
                link = chain(dve, link0)
                for w, which in enumerate(("q", "k")):
                    for f, fn in enumerate(("cos", "sin")):
                        ins = nc.vector.tensor_tensor(tables[:, w, f], C[f"xpos_{fn}_{which}"][:],
                                                      spread(scale[:, 2 * w + f, :], 1, [P, 2, HD]), ALU.mult)
                link(ins)
                for k in range(KD):
                    dve.wait_ge(w_high, k + 1)
                    nc.vector.tensor_tensor(wqkvL[:, k, :], wqkv[:, k, :], wqkvH[:, k, :].bitcast(F32), ALU.subtract)
                dve.wait_ge(w_high, KD + 1)
                link(nc.vector.tensor_tensor(woL[:], wo[:], woH[:].bitcast(F32), ALU.subtract))
        s.again()
        h = s.sb("h", [P, 2, DIM])
        hH, hL = (s.sb(n, [P, KD, SEQ], F32R) for n in ("hT_high", "hT_low"))
        raw = s.sb("raw", [P, 2, 2, INNER])
        vr = s.sb("v_raw", [P, 2, INNER])
        sq = s.sb("squares", [P, 2, INNER])
        ss, rn = s.sb("sum_squares", [P, 2, 2 * H]), s.sb("inv_norm", [P, 2, 2 * H])
        rot = s.sb("rotated", [P, 2, H, HD])
        oH, oL = (s.sb(n, [P, KI, SEQ], F32R) for n in ("oT_high", "oT_low"))
        sem = {n: s.sem(n) for n in ("link", "h_ready", "h_turned", "qkv_done", "by_act", "by_dve", "squared",
                                     "ss_ready", "bounded", "rn_ready", "normalised", "o_turned", "out_done", "prefetched", "turned_high", "turned_low")}
        T_HIGH, T_LOW = sem["turned_high"], sem["turned_low"]
        A, V = sem["by_act"], sem["by_dve"]
        QKV = 6
        turn_o = KI * SEQ // BANK
        STEPS = H + 3

        def turn(front, core, tail):
            turned_h = 1 if front is not None else 0
            turned_o = turn_o if tail is not None else 0
            att.owed = 1 if tail is not None else 0
            made = QKV if front is not None else 0
            readers = [T_LOW] * (turned_h + turned_o) + [A] * made + [V, V]
            USE_QKV, USE_OUT = turned_h + turned_o, turned_h + turned_o + made
            USE_O, USE_H = (0, 1 + turned_h), min(turned_o, 1)
            with nc.Block() as block:
                @block.sync
                def _(sp):
                    if front is not None and core is None:
                        for to, src in prefetch:
                            sp.dma_start(to, src).then_inc(sem["prefetched"], 16)
                        sp.wait_ge(sem["prefetched"], 16 * len(prefetch))

                @block.gpsimd
                def _(pool):
                    if front is None:
                        return
                    nc.gpsimd.tensor_copy(h[:, :, 0:P], y[:, bass.ds(front, 2), 0:P])
                    nc.gpsimd.tensor_copy(h[:, :, P:DIM], shifted[:, bass.ds(front, 2), :]).then_inc(sem["h_ready"], 1)
                    for w in range(2):
                        pool.wait_ge(sem["ss_ready"], w + 1)
                        nc.gpsimd.tensor_scalar(ss[:, w, :], ss[:, w, :], TINY_SQ, None, ALU.max).then_inc(sem["bounded"], 1)
                        pool.wait_ge(sem["bounded"], w + 1)
                        nc.gpsimd.tensor_tensor(rn[:, w, :], ss[:, w, :], C["minus_half"][:, 0:2 * H],
                                                ALU.pow).then_inc(sem["rn_ready"], 1)
                        pool.wait_ge(sem["rn_ready"], w + 1)
                        rows = raw[:, w].rearrange("p t (h d) -> p (t h) d", h=H)
                        nc.gpsimd.tensor_tensor(rows, rows, spread(rn[:, w, :], 2, [P, 2 * H, HD]),
                                                ALU.mult).then_inc(sem["normalised"], 1)

                @block.tensor
                def _(pe):
                    ring = Ring(psA, readers)

                    def beside(step):
                        if step in (-1, 0) and tail is not None:
                            if step == -1:
                                pe.wait_ge(att.o_ready, 1)
                            bank = ring.claim(pe)
                            for i in range(2):
                                k = (step + 1) * 2 + i
                                for t in range(2):
                                    at = (i * 2 + t) * P
                                    src = att.o_rows[:, t, 2 * k:2 * k + 2, :].rearrange("p h d -> p (h d)")
                                    ins = nc.tensor.transpose(bank[:, at:at + P], src, C["ident"][:])
                            ins.then_inc(sem["o_turned"], 1)
                        if step == -1 and front is not None:
                            pe.wait_ge(sem["h_ready"], 1)
                            turn_rows(nc, ring.claim(pe), h, C["ident"], 2, DIM).then_inc(sem["h_turned"], 1)
                        if 0 <= step < QKV and front is not None:
                            if step == 0:
                                pe.wait_ge(T_LOW, min(turned_o, 1) + turned_h)
                            part, t = (1, 0, 2)[step // 2], step % 2
                            bank = ring.claim(pe)
                            for k in range(KD):
                                for i, (hi, wi) in enumerate(((hH, wqkvH), (hL, wqkvH), (hH, wqkvL))):
                                    ins = nc.tensor.matmul(bank[:], hi[:, k, t * P:(t + 1) * P],
                                                           wi[:, k, part * INNER:(part + 1) * INNER],
                                                           start=(k == 0 and i == 0), stop=(k == KD - 1 and i == 2))
                            ins.then_inc(sem["qkv_done"], 1)
                        if step in (QKV + 1, QKV + 2) and tail is not None:
                            t = step - QKV - 1
                            if t == 0:
                                pe.wait_ge(T_LOW, turned_o + turned_h)
                            bank = ring.claim(pe)
                            for k in range(KI):
                                for i, (oi, wi) in enumerate(((oH, woH), (oL, woH), (oH, woL))):
                                    ins = nc.tensor.matmul(bank[:, 0:DIM], oi[:, k, t * P:(t + 1) * P], wi[:, k, :],
                                                           start=(k == 0 and i == 0), stop=(k == KI - 1 and i == 2))
                            ins.then_inc(sem["out_done"], 1)

                    if core is None:
                        for step in range(-1, STEPS):
                            beside(step)
                    else:
                        att.tensor(nc, pe, C, lambda h: C["local"][:], beside)

                @block.scalar
                def _(act):
                    ring = Ring(psA, readers)

                    def beside(step):
                        if step == -1 and core is not None:
                            nc.scalar.copy(att.v_rows[:, :, :, 0:HD],
                                           vr[:].rearrange("p t (h d) -> p t h d", h=H)).then_inc(att.v_ready, 1)
                        if step in (-1, 0) and tail is not None:
                            n = step + 1
                            act.wait_ge(sem["o_turned"], n + 1)
                            nc.scalar.copy(oH[:, 2 * n:2 * n + 2, :],
                                           ring.bank(USE_O[n])[:].rearrange("p (k t) -> p k t", k=2)).then_inc(T_HIGH, 1)
                        if step == -1 and front is not None:
                            act.wait_ge(sem["h_turned"], 1)
                            nc.scalar.copy(hH[:], ring.bank(USE_H)[:].rearrange("p (k t) -> p k t", k=KD)).then_inc(T_HIGH, 1)
                        n = step
                        if 0 <= n < 4 and front is not None:
                            w, t = n // 2, n % 2
                            act.wait_ge(sem["qkv_done"], n + 1)
                            nc.scalar.copy(raw[:, w, t, :], ring.bank(USE_QKV + n)[:]).then_inc(A, 1)
                            act.wait_ge(A, n + 1)
                            if n == 2:
                                act.wait_ge(sem["ss_ready"], 1)
                            nc.scalar.activation(sq[:, t, :], raw[:, w, t, :], ACT.Square).then_inc(sem["squared"], 1)
                        if 4 <= n < QKV and front is not None:
                            act.wait_ge(sem["qkv_done"], n + 1)
                            if core is not None and n == 4:
                                act.wait_ge(att.v_ready, 1)
                            nc.scalar.copy(vr[:, n - 4, :], ring.bank(USE_QKV + n)[:]).then_inc(A, 1)

                    if core is None:
                        for step in range(-1, STEPS):
                            beside(step)
                    else:
                        att.scalar(nc, act, beside)

                @block.vector
                def _(dve):
                    ring = Ring(psA, readers)
                    link = chain(dve, sem["link"])

                    def sum_squares(w):
                        dve.wait_ge(sem["squared"], 2 * w + 2)
                        nc.vector.tensor_reduce(ss[:, w, :], sq[:].rearrange("p t (h d) -> p (t h) d", h=H), AX_X,
                                                ALU.add).then_inc(sem["ss_ready"], 1)

                    def by_position(w, to, t):
                        dve.wait_ge(sem["normalised"], w + 1)
                        r = raw[:, w, t, :].rearrange("p (h d) -> p h d", h=H)
                        cos, sin = tables[:, 1 - w, 0, t, :], tables[:, 1 - w, 1, t, :]
                        half = HD // 2
                        nc.vector.tensor_tensor(rot[:, t, :, 0:half], r[:, :, half:HD],
                                                spread(sin[:, 0:half], 1, [P, H, half]), ALU.mult)
                        nc.vector.tensor_tensor(rot[:, t, :, half:HD], r[:, :, 0:half],
                                                spread(sin[:, half:HD], 1, [P, H, half]), ALU.mult)
                        link(nc.vector.tensor_tensor(to[:, t, :, 0:HD], r, spread(cos, 1, [P, H, HD]), ALU.mult))
                        link(nc.vector.tensor_tensor(to[:, t, :, 0:HD], to[:, t, :, 0:HD], rot[:, t], ALU.add))

                    def beside(step):
                        if step in (-1, 0) and tail is not None:
                            n = step + 1
                            dve.wait_ge(T_HIGH, n + 1 if n == 0 else n + 1 + turned_h)
                            at = slice(2 * n, 2 * n + 2)
                            nc.vector.tensor_tensor(oL[:, at, :], ring.bank(USE_O[n])[:].rearrange("p (k t) -> p k t", k=2),
                                                    oH[:, at, :].bitcast(F32), ALU.subtract).then_inc(T_LOW, 1)
                        if step == -1 and front is not None:
                            dve.wait_ge(T_HIGH, min(turned_o, 1) + 1)
                            nc.vector.tensor_tensor(hL[:], ring.bank(USE_H)[:].rearrange("p (k t) -> p k t", k=KD),
                                                    hH[:].bitcast(F32), ALU.subtract).then_inc(T_LOW, 1)
                        if step in (8, 9) and tail is not None:
                            t = step - 8
                            dve.wait_ge(sem["out_done"], t + 1)
                            nc.vector.tensor_tensor(y[:, tail + t, :], y[:, tail + t, :],
                                                    ring.bank(USE_OUT + t)[:, 0:DIM], ALU.add).then_inc(V, 1)
                        if front is None:
                            return
                        if step == 2:
                            sum_squares(0)
                        if step == 4:
                            sum_squares(1)
                        if step in (5, 6):
                            if core is not None:
                                dve.wait_ge(att.rows_turned, 2 * att.banks)
                            by_position(0, att.k_rows, step - 5)
                        if step in (7, 8):
                            by_position(1, att.q_rows, step - 7)

                    if core is None:
                        att.settle(nc, dve, link)
                        for step in range(-1, STEPS):
                            beside(step)
                    else:
                        att.vector(nc, dve, link, beside)
            s.again()

        turn(0, None, None)
        turn(2, 0, None)
        with nc.Fori(0, BATCH - 2) as b:
            turn(b * 2 + 4, b * 2 + 2, b * 2)
        turn(None, 2 * (BATCH - 1), 2 * (BATCH - 2))
        turn(None, None, 2 * (BATCH - 1))


class GeluWeights:

    def __init__(self, s, FT):
        self.w1, self.w2 = s.sb("w1", [P, KD, 2 * (FT - 1) * P + P]), s.sb("w2", [P, FT, DIM])
        self.b1, self.b2 = s.sb("b1", [P, 2, FT]), s.sb("b2", [P, DIM])
        self.gain, self.bias = s.sb("ln_gain", [P, KD]), s.sb("ln_bias", [P, KD])

    def pairs(self, D, layer):
        return [(self.w1[:], D["L2_w1"][layer]), (self.w2[:], D["L2_w2"][layer]), (self.b1[:], D["L2_b1"][layer]),
                (self.b2[:], D["L2_b2"][layer].partition_broadcast(P)), (self.gain[:], D["L2_ln_g"][layer]),
                (self.bias[:], D["L2_ln_b"][layer])]


def gelu_ffn(nc, C, y, shifted, w, FT, prefetch):
    T = 4
    HALF = P // 2
    WHOLE = (FT - 1) * P

    def shared(f):
        return f == FT - 1

    def rows(f):
        return slice(HALF, P) if shared(f) else slice(0, P)

    TOK = T * P
    with ExitStack() as ctx:
        s = Stage(nc, ctx, "g2")
        ln = LayerNorm(s, T, 2)
        ps_x = [s.ps(f"turned{k}", [P, BANK]) for k in range(KD)]
        psU = [[s.ps(f"up{i}_{u}", [P, BANK]) for u in range(2)] for i in range(2)]
        psD = [s.ps(f"down{i}", [P, DIM]) for i in range(2)]
        w1H, w1L = (s.sb(n, [P, KD, 2 * WHOLE + P], F32R) for n in ("w1_high", "w1_low"))
        w2H, w2L = (s.sb(n, [P, FT, DIM], F32R) for n in ("w2_high", "w2_low"))
        turned = s.sb("turned", [P, KD, TOK])
        hH, hL = (s.sb(n, [P, KD, TOK], F32R) for n in ("h_high", "h_low"))
        gelu = s.sb("gelu", [P, 2, TOK])
        hidden = s.sb("hidden", [P, 2, TOK])
        hidH, hidL = (s.sb(n, [P, FT, TOK], F32R) for n in ("hidden_high", "hidden_low"))
        sem = {n: s.sem(n) for n in ("link", "x_turned", "h_staged", "h_high", "h_low", "up_done", "gelu_done",
                                     "hidden_made", "hidden_high", "hidden_low", "down_done", "bias_added", "y_ready",
                                     "w_high", "w_low", "prefetched", "shift_landed")}

        with nc.Block() as block:
            @block.sync
            def _(sp):
                shift_rows(sp, y, shifted, sem["shift_landed"])

            @block.scalar
            def _(act):
                for k in range(KD):
                    nc.scalar.copy(w1H[:, k, :], w.w1[:, k, :]).then_inc(sem["w_high"], 1)
                nc.scalar.copy(w2H[:], w.w2[:]).then_inc(sem["w_high"], 1)

            @block.vector
            def _(dve):
                for k in range(KD):
                    dve.wait_ge(sem["w_high"], k + 1)
                    nc.vector.tensor_tensor(w1L[:, k, :], w.w1[:, k, :], w1H[:, k, :].bitcast(F32), ALU.subtract)
                dve.wait_ge(sem["w_high"], KD + 1)
                nc.vector.tensor_tensor(w2L[:], w.w2[:], w2H[:].bitcast(F32), ALU.subtract).then_inc(sem["w_low"], 1)
        s.again()

        def turn(front, core):
            with nc.Block() as block:
                @block.sync
                def _(sp):
                    if core is None:
                        for to, src in prefetch:
                            sp.dma_start(to, src).then_inc(sem["prefetched"], 16)
                        sp.wait_ge(sem["prefetched"], 16 * len(prefetch))

                def parts(t):
                    return [y[:, front + t, 0:P], shifted[:, front + t, :]]

                @block.gpsimd
                def _(pool):
                    if front is not None:
                        ln.root(nc, pool, C["minus_half"])
                    if core is not None:
                        for t in range(T):
                            ins = nc.gpsimd.tensor_tensor(y[:, core + t, :], y[:, core + t, :], w.b2[:], ALU.add)
                        ins.then_inc(sem["bias_added"], 1)

                @block.tensor
                def _(pe):
                    for f in range(FT if core is not None else 0):
                        if f >= 2:
                            pe.wait_ge(sem["hidden_made"], f - 1)
                        for u in (1,) if shared(f) else (1, 0):
                            first = 2 * WHOLE if shared(f) else u * WHOLE + f * P
                            at = slice(first, first + P)
                            for k in range(KD):
                                for i, (wi, hi) in enumerate(((w1H, hH), (w1L, hH), (w1H, hL))):
                                    ins = nc.tensor.matmul(psU[f % 2][u][:], wi[:, k, at], hi[:, k, :],
                                                           start=(k == 0 and i == 0), stop=(k == KD - 1 and i == 2))
                        ins.then_inc(sem["up_done"], 1)
                    if front is not None:
                        pe.wait_ge(ln.xn_ready, 1)
                        for k in range(KD):
                            for t in range(T):
                                ins = nc.tensor.transpose(ps_x[k][:, t * P:(t + 1) * P], ln.xn[:, t, k * P:(k + 1) * P],
                                                          C["ident"][:])
                            ins.then_inc(sem["x_turned"], 1)
                    if core is not None:
                        for t in range(T):
                            if t >= 2:
                                pe.wait_ge(sem["y_ready"], t - 1)
                            at = slice(t * P, (t + 1) * P)
                            for f in range(FT):
                                if t == 0:
                                    pe.wait_ge(sem["hidden_low"], f + 1)
                                products = [(hidH, w2H), (hidH, w2L)] + ([] if shared(f) else [(hidL, w2H)])
                                for i, (hi, wi) in enumerate(products):
                                    ins = nc.tensor.matmul(psD[t % 2][:], hi[:, f, at], wi[:, f, :],
                                                           start=(f == 0 and i == 0),
                                                           stop=(f == FT - 1 and i == len(products) - 1))
                            ins.then_inc(sem["down_done"], 1)

                @block.scalar
                def _(act):
                    def keep_high(f):
                        act.wait_ge(sem["hidden_made"], f + 1)
                        nc.scalar.copy(hidH[rows(f), f, :], hidden[rows(f), f % 2, :]).then_inc(sem["hidden_high"], 1)

                    if core is not None:
                        for f in range(FT):
                            act.wait_ge(sem["up_done"], f + 1)
                            if f >= 2:
                                act.wait_ge(sem["hidden_made"], f - 1)
                            gate_rows = slice(0, HALF) if shared(f) else slice(0, P)
                            nc.scalar.activation(gelu[rows(f), f % 2, :], psU[f % 2][1][gate_rows, :], ACT.Gelu,
                                                 bias=w.b1[gate_rows, 1, f:f + 1]).then_inc(sem["gelu_done"], 1)
                            if f:
                                keep_high(f - 1)
                        keep_high(FT - 1)
                    if front is not None:
                        if core is not None:
                            act.wait_ge(sem["up_done"], FT)
                        for k in range(KD):
                            act.wait_ge(sem["h_staged"], k + 1)
                            nc.scalar.copy(hH[:, k, :], turned[:, k, :]).then_inc(sem["h_high"], 1)

                @block.vector
                def _(dve):
                    link = chain(dve, sem["link"])

                    def keep_low(f):
                        dve.wait_ge(sem["hidden_high"], f + 1)
                        to = hidH[0:HALF, f, :] if shared(f) else hidL[:, f, :]
                        nc.vector.tensor_tensor(to, hidden[rows(f), f % 2, :], hidH[rows(f), f, :].bitcast(F32),
                                                ALU.subtract).then_inc(sem["hidden_low"], 1)

                    if front is not None:
                        ln.statistics(nc, link, parts)
                        if core is None:
                            ln.apply(nc, dve, parts)
                    for f in range(FT if core is not None else 0):
                        dve.wait_ge(sem["gelu_done"], f + 1)
                        if f >= 2:
                            dve.wait_ge(sem["hidden_low"], f - 1)
                        at, bank = rows(f), psU[f % 2][1 if shared(f) else 0]
                        nc.vector.scalar_tensor_tensor(hidden[at, f % 2, :], bank[at, :], w.b1[at, 0, f:f + 1],
                                                       gelu[at, f % 2, :], ALU.add, ALU.mult).then_inc(sem["hidden_made"], 1)
                        if f:
                            keep_low(f - 1)
                        if f == 1 and front is not None:
                            ln.apply(nc, dve, parts)
                    if core is not None:
                        keep_low(FT - 1)
                    if front is not None:
                        for k in range(KD):
                            dve.wait_ge(sem["x_turned"], k + 1)
                            nc.vector.tensor_scalar(turned[:, k, :], ps_x[k][:], w.gain[:, k:k + 1], w.bias[:, k:k + 1],
                                                    ALU.mult, ALU.add).then_inc(sem["h_staged"], 1)
                        for k in range(KD):
                            dve.wait_ge(sem["h_high"], k + 1)
                            nc.vector.tensor_tensor(hL[:, k, :], turned[:, k, :], hH[:, k, :].bitcast(F32),
                                                    ALU.subtract).then_inc(sem["h_low"], 1)
                    if core is not None:
                        dve.wait_ge(sem["bias_added"], 1)
                        for t in range(T):
                            dve.wait_ge(sem["down_done"], t + 1)
                            nc.vector.tensor_tensor(y[:, core + t, :], y[:, core + t, :], psD[t % 2][:],
                                                    ALU.add).then_inc(sem["y_ready"], 1)
            s.again()

        turn(0, None)
        with nc.Fori(0, TILES // T - 1) as c:
            turn(c * T + T, c * T)
        turn(None, TILES - T)


def constants():
    bf = mybir.dt.np(BF16)
    p = np.arange(P)
    c = {}
    c["ident"] = np.eye(P, dtype=np.float32)
    c["ident_bf"] = np.eye(P).astype(bf)

    def masks(allowed):
        q, k = p[:, None], p[None, :]
        m = np.concatenate([allowed(q, k), allowed(q + P, k), allowed(q + P, k + P)], 1)
        return np.where(m, 0.0, MASKED).astype(bf)

    c["causal"] = masks(lambda q, k: k <= q)
    c["window"] = masks(lambda q, k: (k <= q) & (k >= q - 62))
    c["local"] = masks(lambda q, k: (k <= q) & (q <= k + P))
    c["head_blocks"] = (p[:, None] // 16 == p[None, :] // 16).astype(np.float32)
    c["iota8"] = np.tile(np.arange(EXPERTS, dtype=np.float32), (P, 1))
    t = np.arange(SEQ, dtype=np.float32)

    def by_token(a):
        return np.ascontiguousarray(a.reshape(2, P, -1).transpose(1, 0, 2)).astype(np.float32)

    inv = (1.0 / np.float32(10000.0) ** (np.arange(0, 16, 2, dtype=np.float32) / 16)).astype(np.float32)
    f = t[:, None] * inv[None, :]
    c["rope_cos_k"], c["rope_sin_k"] = by_token(np.cos(f)), by_token(np.sin(f))
    c["rope_cos_q"], c["rope_sin_q"] = c["rope_cos_k"] * np.float32(0.25), c["rope_sin_k"] * np.float32(0.25)
    half = np.arange(0, 64, 2, dtype=np.float32)
    inv = (1.0 / np.float32(10000.0) ** (half / 64)).astype(np.float32)
    f = t[:, None] * inv[None, :]
    f = np.concatenate([f, f], -1)
    base = (half + np.float32(0.4 * 64)) / np.float32(1.4 * 64)
    scale = base[None, :] ** ((t - SEQ // 2) / np.float32(64.0))[:, None]
    scale = np.concatenate([scale, scale], -1)
    sign = np.where(np.arange(64) < 32, -1.0, 1.0).astype(np.float32)
    c["xpos_cos_q"], c["xpos_sin_q"] = by_token(np.cos(f) * scale * 8), by_token(np.sin(f) * scale * sign * 8)
    c["xpos_cos_k"], c["xpos_sin_k"] = by_token(np.cos(f) / scale), by_token(np.sin(f) / scale * sign)
    return c


def chunks(w):
    return w.reshape(-1, P, w.shape[1]).transpose(1, 0, 2)


def layouts(i):
    d = {"x": i["x"].reshape(TILES, P, DIM).transpose(1, 0, 2)}
    ctxT = i["ctx_1024"].reshape(BATCH, SEQ, KD, P).transpose(0, 3, 2, 1)
    d["ctxT"] = np.concatenate([ctxT, ctxT[:2]], 0)
    d["ctx"] = i["ctx_1024"].reshape(BATCH, 2, P, DIM).transpose(0, 2, 1, 3)
    d["mask_if1"] = i["mask_BxS2_if1"].reshape(TILES, P).T
    d["mask_bk1"] = i["mask_BxS2_bk1"].reshape(TILES, P).T
    d["mask_bk0"] = i["mask_BxS2_bk0"]
    for l in (0, 1, 2):
        n = f"L{l}_xattn_"
        d[f"L{l}_wqT"] = chunks(i[n + "Wq"].T if l < 2 else i[n + "Wq"])
        d[f"L{l}_wkvT"] = chunks(np.concatenate([i[n + "Wk"].T, i[n + "Wv"].T] if l < 2 else
                                                [i[n + "Wk"], i[n + "Wv"]], 1))
        d[f"L{l}_woT"] = chunks(i[n + "Wo"].T if l < 2 else i[n + "Wo"])
        d[f"L{l}_bq"], d[f"L{l}_bo"] = i[n + "bq"], i[n + "bo"]
        d[f"L{l}_bkv"] = np.concatenate([i[n + "bk"], i[n + "bv"]])
    d["L1_bq_col"] = i["L1_xattn_bq"].reshape(KD, P).T
    for w in ("q", "k", "o"):
        d[f"L3_w{w}T"] = chunks(i[f"L3_xattn_W{w}"].T)
    d["L3_bq_col"], d["L3_bk_col"] = i["L3_xattn_bq"].reshape(KD, P).T, i["L3_xattn_bk"].reshape(KD, P).T
    d["L3_bo"] = i["L3_xattn_bo"]
    d["L0_gate"], d["L3_gate"] = chunks(i["L0_ffn_gate"]), chunks(i["L3_ffn_gate_w"].T)
    d["L0_b2"] = i["L0_ffn_b2"]

    def rows_of(w):
        e, k, n = w.shape
        w = np.concatenate([w, np.zeros((e, -k % P, n), w.dtype)], 1)
        return w.reshape(e, -1, P, n).transpose(0, 2, 1, 3).reshape(e, P, -1)

    def wrapped(parts):
        a = np.concatenate(parts, 2)
        return np.concatenate([a, a[:1]], 0)

    d["L0_experts"] = wrapped([rows_of(i["L0_ffn_W1"]), i["L0_ffn_b1"].reshape(EXPERTS, -1, P).transpose(0, 2, 1),
                               rows_of(i["L0_ffn_W2"])])

    w1, w3 = (i[f"L3_ffn_{w}"].transpose(0, 2, 1) for w in ("w1", "w3"))
    w2 = i["L3_ffn_w2"].transpose(0, 2, 1)
    whole = w2.shape[1] // P * P
    d["L3_experts"] = wrapped([rows_of(w1[:, :, :whole]), rows_of(w3[:, :, :whole]),
                               rows_of(np.concatenate([w1[:, :, whole:], w3[:, :, whole:]], 2)),
                               rows_of(np.concatenate([w2[:, :whole], w2[:, whole:], w2[:, whole:]], 1))])
    w = np.concatenate([rows_of(i[f"L1_ffn_w_{n}"].T[None])[0] for n in ("gate", "up", "down")], 1)
    d["L1_ffn"] = w.reshape(P, 4, -1).transpose(1, 0, 2)
    n = "L2_ffn_"
    depth = i[n + "wqkv"].shape[0]
    hid = i[n + "w2"].shape[1]

    def by_layer(f):
        return np.stack([f(l) for l in range(depth)])

    def and_first(a):
        return np.concatenate([a, a[:1]], 0)

    d["L2_wqkv"] = and_first(by_layer(lambda l: chunks(i[n + "wqkv"][l])))
    d["L2_wo"] = and_first(by_layer(lambda l: chunks(i[n + "wo"][l])))
    whole = hid // P * P

    def half_tile(v, axis):
        pad = list(v.shape)
        pad[axis] = P // 2 - v.shape[axis]
        return np.concatenate([v, np.zeros(pad, v.dtype)], axis)

    w1 = i[n + "w1"].reshape(depth, DIM, 2, hid)
    w1 = np.concatenate([w1[:, :, 0, :whole], w1[:, :, 1, :whole], half_tile(w1[:, :, 1, whole:], 2),
                         half_tile(w1[:, :, 0, whole:], 2)], 2)
    d["L2_w1"] = by_layer(lambda l: chunks(w1[l]))
    rest = half_tile(i[n + "w2"][:, whole:], 1)
    d["L2_w2"] = rows_of(np.concatenate([i[n + "w2"][:, :whole], rest, rest], 1)).reshape(depth, P, -1, DIM)
    b1 = i[n + "b1"].reshape(depth, 2, hid)
    rest = half_tile(b1[:, :, whole:], 2)
    b1 = np.concatenate([b1[:, :, :whole], rest[:, ::-1].reshape(depth, 1, P).repeat(2, 1)], 2)
    d["L2_b1"] = b1.reshape(depth, 2, -1, P).transpose(0, 3, 1, 2)
    d["L2_b2"] = i[n + "b2"]
    d["L2_ln_g"], d["L2_ln_b"] = (i[n + v].reshape(depth, KD, P).transpose(0, 2, 1) for v in ("ln_g", "ln_b"))
    qs, ks = i[n + "q_scale"], i[n + "k_scale"]
    d["L2_qk_scale"] = and_first(np.stack([qs, np.concatenate([qs[:, 32:], qs[:, :32]], 1),
                                           ks, np.concatenate([ks[:, 32:], ks[:, :32]], 1)], 1))
    return d


STAGES = [
    ("L0x", lambda nc, x, C, D: cross_attention(nc, x, C, D, 0, False)),
    ("L0f", lambda nc, x, C, D: mixture(nc, x, C, D, 0)),
    ("L1x", layer_one),
    ("L2x", lambda nc, x, C, D: cross_attention(nc, x, C, D, 2, True)),
    ("L2f", local_attention_block),
    ("L3x", memory_attention),
    ("L3f", lambda nc, x, C, D: mixture(nc, x, C, D, 3)),
]


def program(nc, D, out, const_inputs, stages):
    with ExitStack() as ctx:
        s = Stage(nc, ctx, "all")
        x = s.sb("x", [P, TILES, DIM])
        C = {}
        pairs = [(x[:], D["x"])]
        for name, src in const_inputs.items():
            C[name] = s.sb(name, list(src.shape), src.dtype)
            pairs.append((C[name][:], src))
        C["minus_half"] = s.sb("minus_half", [P, 2 * TILES])
        set_done = s.sem("set_done")
        stored = s.sem("stored")
        load_block(nc, s, pairs)
        with nc.Block() as block:
            @block.vector
            def _(dve):
                nc.vector.memset(C["minus_half"][:], -0.5).then_inc(set_done, 1)
                dve.wait_ge(set_done, 1)
        for _, stage in stages:
            stage(nc, x, C, D)
        with nc.Block() as block:
            @block.sync
            def _(sp):
                sp.dma_start(out, x[:]).then_inc(stored, 16)
                sp.wait_ge(stored, 16)


def kernel(**inputs):
    import concourse.bacc as bacc
    from concourse.bass_utils import run_bass_kernel_spmd

    nc = bacc.Bacc("TRN2", target_bir_lowering=False, num_devices=1)
    arrays, aps = {}, []
    for group in (layouts(inputs), constants()):
        made = {}
        for name, a in group.items():
            a = np.ascontiguousarray(a)
            arrays[f"in_{name}"] = a
            kind = U8 if a.dtype == bool else mybir.dt.from_np(a.dtype)
            made[name] = nc.dram_tensor(f"in_{name}", a.shape, kind, kind="ExternalInput").ap()
        aps.append(made)
    out = nc.dram_tensor("out_x", (P, TILES, DIM), F32, kind="ExternalOutput").ap()
    program(nc, aps[0], out, aps[1], STAGES)
    r = run_bass_kernel_spmd(nc, [arrays], core_ids=[0])
    y = r.results[0]["out_x"]
    return y.transpose(1, 0, 2).reshape(BATCH, SEQ, DIM)
```
